# Optimizing a Trainium2 kernel written in Bass

```python
import numpy as np
import jax
import jax.numpy as jnp

def _softmax(x, axis=-1):
    return jax.nn.softmax(x, axis=axis)

def _gelu(x):
    return jax.nn.gelu(x, approximate=True)

def _silu(x):
    return jax.nn.silu(x)

def _sigmoid(x):
    return jax.nn.sigmoid(x)

def _layernorm(x, axis=-1, eps=1e-05):
    m = jnp.mean(x, axis=axis, keepdims=True)
    v = jnp.var(x, axis=axis, keepdims=True)
    return (x - m) / jnp.sqrt(v + eps)

def _scatter_add(tgt, idx, src, axis=0):
    return tgt.at[idx].add(src)

def _segment_sum(src, seg, n):
    return jax.ops.segment_sum(src, seg, n)
kernel_name = 'mk_decoder_postln_d2_seqx_r8_28addb'

def setup_inputs(seed: int=0):
    np.random.seed(seed)
    _w = jnp.asarray

    def _rec_inputs():
        import jax
        import jax.numpy as jnp
        _rk = jax.random.key(seed)
        x = -1.394e-06 + 0.9999 * jax.random.normal(jax.random.fold_in(_rk, 1), (128, 64, 128), jnp.float32)
        _lenS = 64 - jax.random.randint(jax.random.fold_in(_rk, 7), (128,), 0, max(1, 64 // 4) + 1, jnp.int32)
        _lenS2 = 64 - jax.random.randint(jax.random.fold_in(_rk, 8), (128,), 0, max(1, 64 // 4) + 1, jnp.int32)
        _ctx_1024P = jax.random.normal(jax.random.fold_in(_rk, 11), (128, 16, 128), jnp.float32)
        _ctx_1024c = jax.random.dirichlet(jax.random.fold_in(_rk, 511), 0.3 * jnp.ones((16,), jnp.float32), (128, 64))
        _ctx_1024t = jnp.einsum('bsk,bkd->bsd', _ctx_1024c, _ctx_1024P)
        _ctx_1024t = _ctx_1024t * jax.lax.rsqrt(jnp.mean(jnp.square(_ctx_1024t)) + 1e-12) * 0.953939
        ctx_1024 = -0.000392918 + 0.999932 * (_ctx_1024t + 0.3 * jax.random.normal(jax.random.fold_in(_rk, 611), (128, 64, 128), jnp.float32))
        _validS = jnp.arange(64)[None, :] < _lenS[:, None]
        _validS2 = jnp.arange(64)[None, :] < _lenS2[:, None]
        _causal = jnp.tril(jnp.ones((64, 64), dtype=bool))
        mask_BxS2_bk0 = jnp.logical_not(jnp.broadcast_to(_validS2[:, :], (128, 64)))
        return (x, ctx_1024, mask_BxS2_bk0)
    x, ctx_1024, mask_BxS2_bk0 = _rec_inputs()

    def _L0_attn_setup():
        import jax, jax.numpy as jnp
        import numpy as np
        B, L, D_MODEL = (4, 256, 128)
        D_INNER, N_STATE, K_CONV, DT_RANK = (256, 16, 4, 64)

        def _silu(v):
            return v * jax.nn.sigmoid(v)
        key = jax.random.key(seed)
        ks = jax.random.split(key, 8)
        g = lambda k, shape, s=0.02: jax.random.normal(k, shape, jnp.float32) * s
        A = jnp.tile(jnp.arange(1, N_STATE + 1, dtype=jnp.float32), (D_INNER, 1))
        return {'x': jax.random.normal(ks[0], (B, L, D_MODEL), jnp.float32), 'in_proj_w': g(ks[1], (2 * D_INNER, D_MODEL)), 'conv_w': g(ks[2], (D_INNER, K_CONV), 0.1), 'conv_b': jnp.zeros((D_INNER,), jnp.float32), 'x_proj_w': g(ks[3], (DT_RANK + 2 * N_STATE, D_INNER)), 'dt_proj_w': g(ks[4], (D_INNER, DT_RANK)), 'dt_proj_b': g(ks[5], (D_INNER,), 0.1), 'A_log': jnp.log(A), 'D_param': jnp.ones((D_INNER,), jnp.float32), 'out_proj_w': g(ks[6], (D_MODEL, D_INNER))}
    _L0_attn_all = _L0_attn_setup()
    _L0_attn_in = {k: v for k, v in _L0_attn_all.items() if k in ('in_proj_w', 'conv_w', 'conv_b', 'x_proj_w', 'dt_proj_w', 'dt_proj_b', 'A_log', 'D_param', 'out_proj_w')}
    del _L0_attn_all

    def _L0_xattn_setup():
        import jax, jax.numpy as jnp
        import numpy as np
        DIM = 128
        DIM_LATENT = 128
        DIM_HEAD = 64
        INNER = max(DIM, DIM_LATENT)
        HEADS = INNER // DIM_HEAD
        SCALE = DIM_HEAD ** (-0.5)
        LN_EPS = 1e-05
        RMS_EPS = 1e-08

        def layernorm(x, g, b):
            mu = jnp.mean(x, axis=-1, keepdims=True)
            var = jnp.mean(jnp.square(x - mu), axis=-1, keepdims=True)
            return (x - mu) * jax.lax.rsqrt(var + LN_EPS) * g + b

        def rmsnorm(x, gamma):
            n = jnp.linalg.norm(x, axis=-1, keepdims=True) * x.shape[-1] ** (-0.5)
            return x / jnp.maximum(n, RMS_EPS) * gamma
        key = jax.random.key(seed)
        ks = jax.random.split(key, 8)
        b, n, nl = (8, 256, 64)
        x = jax.random.normal(ks[0], (b, n, DIM), dtype=jnp.float32)
        latents = jax.random.normal(ks[1], (b, nl, DIM_LATENT), dtype=jnp.float32)
        mask = jax.random.randint(ks[2], (b, n), 0, 2).astype(bool)
        init = lambda k, shape, fan_in: jax.random.normal(k, shape, jnp.float32) * fan_in ** (-0.5)
        return {'x': x, 'latents': latents, 'mask': mask, 'ln_x_g': jnp.ones((DIM,), jnp.float32), 'ln_x_b': jnp.zeros((DIM,), jnp.float32), 'ln_l_g': jnp.ones((DIM_LATENT,), jnp.float32), 'ln_l_b': jnp.zeros((DIM_LATENT,), jnp.float32), 'q_gamma': jnp.ones((DIM_HEAD,), jnp.float32), 'k_gamma': jnp.ones((DIM_HEAD,), jnp.float32), 'W_q': init(ks[3], (DIM_LATENT, INNER), DIM_LATENT), 'W_kv': init(ks[4], (DIM, 2 * INNER), DIM), 'W_out': init(ks[5], (INNER, DIM_LATENT), INNER), 'b_out': jnp.zeros((DIM_LATENT,), jnp.float32)}
    _L0_xattn_all = _L0_xattn_setup()
    _L0_xattn_in = {k: v for k, v in _L0_xattn_all.items() if k in ('ln_x_g', 'ln_x_b', 'ln_l_g', 'ln_l_b', 'q_gamma', 'k_gamma', 'W_q', 'W_kv', 'W_out', 'b_out')}
    del _L0_xattn_all

    def _L0_ffn_setup():
        import jax, jax.numpy as jnp
        import numpy as np
        B, T, D = (2, 256, 128)
        DCD = 512
        RET = 128
        NEXP = 512
        NKEYS = 64
        H = 4
        KPH = 8
        key = jax.random.key(seed)
        ks = jax.random.split(key, 10)
        s = lambda k, shape, scale: jax.random.normal(k, shape, jnp.float32) * scale
        return {'hidden_states': jax.random.normal(ks[0], (B, T, D), jnp.float32), 'Wg': s(ks[1], (D, DCD), 0.02), 'bg': jnp.zeros((DCD,), jnp.float32), 'Wu': s(ks[2], (D, DCD), 0.02), 'bu': jnp.zeros((DCD,), jnp.float32), 'Wd': s(ks[3], (DCD, D), 0.02), 'bd': jnp.zeros((D,), jnp.float32), 'Wq': s(ks[4], (D, RET * H), 0.02), 'keys': s(ks[5], (H, NKEYS, 2, RET // 2), 0.02), 'down_embed': s(ks[6], (NEXP, D), 0.02), 'up_embed': s(ks[7], (NEXP, D), 0.02)}
    _L0_ffn_all = _L0_ffn_setup()
    _L0_ffn_in = {k: v for k, v in _L0_ffn_all.items() if k in ('Wg', 'bg', 'Wu', 'bu', 'Wd', 'bd', 'Wq', 'keys', 'down_embed', 'up_embed')}
    del _L0_ffn_all

    def _L1_attn_setup():
        import jax, jax.numpy as jnp
        import numpy as np
        B, K, D = (8, 256, 128)
        INNER = 2 * D
        EPS = 1e-05

        def _silu(x):
            return x * jax.nn.sigmoid(x)
        key = jax.random.key(seed)
        k0, k1, k2, k3 = jax.random.split(key, 4)
        s_in = 1.0 / np.sqrt(D)
        s_inner = 1.0 / np.sqrt(INNER)
        return {'x': jax.random.normal(k0, (B, K, D), dtype=jnp.float32), 'w_norm': jnp.ones((D,), dtype=jnp.float32), 'W_in': (jax.random.normal(k1, (2 * INNER, D)) * s_in).astype(jnp.float32), 'W_dt': (jax.random.normal(k2, (INNER, INNER)) * s_inner).astype(jnp.float32), 'b_dt': jnp.zeros((INNER,), dtype=jnp.float32), 'W_out': (jax.random.normal(k3, (D, INNER)) * s_inner).astype(jnp.float32)}
    _L1_attn_all = _L1_attn_setup()
    _L1_attn_in = {k: v for k, v in _L1_attn_all.items() if k in ('w_norm', 'W_in', 'W_dt', 'b_dt', 'W_out')}
    del _L1_attn_all

    def _L1_xattn_setup():
        import jax, jax.numpy as jnp
        import numpy as np
        E, T, H, F = (16, 256, 128, 512)
        key = jax.random.key(seed)
        kx, k1, k2, k3 = jax.random.split(key, 4)
        s = 1.0 / np.sqrt(H)
        return {'x': jax.random.normal(kx, (E, T, H), dtype=jnp.float32), 'w1': jax.random.normal(k1, (E, F, H), dtype=jnp.float32) * s, 'v1': jax.random.normal(k2, (E, F, H), dtype=jnp.float32) * s, 'w2': jax.random.normal(k3, (E, F, H), dtype=jnp.float32) * s}
    _L1_xattn_all = _L1_xattn_setup()
    _L1_xattn_in = {k: v for k, v in _L1_xattn_all.items() if k in ()}
    del _L1_xattn_all

    def _L1_ffn_setup():
        import jax, jax.numpy as jnp
        import numpy as np
        D_MODEL = 128
        FFN = 128
        N_EXPERTS = 8
        N_SHARED = 1
        TOP_K = 2
        B, S = (2, 256)

        def _swiglu(h):
            a, b = jnp.split(h, 2, axis=-1)
            return jax.nn.silu(a) * b
        key = jax.random.key(seed)
        ks = jax.random.split(key, 12)
        sc = 0.02
        return {'x': jax.random.normal(ks[0], (B, S, D_MODEL), dtype=jnp.float32), 'gate_w': jax.random.normal(ks[1], (D_MODEL, N_EXPERTS), dtype=jnp.float32) * sc, 'gate_b': jnp.zeros((N_EXPERTS,), dtype=jnp.float32), 'sw1': jax.random.normal(ks[2], (N_SHARED, D_MODEL, 2 * FFN), dtype=jnp.float32) * sc, 'sb1': jnp.zeros((N_SHARED, 2 * FFN), dtype=jnp.float32), 'sw2': jax.random.normal(ks[3], (N_SHARED, FFN, D_MODEL), dtype=jnp.float32) * sc, 'sb2': jnp.zeros((N_SHARED, D_MODEL), dtype=jnp.float32), 'rw1': jax.random.normal(ks[4], (N_EXPERTS, D_MODEL, 2 * FFN), dtype=jnp.float32) * sc, 'rb1': jnp.zeros((N_EXPERTS, 2 * FFN), dtype=jnp.float32), 'rw2': jax.random.normal(ks[5], (N_EXPERTS, FFN, D_MODEL), dtype=jnp.float32) * sc, 'rb2': jnp.zeros((N_EXPERTS, D_MODEL), dtype=jnp.float32)}
    _L1_ffn_all = _L1_ffn_setup()
    _L1_ffn_in = {k: v for k, v in _L1_ffn_all.items() if k in ('gate_w', 'gate_b', 'sw1', 'sb1', 'sw2', 'sb2', 'rw1', 'rb1', 'rw2', 'rb2')}
    del _L1_ffn_all
    return {'x': x, 'ctx_1024': ctx_1024, 'mask_BxS2_bk0': mask_BxS2_bk0, 'L0_attn_in_proj_w': _L0_attn_in['in_proj_w'], 'L0_attn_conv_w': _L0_attn_in['conv_w'], 'L0_attn_conv_b': _L0_attn_in['conv_b'], 'L0_attn_x_proj_w': _L0_attn_in['x_proj_w'], 'L0_attn_dt_proj_w': _L0_attn_in['dt_proj_w'], 'L0_attn_dt_proj_b': _L0_attn_in['dt_proj_b'], 'L0_attn_A_log': _L0_attn_in['A_log'], 'L0_attn_D_param': _L0_attn_in['D_param'], 'L0_attn_out_proj_w': _L0_attn_in['out_proj_w'], 'L0_xattn_ln_x_g': _L0_xattn_in['ln_x_g'], 'L0_xattn_ln_x_b': _L0_xattn_in['ln_x_b'], 'L0_xattn_ln_l_g': _L0_xattn_in['ln_l_g'], 'L0_xattn_ln_l_b': _L0_xattn_in['ln_l_b'], 'L0_xattn_q_gamma': _L0_xattn_in['q_gamma'], 'L0_xattn_k_gamma': _L0_xattn_in['k_gamma'], 'L0_xattn_W_q': _L0_xattn_in['W_q'], 'L0_xattn_W_kv': _L0_xattn_in['W_kv'], 'L0_xattn_W_out': _L0_xattn_in['W_out'], 'L0_xattn_b_out': _L0_xattn_in['b_out'], 'L0_ffn_Wg': _L0_ffn_in['Wg'], 'L0_ffn_bg': _L0_ffn_in['bg'], 'L0_ffn_Wu': _L0_ffn_in['Wu'], 'L0_ffn_bu': _L0_ffn_in['bu'], 'L0_ffn_Wd': _L0_ffn_in['Wd'], 'L0_ffn_bd': _L0_ffn_in['bd'], 'L0_ffn_Wq': _L0_ffn_in['Wq'], 'L0_ffn_keys': _L0_ffn_in['keys'], 'L0_ffn_down_embed': _L0_ffn_in['down_embed'], 'L0_ffn_up_embed': _L0_ffn_in['up_embed'], 'L1_attn_w_norm': _L1_attn_in['w_norm'], 'L1_attn_W_in': _L1_attn_in['W_in'], 'L1_attn_W_dt': _L1_attn_in['W_dt'], 'L1_attn_b_dt': _L1_attn_in['b_dt'], 'L1_attn_W_out': _L1_attn_in['W_out'], 'L1_ffn_gate_w': _L1_ffn_in['gate_w'], 'L1_ffn_gate_b': _L1_ffn_in['gate_b'], 'L1_ffn_sw1': _L1_ffn_in['sw1'], 'L1_ffn_sb1': _L1_ffn_in['sb1'], 'L1_ffn_sw2': _L1_ffn_in['sw2'], 'L1_ffn_sb2': _L1_ffn_in['sb2'], 'L1_ffn_rw1': _L1_ffn_in['rw1'], 'L1_ffn_rb1': _L1_ffn_in['rb1'], 'L1_ffn_rw2': _L1_ffn_in['rw2'], 'L1_ffn_rb2': _L1_ffn_in['rb2']}

def reference(x, ctx_1024, mask_BxS2_bk0, L0_attn_in_proj_w, L0_attn_conv_w, L0_attn_conv_b, L0_attn_x_proj_w, L0_attn_dt_proj_w, L0_attn_dt_proj_b, L0_attn_A_log, L0_attn_D_param, L0_attn_out_proj_w, L0_xattn_ln_x_g, L0_xattn_ln_x_b, L0_xattn_ln_l_g, L0_xattn_ln_l_b, L0_xattn_q_gamma, L0_xattn_k_gamma, L0_xattn_W_q, L0_xattn_W_kv, L0_xattn_W_out, L0_xattn_b_out, L0_ffn_Wg, L0_ffn_bg, L0_ffn_Wu, L0_ffn_bu, L0_ffn_Wd, L0_ffn_bd, L0_ffn_Wq, L0_ffn_keys, L0_ffn_down_embed, L0_ffn_up_embed, L1_attn_w_norm, L1_attn_W_in, L1_attn_W_dt, L1_attn_b_dt, L1_attn_W_out, L1_ffn_gate_w, L1_ffn_gate_b, L1_ffn_sw1, L1_ffn_sb1, L1_ffn_sw2, L1_ffn_sb2, L1_ffn_rw1, L1_ffn_rb1, L1_ffn_rw2, L1_ffn_rb2):
    import jax
    import jax.numpy as jnp

    def _L0_attn_ref(x, in_proj_w, conv_w, conv_b, x_proj_w, dt_proj_w, dt_proj_b, A_log, D_param, out_proj_w):
        import jax, jax.numpy as jnp
        import numpy as np
        B, L, D_MODEL = (4, 256, 128)
        D_INNER, N_STATE, K_CONV, DT_RANK = (256, 16, 4, 64)

        def _silu(v):
            return v * jax.nn.sigmoid(v)
        b, seqlen, _ = x.shape
        x_and_res = jnp.einsum('bld,ed->ble', x, in_proj_w)
        x_in, res = jnp.split(x_and_res, 2, axis=-1)
        xp = jnp.pad(x_in, ((0, 0), (K_CONV - 1, 0), (0, 0)))
        conv = conv_b
        for k in range(K_CONV):
            conv = conv + xp[:, k:k + seqlen, :] * conv_w[:, k]
        u = _silu(conv)
        x_dbl = jnp.einsum('bld,ed->ble', u, x_proj_w)
        dt_in, Bm, Cm = jnp.split(x_dbl, [DT_RANK, DT_RANK + N_STATE], axis=-1)
        dt = jax.nn.softplus(jnp.einsum('blr,er->ble', dt_in, dt_proj_w) + dt_proj_b)
        A = -jnp.exp(A_log)
        dts = jnp.swapaxes(dt, 0, 1)
        Bs = jnp.swapaxes(Bm, 0, 1)
        Cs = jnp.swapaxes(Cm, 0, 1)
        us = jnp.swapaxes(u, 0, 1)

        def step(h, t):
            dt_t, B_t, C_t, u_t = t
            dA = jnp.exp(dt_t[:, :, None] * A)
            h = dA * h + (dt_t * u_t)[:, :, None] * B_t[:, None, :]
            y_t = jnp.einsum('bdn,bn->bd', h, C_t)
            return (h, y_t)
        h0 = jnp.zeros((b, D_INNER, N_STATE), x.dtype)
        _, ys = jax.lax.scan(step, h0, (dts, Bs, Cs, us))
        y = jnp.swapaxes(ys, 0, 1) + u * D_param
        y = y * _silu(res)
        return jnp.einsum('bld,od->blo', y, out_proj_w)

    def _L0_xattn_ref(x, latents, mask, ln_x_g, ln_x_b, ln_l_g, ln_l_b, q_gamma, k_gamma, W_q, W_kv, W_out, b_out):
        import jax, jax.numpy as jnp
        import numpy as np
        DIM = 128
        DIM_LATENT = 128
        DIM_HEAD = 64
        INNER = max(DIM, DIM_LATENT)
        HEADS = INNER // DIM_HEAD
        SCALE = DIM_HEAD ** (-0.5)
        LN_EPS = 1e-05
        RMS_EPS = 1e-08

        def layernorm(x, g, b):
            mu = jnp.mean(x, axis=-1, keepdims=True)
            var = jnp.mean(jnp.square(x - mu), axis=-1, keepdims=True)
            return (x - mu) * jax.lax.rsqrt(var + LN_EPS) * g + b

        def rmsnorm(x, gamma):
            n = jnp.linalg.norm(x, axis=-1, keepdims=True) * x.shape[-1] ** (-0.5)
            return x / jnp.maximum(n, RMS_EPS) * gamma
        b, n, _ = x.shape
        nl = latents.shape[1]
        xn = layernorm(x, ln_x_g, ln_x_b)
        ln = layernorm(latents, ln_l_g, ln_l_b)
        q = ln @ W_q
        kv = jnp.concatenate([xn @ W_kv, ln @ W_kv], axis=1)
        k, v = (kv[..., :INNER], kv[..., INNER:])
        to_heads = lambda t: t.reshape(t.shape[0], t.shape[1], HEADS, DIM_HEAD).transpose(0, 2, 1, 3)
        q, k, v = (to_heads(q), to_heads(k), to_heads(v))
        qn = rmsnorm(q, q_gamma) * SCALE
        kn = rmsnorm(k, k_gamma)
        sim = jnp.einsum('bhid,bhjd->bhij', qn, kn)
        full_mask = jnp.pad(mask, ((0, 0), (0, nl)), constant_values=True)
        neg = -jnp.finfo(sim.dtype).max
        sim = jnp.where(full_mask[:, None, None, :], sim, neg)
        attn = jax.nn.softmax(sim.astype(jnp.float32), axis=-1).astype(sim.dtype)
        out = jnp.einsum('bhij,bhjd->bhid', attn, v)
        out = out.transpose(0, 2, 1, 3).reshape(b, nl, INNER)
        return out @ W_out + b_out

    def _L0_ffn_ref(hidden_states, Wg, bg, Wu, bu, Wd, bd, Wq, keys, down_embed, up_embed):
        import jax, jax.numpy as jnp
        import numpy as np
        B, T, D = (2, 256, 128)
        DCD = 512
        RET = 128
        NEXP = 512
        NKEYS = 64
        H = 4
        KPH = 8
        b, t, d = hidden_states.shape
        q = (hidden_states @ Wq).reshape(b, t, 2, H, RET // 2)
        sim = jnp.einsum('btphn,hkpn->pbthk', q, keys)
        sc, ix = jax.lax.top_k(sim, KPH)
        sx, sy = (sc[0], sc[1])
        ixx, ixy = (ix[0], ix[1])
        all_sc = (sx[..., :, None] + sy[..., None, :]).reshape(b, t, H, KPH * KPH)
        all_ix = (ixx[..., :, None] * NKEYS + ixy[..., None, :]).reshape(b, t, H, KPH * KPH)
        scores, pk = jax.lax.top_k(all_sc, KPH)
        idx = jnp.take_along_axis(all_ix, pk, axis=-1)
        de = down_embed[idx]
        ue = up_embed[idx]
        w = jnp.einsum('btd,bthkd->bthk', hidden_states, de)
        w = jax.nn.silu(w) * jax.nn.softmax(scores, axis=-1)
        experts_states = jnp.einsum('bthk,bthkd->btd', w, ue)
        mlp = jax.nn.silu(hidden_states @ Wg + bg) * (hidden_states @ Wu + bu) @ Wd + bd
        return mlp + experts_states

    def _L1_attn_ref(x, w_norm, W_in, W_dt, b_dt, W_out):
        import jax, jax.numpy as jnp
        import numpy as np
        B, K, D = (8, 256, 128)
        INNER = 2 * D
        EPS = 1e-05

        def _silu(x):
            return x * jax.nn.sigmoid(x)
        h = x * jax.lax.rsqrt(jnp.mean(x * x, axis=-1, keepdims=True) + EPS) * w_norm
        uv = jnp.einsum('bkd,ed->bke', h, W_in)
        u, z = (uv[..., :INNER], uv[..., INNER:])
        u = _silu(u)
        lam = jax.nn.sigmoid(jnp.einsum('bki,ji->bkj', u, W_dt) + b_dt)

        def step(s, inp):
            lam_t, u_t = inp
            s = lam_t * s + (1.0 - lam_t) * u_t
            return (s, s)
        lam_k = jnp.moveaxis(lam, 1, 0)
        u_k = jnp.moveaxis(u, 1, 0)
        s0 = jnp.zeros((x.shape[0], INNER), dtype=x.dtype)
        _, ys = jax.lax.scan(step, s0, (lam_k, u_k))
        s = jnp.moveaxis(ys, 0, 1)
        s = s * _silu(z)
        y = jnp.einsum('bki,di->bkd', s, W_out)
        return x + y

    def _L1_xattn_ref(x, w1, v1, w2):
        import jax, jax.numpy as jnp
        import numpy as np
        E, T, H, F = (16, 256, 128, 512)
        x1 = jnp.einsum('eth,efh->etf', x, w1)
        x2 = jnp.einsum('eth,efh->etf', x, v1)
        h = jax.nn.gelu(x1, approximate=True) * x2
        return jnp.einsum('etf,efh->eth', h, w2)

    def _L1_ffn_ref(x, gate_w, gate_b, sw1, sb1, sw2, sb2, rw1, rb1, rw2, rb2):
        import jax, jax.numpy as jnp
        import numpy as np
        D_MODEL = 128
        FFN = 128
        N_EXPERTS = 8
        N_SHARED = 1
        TOP_K = 2
        B, S = (2, 256)

        def _swiglu(h):
            a, b = jnp.split(h, 2, axis=-1)
            return jax.nn.silu(a) * b
        hs = jnp.einsum('bsd,ndf->nbsf', x, sw1) + sb1[:, None, None, :]
        shared_out = jnp.einsum('nbsf,nfd->bsd', _swiglu(hs), sw2) + sb2.sum(0)
        probs = jax.nn.softmax(x @ gate_w + gate_b, axis=-1)
        topk_probs, topk_idx = jax.lax.top_k(probs, TOP_K)
        cw = jnp.sum(jax.nn.one_hot(topk_idx, N_EXPERTS, dtype=x.dtype) * topk_probs[..., None], axis=2)
        hr = jnp.einsum('bsd,edf->ebsf', x, rw1) + rb1[:, None, None, :]
        out_e = jnp.einsum('ebsf,efd->ebsd', _swiglu(hr), rw2) + rb2[:, None, None, :]
        routed_out = jnp.einsum('ebsd,bse->bsd', out_e, cw)
        return shared_out + routed_out
    x = _layernorm(x + _L0_attn_ref(x, L0_attn_in_proj_w, L0_attn_conv_w, L0_attn_conv_b, L0_attn_x_proj_w, L0_attn_dt_proj_w, L0_attn_dt_proj_b, L0_attn_A_log, L0_attn_D_param, L0_attn_out_proj_w), axis=-1)
    x = _layernorm(x + _L0_xattn_ref(ctx_1024, x, mask_BxS2_bk0, L0_xattn_ln_x_g, L0_xattn_ln_x_b, L0_xattn_ln_l_g, L0_xattn_ln_l_b, L0_xattn_q_gamma, L0_xattn_k_gamma, L0_xattn_W_q, L0_xattn_W_kv, L0_xattn_W_out, L0_xattn_b_out), axis=-1)
    x = _layernorm(x + _L0_ffn_ref(x, L0_ffn_Wg, L0_ffn_bg, L0_ffn_Wu, L0_ffn_bu, L0_ffn_Wd, L0_ffn_bd, L0_ffn_Wq, L0_ffn_keys, L0_ffn_down_embed, L0_ffn_up_embed), axis=-1)
    x = _layernorm(x + _L1_attn_ref(x, L1_attn_w_norm, L1_attn_W_in, L1_attn_W_dt, L1_attn_b_dt, L1_attn_W_out), axis=-1)
    x = _layernorm(x + _L1_xattn_ref(x, ctx_1024, ctx_1024, ctx_1024), axis=-1)
    x = _layernorm(x + _L1_ffn_ref(x, L1_ffn_gate_w, L1_ffn_gate_b, L1_ffn_sw1, L1_ffn_sb1, L1_ffn_sw2, L1_ffn_sb2, L1_ffn_rw1, L1_ffn_rb1, L1_ffn_rw2, L1_ffn_rb2), axis=-1)
    return x

_drawn_inputs = setup_inputs


def setup_inputs(seed=0):
    import zlib

    import numpy as np

    out = dict(_drawn_inputs(seed))
    spreads = {'L0_attn_conv_b': (0.0, 0.8),
     'L0_attn_D_param': (1.0, 0.6),
     'L0_xattn_ln_x_g': (1.0, 0.6),
     'L0_xattn_ln_x_b': (0.0, 0.484),
     'L0_xattn_ln_l_g': (1.0, 0.2),
     'L0_xattn_ln_l_b': (0.0, 0.1),
     'L0_xattn_q_gamma': (1.0, 0.2),
     'L0_xattn_k_gamma': (1.0, 0.2),
     'L0_xattn_b_out': (0.0, 0.1),
     'L0_ffn_bg': (0.0, 0.8),
     'L0_ffn_bu': (0.0, 0.8),
     'L0_ffn_bd': (0.0, 0.1),
     'L1_attn_w_norm': (1.0, 0.2),
     'L1_attn_b_dt': (0.0, 0.8),
     'L1_ffn_gate_b': (0.0, 0.684),
     'L1_ffn_sb1': (0.0, 0.8),
     'L1_ffn_sb2': (0.0, 0.384),
     'L1_ffn_rb1': (0.0, 0.8),
     'L1_ffn_rb2': (0.0, 1.033)}
    factors = {'L0_attn_in_proj_w': 8.0,
     'L0_attn_conv_w': 8.0,
     'L0_attn_x_proj_w': 8.0,
     'L0_attn_dt_proj_w': 8.0,
     'L0_attn_dt_proj_b': 8.0,
     'L0_attn_A_log': 8.0,
     'L0_attn_out_proj_w': 8.0,
     'L0_ffn_Wg': 4.738,
     'L0_ffn_Wu': 4.784,
     'L0_ffn_Wd': 4.223,
     'L0_ffn_Wq': 8.0,
     'L0_ffn_keys': 8.0,
     'L0_ffn_down_embed': 7.892,
     'L0_ffn_up_embed': 8.0,
     'L1_ffn_gate_w': 2.917,
     'L1_ffn_sw1': 8.0,
     'L1_ffn_sw2': 8.0,
     'L1_ffn_rw1': 8.0,
     'L1_ffn_rw2': 8.0}
    for name, (base, spread) in spreads.items():
        noise = np.random.default_rng([zlib.crc32(name.encode()), seed]).standard_normal(out[name].shape)
        drawn = base * np.exp(spread * noise) if base else spread * noise
        out[name] = jnp.asarray(drawn.astype(out[name].dtype))
    for name, factor in factors.items():
        out[name] = (out[name] * factor).astype(out[name].dtype)
    return out
```

```python
from contextlib import ExitStack

import numpy as np
import concourse.bass as bass
from concourse import mybir

F32 = mybir.dt.float32
BF16 = mybir.dt.bfloat16
U8 = mybir.dt.uint8
U32 = mybir.dt.uint32
ALU = mybir.AluOpType
ACT = mybir.ActivationFunctionType
AX = mybir.AxisListType.X

D = 128
B, S = 128, 64
TOK = B * S
CH = 512
NCH = TOK // CH
SEQ = CH // S
TILES = CH // 128
EPS = 1e-5
BIG = 1e30

INNER = 256
HALF = INNER // 128
NSTATE, KCONV, RANK = 16, 4, 64
PAIRS = NSTATE // 2
AT_U, AT_Z, AT_HI, AT_SP = 3, 3, 5, 6

HEADS, HD = 2, 64

DCD = 512
BLK = DCD // 128
PKH, NK, TOPK = 4, 64, 8
NEXP = 512
ROWS = NEXP // NK

EXPERTS, FFN = 8, 128


def wait(eng, sem, value):
    if isinstance(value, int) and value <= 0:
        return
    eng.wait_ge(sem, value)


class Progress:

    def __init__(self, sems, steps):
        self.sems, self.steps, self.at = sems, steps, {}

    def value(self, it, step):
        return it * len(self.steps) + self.steps.index(step) + 1

    def done(self, ins, u, step):
        k = self.at.get(u, 0)
        assert self.steps[k % len(self.steps)] == step, (self.steps[k % len(self.steps)], step)
        self.at[u] = k + 1
        ins.then_inc(self.sems[u], 1)


def await_(eng, prog, u, it, step):
    eng.wait_ge(prog.sems[u], prog.value(it, step))


def cols(i):
    return bass.ds(i * CH, CH)


def mamba(nc, g):
    ctx = ExitStack()
    with ctx:
        sb = lambda n, s, d=F32: ctx.enter_context(nc.sbuf_tensor(n, s, d))
        ps = lambda n, s: ctx.enter_context(nc.psum_tensor(n, s, F32))
        sem = lambda n: ctx.enter_context(nc.semaphore(n))
        W = {n: sb("m_" + n, s) for n, s in dict(
            win=[128, 4 * 128], convw=[128, KCONV, INNER], convb=[128, HALF], xproj=[128, HALF, 64 + 96],
            dtproj=[RANK, INNER], dtb=[128, HALF], alog=[128, HALF, NSTATE], dpar=[128, HALF],
            woT=[128, HALF * 128]).items()}
        wconv = sb("wconv", [128, KCONV, INNER])
        nega = sb("nega", [128, HALF, NSTATE])
        wout = sb("wout_c", [128, HALF, 128])
        xin = [sb(f"xin{q}", [128, CH]) for q in range(2)]
        xre = sb("xre", [128, CH])
        u = [sb(f"u{q}", [128, HALF, CH]) for q in range(2)]
        z = [sb(f"z{q}", [128, HALF, CH]) for q in range(2)]
        dt = [sb(f"dt{q}", [128, HALF, CH]) for q in range(2)]
        dtu = [sb(f"dtu{q}", [128, HALF, CH]) for q in range(2)]
        parts = [sb(f"parts{q}", [96, CH], BF16) for q in range(2)]
        dtin = sb("dtin", [RANK, CH])
        r1 = sb("r1", [64, CH])
        ab = sb("ab", [128, HALF, CH])
        rl = sb("rl", [128, HALF, CH])
        ex = sb("ex", [128, HALF, CH])
        ln = sb("ln", [128, HALF, CH])
        wm1 = sb("wm1", [128, HALF, CH])
        bs = [sb(f"bs{k}", [128, 2, CH]) for k in range(2)]
        dA = [sb(f"dA{k}", [128, 2, CH]) for k in range(4)]
        dbu = [sb(f"dbu{k}", [128, 2, CH]) for k in range(4)]
        hs = [sb(f"hs{k}", [128, 2, CH]) for k in range(2)]
        hc = [sb(f"hc{k}", [128, 2, CH]) for k in range(2)]
        yd = sb("yd", [128, HALF, CH])
        sq = sb("m_sq", [128, CH])
        rs = sb("m_rs", [128, CH])
        pB = ps("pB", [128, 2, CH])
        pC = ps("pC", [128, 2, CH])
        pY = ps("pY", [128, HALF, CH])
        mA = ps("mA", [128, CH])
        mB = ps("mB", [128, CH])

        s_w, s_wprep, s_wp, s_neg = sem("m_w"), sem("m_wprep"), sem("m_wp"), sem("m_neg")
        s_xin = [sem(f"s_xin{q}") for q in range(2)]
        s_B, s_C, s_ysum, s_xre = sem("s_B"), sem("s_C"), sem("s_ysum"), sem("s_xre")
        s_conv, s_res, s_xdbl, s_dtp, s_xc, s_var = (sem("s_" + n) for n in "conv res xdbl dtp xc var".split())
        s_bs, s_dA, s_u, s_z, s_hi, s_ab, s_ex, s_ln, s_sq, s_lnv, s_rs = (sem("s_" + n) for n in "bs dA u z hi ab ex ln sq lnv rs".split())
        s_dbu, s_t = sem("s_dbu"), sem("s_t")
        s_scan, s_hc, s_r1, s_mid, s_lo, s_wm1, s_c, s_dt, s_dtu, s_yd, s_yz, s_x1 = (
            sem("s_" + n) for n in "scan hc r1 mid lo wm1 c dt dtu yd yz x1".split())

        ld = g["in"]
        seqs = lambda ap: ap.rearrange("p (s t) -> p s t", t=S)

        def over_chunks(eng, body):
            for i in range(2):
                body(i, i % 2, i == 0, False)
            with eng.Fori(1, NCH // 2 - 1) as ib:
                for q in range(2):
                    body(ib * 2 + q, q, False, False)
            for i in range(NCH - 2, NCH):
                body(i, i % 2, False, i == NCH - 1)

        with nc.Block() as block:
            @block.sync
            def _(sp):
                for n in W:
                    sp.dma_start(W[n][:], ld[n]).then_inc(s_w, 16)
                sp.dma_start(xin[0][:], ld["xT"][:, 0:CH]).then_inc(s_xin[0], 16)

                def body(i, q, first, last):
                    if not last:
                        wait(sp, s_res, i)
                        sp.dma_start(xin[1 - q][:], ld["xT"][:, cols(i + 1)]).then_inc(s_xin[1 - q], 16)
                    wait(sp, s_xc, i)
                    sp.dma_start(xre[:], ld["xT"][:, cols(i)]).then_inc(s_xre, 16)

                over_chunks(sp, body)

            @block.tensor
            def _(pe):
                pe.wait_ge(s_w, 16 * len(W))
                pe.wait_ge(g["s_const"], g["const_ready"])
                for h in range(HALF):
                    mm = pe.matmul(mA[:, h * 128:(h + 1) * 128], W["woT"][:, h * 128:(h + 1) * 128], g["cen"][:],
                                   start=True, stop=True)
                mm.then_inc(s_wprep, 1)
                pe.wait_ge(s_wp, 1 + KCONV)

                def conv(n, q, h, xin_count):
                    if h == 0:
                        pe.wait_ge(s_xin[q], xin_count)
                        wait(pe, s_x1, n - 2)
                    m = (mA, mB)[h]
                    x3 = seqs(xin[q][:])
                    for k in reversed(range(KCONV)):
                        sh = KCONV - 1 - k
                        mm = pe.matmul(seqs(m[:])[:, :, sh:S], wconv[:, k, h * 128:(h + 1) * 128],
                                       x3[:, :, 0:S - sh], start=(sh == 0), stop=(k == 0))
                    mm.then_inc(s_conv, 1)

                def res(n, q):
                    pe.wait_ge(s_u, n + 1)
                    for h, m in ((0, mA), (1, mB)):
                        mm = pe.matmul(m[:], W["win"][:, INNER + h * 128:INNER + (h + 1) * 128], xin[q][:],
                                       start=True, stop=True)
                    mm.then_inc(s_res, 1)

                def xdbl(n, q):
                    pe.wait_ge(s_z, n + 1)
                    for h in range(HALF):
                        pe.matmul(mA[0:96, :], W["xproj"][:, h, RANK:RANK + 96], u[q][:, h, :],
                                  start=(h == 0), stop=(h == HALF - 1))
                    for h in range(HALF):
                        mm = pe.matmul(mB[0:RANK, :], W["xproj"][:, h, 0:RANK], u[q][:, h, :],
                                       start=(h == 0), stop=(h == HALF - 1))
                    mm.then_inc(s_xdbl, 1)

                def dtp(n, q):
                    pe.wait_ge(s_hi, n + 1)
                    pe.wait_ge(s_r1, n + 1)
                    for h, m in ((0, mA), (1, mB)):
                        mm = pe.matmul(m[:], W["dtproj"][:, h * 128:(h + 1) * 128], dtin[:], start=True, stop=True)
                    mm.then_inc(s_dtp, 1)

                def spread(row, m, q, done):
                    for j in range(2):
                        mm = pe.matmul(m[:, j, :], g["sel"][:, row + j, :], parts[q][:], start=True, stop=True)
                    mm.then_inc(done, 1)

                def centre(n):
                    pe.wait_ge(s_xre, 16 * (n + 1))
                    pe.wait_ge(s_yz, n + 1)
                    pe.matmul(mA[:], g["cen"][:], xre[:], start=True, stop=False)
                    for h in range(HALF):
                        mm = pe.matmul(mA[:], wout[:, h, :], yd[:, h, :], start=False, stop=(h == HALF - 1))
                    mm.then_inc(s_xc, 1)

                def variance(n):
                    pe.wait_ge(s_sq, n + 1)
                    pe.matmul(mB[:], g["avg"][:], sq[:], start=True, stop=True).then_inc(s_var, 1)

                def body(i, q, first, last):
                    xin_count = 16 if first else ((i + 1 - (1 - q)) // 2 + 1) * 16
                    for p in range(PAIRS):
                        P = i * PAIRS + p

                        def between():
                            if p < PAIRS - 2 or not last:
                                if p == PAIRS - 2:
                                    pe.wait_ge(s_lo, i + 2)
                                pe.wait_ge(s_bs, P + 2)
                                spread(2 * ((p + 2) % PAIRS), pB, q if p < PAIRS - 2 else 1 - q, s_B)
                            if not last and p < 2:
                                conv(i + 1, 1 - q, p, xin_count)
                            if not last and p == 2:
                                res(i + 1, 1 - q)
                            if not last and p == 3:
                                xdbl(i + 1, 1 - q)
                            if not last and p == 4:
                                dtp(i + 1, 1 - q)
                            if not first and p == 5:
                                if not last:
                                    pe.wait_ge(s_ab, i + 2)
                                centre(i - 1)
                            if not first and p == 6:
                                variance(i - 1)

                        if p == 0:
                            between()
                            wait(pe, s_yd, i)
                        for h in range(HALF):
                            pe.wait_ge(s_hc, P * 2 + h + 1)
                            if h == 1 and (p < PAIRS - 1 or not last):
                                spread(NSTATE + 2 * ((p + 1) % PAIRS), pC, q if p < PAIRS - 1 else 1 - q, s_C)
                            for j in range(2):
                                mm = pe.matmul(pY[:, h, :], g["eye"][:], hc[h][:, j, :], start=(p == 0 and j == 0),
                                               stop=(p == PAIRS - 1 and j == 1))
                            mm.then_inc(s_ysum, 1)
                            if h == 0 and p:
                                between()

                for h in range(HALF):
                    conv(0, 0, h, 16)
                res(0, 0)
                xdbl(0, 0)
                dtp(0, 0)
                pe.wait_ge(s_lo, 1)
                spread(0, pB, 0, s_B)
                spread(NSTATE, pC, 0, s_C)
                pe.wait_ge(s_bs, 1)
                spread(2, pB, 0, s_B)
                over_chunks(pe, body)
                centre(NCH - 1)
                variance(NCH - 1)

            @block.scalar
            def _(act):
                act.wait_ge(s_w, 16 * len(W))
                act.activation(nega[:], W["alog"][:], ACT.Exp).then_inc(s_neg, 1)
                act.wait_ge(s_wprep, 1)
                act.activation(wout[:], mA[:, 0:HALF * 128].rearrange("p (h n) -> p h n", h=HALF), ACT.Copy)\
                   .then_inc(s_wp, 1)

                def drive(n, q):
                    wait(act, s_yz, n - 1)
                    for h, m in ((0, mA), (1, mB)):
                        act.wait_ge(s_conv, 2 * n + h + 1)
                        a = act.activation(u[q][:, h, :], m[:], ACT.Silu, bias=W["convb"][:, h:h + 1])
                    a.then_inc(s_u, 1)

                def gate(n, q):
                    act.wait_ge(s_res, n + 1)
                    for h, m in ((0, mA), (1, mB)):
                        a = act.activation(z[q][:, h, :], m[:], ACT.Silu)
                    a.then_inc(s_z, 1)

                def high(n, q):
                    act.wait_ge(s_xdbl, n + 1)
                    wait(act, s_C, (n - 1) * PAIRS)
                    act.activation(parts[q][:], mA[0:96, :], ACT.Copy)
                    wait(act, s_dtp, n)
                    act.activation(dtin[:], mB[0:RANK, :], ACT.Copy).then_inc(s_hi, 1)

                def softplus(n):
                    act.wait_ge(s_dtp, n + 1)
                    wait(act, s_dtu, n)
                    for h, m in ((0, mA), (1, mB)):
                        act.activation(ab[:, h, :], m[:], ACT.Abs, bias=W["dtb"][:, h:h + 1])
                        a = act.activation(rl[:, h, :], m[:], ACT.Relu, bias=W["dtb"][:, h:h + 1])
                    a.then_inc(s_ab, 1)
                    act.wait_ge(s_ab, n + 1)
                    act.activation(ex[:], ab[:], ACT.Exp, scale=-1.0).then_inc(s_ex, 1)
                    act.wait_ge(s_ex, n + 1)
                    act.activation(ln[:], ex[:], ACT.Ln, bias=1.0).then_inc(s_ln, 1)

                def squares(n):
                    act.wait_ge(s_xc, n + 1)
                    wait(act, s_var, n)
                    act.activation(sq[:], mA[:], ACT.Square).then_inc(s_sq, 1)

                def rsqrt(n):
                    act.wait_ge(s_var, n + 1)
                    wait(act, s_x1, n)
                    act.activation(rs[:], mB[:], ACT.Ln, bias=g["eps"][:]).then_inc(s_lnv, 1)
                    act.wait_ge(s_lnv, n + 1)
                    act.activation(rs[:], rs[:], ACT.Exp, scale=-0.5).then_inc(s_rs, 1)

                def body(i, q, first, last):
                    for p in range(PAIRS):
                        act.wait_ge(s_B, i * PAIRS + p + 1)
                        wait(act, s_dbu, (i * PAIRS + p) * 2 - 2)
                        act.activation(bs[p % 2][:], pB[:], ACT.Copy).then_inc(s_bs, 1)
                        if p == 0:
                            act.wait_ge(s_dt, i + 1)
                        for h in range(HALF):
                            k = (p * 2 + h) % 4
                            wait(act, s_scan, (i * PAIRS + p) * 2 + h - 3)
                            for j in range(2):
                                a = act.activation(seqs(dA[k][:, j, :])[:, :, 1:S], seqs(dt[q][:, h, :])[:, :, 1:S],
                                                   ACT.Exp, scale=nega[:, h, 2 * p + j:2 * p + j + 1])
                            a.then_inc(s_dA, 1)
                        if not last and p == AT_U:
                            drive(i + 1, 1 - q)
                        if not last and p == AT_Z:
                            gate(i + 1, 1 - q)
                        if not last and p == AT_HI:
                            high(i + 1, 1 - q)
                        if not last and p == AT_SP:
                            softplus(i + 1)
                        if not first and p == PAIRS - 1:
                            squares(i - 1)
                            rsqrt(i - 1)

                act.wait_ge(s_neg, 2)
                drive(0, 0)
                gate(0, 0)
                high(0, 0)
                softplus(0)
                over_chunks(act, body)
                squares(NCH - 1)
                rsqrt(NCH - 1)

            @block.gpsimd
            def _(pool):
                def relu_ln(n):
                    pool.wait_ge(s_ln, n + 1)
                    pool.tensor_tensor(ln[:], ln[:], rl[:], ALU.add).then_inc(s_t, 1)

                def body(i, q, first, last):
                    for p in range(PAIRS):
                        if p == 0:
                            pool.wait_ge(s_dtu, i + 1)
                        if not last and p == PAIRS - 1:
                            relu_ln(i + 1)
                        pool.wait_ge(s_bs, i * PAIRS + p + 1)
                        for h in range(HALF):
                            k = (p * 2 + h) % 4
                            wait(pool, s_scan, (i * PAIRS + p) * 2 + h - 3)
                            pool.tensor_tensor(dbu[k][:], dtu[q][:, h, None, :].to_broadcast([128, 2, CH]), bs[p % 2][:],
                                               ALU.mult).then_inc(s_dbu, 1)

                relu_ln(0)
                over_chunks(pool, body)

            @block.vector
            def _(dve):
                dve.wait_ge(s_w, 16 * len(W))
                for k in range(KCONV):
                    dve.tensor_tensor(wconv[:, k, :], W["win"][:, 0:INNER], W["convw"][:, k, :], ALU.mult)\
                       .then_inc(s_wp, 1)
                for k in range(4):
                    for j in range(2):
                        dve.memset(seqs(dA[k][:, j, :])[:, :, 0:1], 0.0)
                dve.wait_ge(s_neg, 1)
                dve.tensor_scalar(nega[:], nega[:], -1.0, None, ALU.mult).then_inc(s_neg, 1)

                def remainders(n, q):
                    dve.wait_ge(s_hi, n + 1)
                    dve.tensor_tensor(r1[:], mA[0:64, :], parts[q][0:64, :], ALU.subtract).then_inc(s_r1, 1)
                    dve.wait_ge(s_r1, n + 1)
                    dve.tensor_copy(parts[q][0:64, :], r1[:]).then_inc(s_mid, 1)
                    dve.wait_ge(s_mid, n + 1)
                    dve.tensor_tensor(parts[q][0:32, :], r1[0:32, :], parts[q][0:32, :], ALU.subtract).then_inc(s_lo, 1)

                def correction(n):
                    dve.wait_ge(s_ex, n + 1)
                    dve.tensor_scalar(wm1[:], ex[:], 1.0, -1.0, ALU.add, ALU.add).then_inc(s_wm1, 1)
                    dve.wait_ge(s_wm1, n + 1)
                    dve.tensor_tensor(wm1[:], ex[:], wm1[:], ALU.subtract).then_inc(s_c, 1)

                def step(n, q):
                    dve.wait_ge(s_c, n + 1)
                    dve.wait_ge(s_t, n + 1)
                    wait(dve, s_dA, (n - 1) * PAIRS * 2)
                    wait(dve, s_dbu, (n - 1) * PAIRS * 2)
                    dve.tensor_tensor(dt[q][:], wm1[:], ln[:], ALU.add).then_inc(s_dt, 1)
                    dve.wait_ge(s_dt, n + 1)
                    dve.tensor_tensor(dtu[q][:], dt[q][:], u[q][:], ALU.mult).then_inc(s_dtu, 1)

                def skip(n, q):
                    dve.wait_ge(s_ysum, (n + 1) * PAIRS * 2)
                    wait(dve, s_xc, n)
                    for h in range(HALF):
                        a = dve.scalar_tensor_tensor(yd[:, h, :], u[q][:, h, :], W["dpar"][:, h:h + 1], pY[:, h, :],
                                                     ALU.mult, ALU.add)
                    a.then_inc(s_yd, 1)

                def gated(n, q):
                    dve.wait_ge(s_yd, n + 1)
                    dve.tensor_tensor(yd[:], yd[:], z[q][:], ALU.mult).then_inc(s_yz, 1)

                def normed(n):
                    dve.wait_ge(s_rs, n + 1)
                    dve.tensor_tensor(g["resid"][:, cols(n)], mA[:], rs[:], ALU.mult).then_inc(s_x1, 1)

                def body(i, q, first, last):
                    for p in range(PAIRS):
                        for h in range(HALF):
                            k, n = (p * 2 + h) % 4, (i * PAIRS + p) * 2 + h
                            dve.wait_ge(s_dA, n + 1)
                            dve.wait_ge(s_dbu, n + 1)
                            wait(dve, s_hc, n - 1)
                            dve.tensor_tensor_scan(hs[h][:].rearrange("p j t -> p (j t)"),
                                                   dA[k][:].rearrange("p j t -> p (j t)"),
                                                   dbu[k][:].rearrange("p j t -> p (j t)"), 0.0, ALU.mult, ALU.add)\
                               .then_inc(s_scan, 1)
                            if not first and p == 0 and h == 0:
                                skip(i - 1, 1 - q)
                            dve.wait_ge(s_scan, n + 1)
                            dve.wait_ge(s_C, i * PAIRS + p + 1)
                            wait(dve, s_ysum, n - 1)
                            dve.tensor_tensor(hc[h][:], hs[h][:], pC[:], ALU.mult).then_inc(s_hc, 1)
                            if h == 1:
                                continue
                            if not first and p == 1:
                                gated(i - 1, 1 - q)
                            if not last and p == 4:
                                remainders(i + 1, 1 - q)
                            if not last and p == 5:
                                correction(i + 1)
                            if not last and p == 6:
                                step(i + 1, 1 - q)
                            if not first and p == PAIRS - 1:
                                normed(i - 1)

                remainders(0, 0)
                correction(0)
                step(0, 0)
                over_chunks(dve, body)
                skip(NCH - 1, (NCH - 1) % 2)
                gated(NCH - 1, (NCH - 1) % 2)
                normed(NCH - 1)


class Stage:

    def __init__(self, nc, ctx, tag, pe, act, dve, pool):
        self.nc, self.ctx, self.tag = nc, ctx, tag
        self.pX = [ctx.enter_context(nc.psum_tensor(f"{tag}_ps{u}", [128, 4, CH], F32)) for u in range(2)]
        streams = lambda e: [self.sem(f"{e}{u}") for u in range(2)]
        count = lambda e, steps: Progress(streams(e) if steps else [], steps.split())
        self.PE, self.ACT, self.DVE, self.POOL = count("pe", pe), count("act", act), count("dve", dve), count("pool", pool)
        self.ticks, self.n_ticks = self.sb("ticks", [128, 32]), 0
        self.s_w, self.s_prep, self.s_copied = self.sem("w"), self.sem("prep"), self.sem("copied")

    def carry(self, dve):
        dve.memset(self.ticks[:, self.n_ticks:self.n_ticks + 1], 0.0)
        self.n_ticks += 1

    def sem(self, n):
        return self.ctx.enter_context(self.nc.semaphore(f"{self.tag}_{n}"))

    def sb(self, n, s, d=F32):
        return self.ctx.enter_context(self.nc.sbuf_tensor(f"{self.tag}_{n}", s, d))

    def two(self, n, s, d=F32):
        return [self.sb(f"{n}{u}", s, d) for u in range(2)]


def over_pairs(eng, body):
    body(0, True)
    with eng.Fori(1, NCH // 2) as it:
        body(it, False)


def load_weights(eng, W, ld, sem):
    for n in W:
        eng.dma_start(W[n][:], ld[n]).then_inc(sem, 16)


def centred_rows(pe, psum, wT, blocks, cen):
    for b in range(blocks):
        mm = pe.matmul(psum[:, b * 128:(b + 1) * 128], wT[:, b * 128:(b + 1) * 128], cen, start=True, stop=True)
    return mm


def take_input(dve, st, g, xs, it, u, first):
    if not first:
        await_(dve, st.DVE, u, it - 1, "norm")
    st.DVE.done(dve.tensor_scalar(xs[u][:], g["resid"][:, cols(it * 2 + u)], 1.0, 0.0, ALU.mult, ALU.add), u, "xs")


def rsqrt_steps(act, st, g, it, u, src, rs):
    st.ACT.done(act.activation(rs, src, ACT.Ln, bias=g["eps"][:]), u, "ln")
    await_(act, st.ACT, u, it, "ln")
    st.ACT.done(act.activation(rs, rs, ACT.Exp, scale=-0.5), u, "rs")


def cross(nc, g):
    ctx = ExitStack()
    with ctx:
        st = Stage(nc, ctx, "x",
                   pe="cen var qk ms v sim pT av out vout",
                   act="sq lnc rsc sqk gq gk lnk rsk vs exp pT av sqo ln rs",
                   dve="xs hat affine guard qn mb mask max sub sum rec pn norm",
                   pool="")
        PE, A_, V_, P_, pX = st.PE, st.ACT, st.DVE, st.POOL, st.pX
        W = {n: st.sb(n, s) for n, s in dict(xwq=[128, 128], xwkv=[128, 256], xwoT=[128, 128], xbo=[128, 1], gx=[128, 1],
                                             bx=[128, 1], gl=[128, 1], bl=[128, 1], gq=[128, 1], gk=[128, 1]).items()}
        mask = st.sb("mask", [128, B // 2 * S], U8)
        wo, cb, gqs = st.sb("wo", [128, 128]), st.sb("cb", [128, 1]), st.sb("gqs", [128, 1])
        cin, xs = st.two("cin", [128, CH]), st.two("xs", [128, CH])
        sq, rs = st.two("sq", [128, 3, CH]), st.two("rs", [128, 3, CH])
        cn = st.two("cn", [128, 2, CH])
        qk = st.two("qk", [128, 3, CH])
        qn, kn = st.two("qn", [128, CH]), st.two("kn", [128, SEQ, 2, S])
        vs = st.two("vs", [128, SEQ, 128])
        mb = st.two("mb", [128, SEQ // 2, S])
        mx, sm = st.two("mx", [128, SEQ]), st.two("sm", [128, SEQ])
        pr, pT = st.two("pr", [128, SEQ, 128]), st.two("pT", [128, 2, CH])
        ao = st.two("ao", [128, CH])
        s_cin = [st.sem(f"cin{u}") for u in range(2)]
        ld = g["in"]

        with nc.Block() as block:
            @block.sync
            def _(sp):
                for u in range(2):
                    sp.dma_start(cin[u][:], ld["ctxT"][:, cols(u)]).then_inc(s_cin[u], 16)
                load_weights(sp, W, ld, st.s_w)
                for r in range(2):
                    sp.dma_start(mask[r * S:(r + 1) * S, :],
                                 ld["mask"][r:r + 1, :].to_broadcast([S, B // 2 * S])).then_inc(st.s_w, 16)
                with sp.Fori(0, NCH // 2 - 1) as it:
                    for u in range(2):
                        await_(sp, PE, u, it, "cen")
                        sp.dma_start(cin[u][:], ld["ctxT"][:, cols(it * 2 + 2 + u)]).then_inc(s_cin[u], 16)
            wready = 16 * (len(W) + 2)

            @block.tensor
            def _(pe):
                pe.wait_ge(st.s_w, wready)
                centred_rows(pe, pX[0][:, 0, :], W["xwoT"], 1, g["cen"][:])
                pe.matmul(pX[0][:, 0, 128:129], g["cen"][:], W["xbo"][:], start=True, stop=True).then_inc(st.s_prep, 1)
                pe.wait_ge(st.s_copied, 2)

                def body(it, first):
                    for u in range(2):
                        pe.wait_ge(s_cin[u], (it + 1) * 16)
                        await_(pe, V_, u, it, "xs")
                        pe.matmul(pX[u][:, 0, :], g["cen"][:], cin[u][:], start=True, stop=True)
                        PE.done(pe.matmul(pX[u][:, 1, :], g["cen"][:], xs[u][:], start=True, stop=True), u, "cen")
                    for u in range(2):
                        await_(pe, A_, u, it, "sq")
                        for k in range(2):
                            mm = pe.matmul(pX[u][:, 2 + k, :], g["avg"][:], sq[u][:, k, :], start=True, stop=True)
                        PE.done(mm, u, "var")
                    for u in range(2):
                        await_(pe, V_, u, it, "affine")
                        pe.matmul(pX[u][:, 0, :], W["xwq"][:], cn[u][:, 1, :], start=True, stop=True)
                        for k in range(2):
                            mm = pe.matmul(pX[u][:, 1 + k, :], W["xwkv"][:, 0:128], cn[u][:, k, :], start=True, stop=True)
                        PE.done(mm, u, "qk")
                    for u in range(2):
                        await_(pe, A_, u, it, "gk")
                        for k in range(3):
                            mm = pe.matmul(pX[u][:, k, :], g["avgh"][:], sq[u][:, k, :], start=True, stop=True)
                        PE.done(mm, u, "ms")
                    for u in range(2):
                        await_(pe, V_, u, it, "qn")
                        for b in range(SEQ):
                            for k in range(2):
                                mm = pe.matmul(pX[u][k * S:(k + 1) * S, 2 + b // 4, (b % 4) * 128:(b % 4 + 1) * 128],
                                               cn[u][:, k, b * S:(b + 1) * S], W["xwkv"][:, 128:256],
                                               start=True, stop=True)
                        PE.done(mm, u, "v")
                    for u in range(2):
                        for h in range(HEADS):
                            for b in range(SEQ):
                                r, pair = b % 2, b // 2
                                mm = pe.matmul(pX[u][r * S:(r + 1) * S, h, pair * 128:(pair + 1) * 128],
                                               qn[u][h * HD:(h + 1) * HD, b * S:(b + 1) * S],
                                               kn[u][h * HD:(h + 1) * HD, b, :, :].rearrange("p k t -> p (k t)"),
                                               start=True, stop=True)
                        PE.done(mm, u, "sim")
                    for u in range(2):
                        await_(pe, V_, u, it, "pn")
                        for k in range(SEQ):
                            mm = pe.transpose(pX[u][:, k // 4, (k % 4) * 128:(k % 4 + 1) * 128], pr[u][:, k, :],
                                              g["eye"][:])
                        PE.done(mm, u, "pT")
                    for u in range(2):
                        await_(pe, A_, u, it, "pT")
                        await_(pe, A_, u, it, "vs")
                        for b in range(SEQ):
                            for h in range(HEADS):
                                mm = pe.matmul(pX[u][h * HD:(h + 1) * HD, 2, b * S:(b + 1) * S],
                                               vs[u][:, b, h * HD:(h + 1) * HD],
                                               pT[u][:, h, b * S:(b + 1) * S], start=True, stop=True)
                        PE.done(mm, u, "av")
                    for u in range(2):
                        await_(pe, A_, u, it, "av")
                        pe.matmul(pX[u][:, 3, :], g["cen"][:], xs[u][:], start=True, stop=False)
                        PE.done(pe.matmul(pX[u][:, 3, :], wo[:], ao[u][:], start=False, stop=True), u, "out")
                    for u in range(2):
                        await_(pe, A_, u, it, "sqo")
                        PE.done(pe.matmul(pX[u][:, 0, :], g["avg"][:], sq[u][:, 0, :], start=True, stop=True), u, "vout")
                over_pairs(pe, body)

            @block.scalar
            def _(act):
                act.wait_ge(st.s_prep, 1)
                act.activation(wo[:], pX[0][:, 0, 0:128], ACT.Copy)
                act.activation(cb[:], pX[0][:, 0, 128:129], ACT.Copy).then_inc(st.s_copied, 1)

                def body(it, first):
                    for u in range(2):
                        await_(act, PE, u, it, "cen")
                        A_.done(act.activation(sq[u][:, 0:2, :], pX[u][:, 0:2, :], ACT.Square), u, "sq")
                    for u in range(2):
                        await_(act, PE, u, it, "var")
                        A_.done(act.activation(rs[u][:, 0:2, :], pX[u][:, 2:4, :], ACT.Ln, bias=g["eps"][:]), u, "lnc")
                        await_(act, A_, u, it, "lnc")
                        A_.done(act.activation(rs[u][:, 0:2, :], rs[u][:, 0:2, :], ACT.Exp, scale=-0.5), u, "rsc")
                    for u in range(2):
                        await_(act, PE, u, it, "qk")
                        A_.done(act.activation(sq[u][:], pX[u][:, 0:3, :], ACT.Square), u, "sqk")
                        A_.done(act.activation(qk[u][:, 0, :], pX[u][:, 0, :], ACT.Copy, scale=gqs[:]), u, "gq")
                        A_.done(act.activation(qk[u][:, 1:3, :], pX[u][:, 1:3, :], ACT.Copy, scale=W["gk"][:]), u, "gk")
                    for u in range(2):
                        await_(act, V_, u, it, "guard")
                        A_.done(act.activation(rs[u][:], rs[u][:], ACT.Ln), u, "lnk")
                        await_(act, A_, u, it, "lnk")
                        A_.done(act.activation(rs[u][:], rs[u][:], ACT.Exp, scale=-0.5), u, "rsk")
                    for u in range(2):
                        await_(act, PE, u, it, "v")
                        A_.done(act.activation(vs[u][:].rearrange("p (k b) d -> p k (b d)", k=2), pX[u][:, 2:4, :], ACT.Copy), u, "vs")
                    for u in range(2):
                        await_(act, V_, u, it, "sub")
                        A_.done(act.activation(pr[u][:], pr[u][:], ACT.Exp), u, "exp")
                    for u in range(2):
                        await_(act, PE, u, it, "pT")
                        A_.done(act.activation(pT[u][:], pX[u][:, 0:2, :], ACT.Copy), u, "pT")
                    for u in range(2):
                        await_(act, PE, u, it, "av")
                        A_.done(act.activation(ao[u][:], pX[u][:, 2, :], ACT.Copy), u, "av")
                    for u in range(2):
                        await_(act, PE, u, it, "out")
                        A_.done(act.activation(sq[u][:, 0, :], pX[u][:, 3, :], ACT.Square, bias=cb[:]), u, "sqo")
                    for u in range(2):
                        await_(act, PE, u, it, "vout")
                        rsqrt_steps(act, st, g, it, u, pX[u][:, 0, :], rs[u][:, 0, :])
                over_pairs(act, body)

            @block.vector
            def _(dve):
                dve.wait_ge(st.s_w, wready)
                dve.tensor_scalar(gqs[:], W["gq"][:], HD ** -0.5, None, ALU.mult).then_inc(st.s_copied, 1)

                def body(it, first):
                    for u in range(2):
                        take_input(dve, st, g, xs, it, u, first)
                    for u in range(2):
                        await_(dve, A_, u, it, "rsc")
                        V_.done(dve.tensor_tensor(cn[u][:], pX[u][:, 0:2, :], rs[u][:, 0:2, :], ALU.mult), u, "hat")
                        await_(dve, V_, u, it, "hat")
                        dve.tensor_scalar(cn[u][:, 0, :], cn[u][:, 0, :], W["gx"][:], W["bx"][:], ALU.mult, ALU.add)
                        V_.done(dve.tensor_scalar(cn[u][:, 1, :], cn[u][:, 1, :], W["gl"][:], W["bl"][:], ALU.mult,
                                                  ALU.add), u, "affine")
                    for u in range(2):
                        await_(dve, PE, u, it, "ms")
                        V_.done(dve.tensor_scalar(rs[u][:], pX[u][:, 0:3, :], 1e-16, None, ALU.max), u, "guard")
                    for u in range(2):
                        await_(dve, A_, u, it, "rsk")
                        dve.tensor_tensor(qn[u][:], qk[u][:, 0, :], rs[u][:, 0, :], ALU.mult)
                        V_.done(dve.tensor_tensor(kn[u][:].rearrange("p b k t -> p k b t"),
                                                  qk[u][:, 1:3, :].rearrange("p k (b t) -> p k b t", b=SEQ),
                                                  rs[u][:, 1:3, :].rearrange("p k (b t) -> p k b t", b=SEQ),
                                                  ALU.mult), u, "qn")
                    for u in range(2):
                        n = SEQ // 2 * S
                        V_.done(dve.tensor_scalar(mb[u][:].rearrange("p a t -> p (a t)"), mask[:, bass.ds((it * 2 + u) * n, n)],
                                                  -1.0, BIG, ALU.add, ALU.mult), u, "mb")
                        await_(dve, PE, u, it, "sim")
                        await_(dve, V_, u, it, "mb")
                        keys = pX[u][:, 0:2, :].rearrange("p h (a k t) -> p h a k t", k=2, t=S)[:, :, :, 0, :]
                        V_.done(dve.tensor_tensor(keys, keys, mb[u][:, None, :, :].to_broadcast([128, 2, SEQ // 2, S]),
                                                  ALU.add), u, "mask")
                        await_(dve, V_, u, it, "mask")
                        sim = pX[u][:, 0:2, :].rearrange("p h (a k) -> p (h a) k", k=128)
                        V_.done(dve.tensor_reduce(mx[u][:], sim, AX, ALU.max), u, "max")
                        await_(dve, V_, u, it, "max")
                        V_.done(dve.tensor_tensor(pr[u][:], sim, mx[u][:].unsqueeze(2).to_broadcast([128, SEQ, 128]),
                                                  ALU.subtract), u, "sub")
                    for u in range(2):
                        await_(dve, A_, u, it, "exp")
                        V_.done(dve.tensor_reduce(sm[u][:], pr[u][:], AX, ALU.add), u, "sum")
                        await_(dve, V_, u, it, "sum")
                        V_.done(dve.reciprocal(sm[u][:], sm[u][:]), u, "rec")
                        await_(dve, V_, u, it, "rec")
                        V_.done(dve.tensor_tensor(pr[u][:], pr[u][:], sm[u][:].unsqueeze(2).to_broadcast([128, SEQ, 128]),
                                                  ALU.mult), u, "pn")
                    for u in range(2):
                        await_(dve, A_, u, it, "rs")
                        V_.done(dve.scalar_tensor_tensor(g["resid"][:, cols(it * 2 + u)], pX[u][:, 3, :], cb[:],
                                                         rs[u][:, 0, :], ALU.add, ALU.mult), u, "norm")
                over_pairs(dve, body)


def experts(nc, g):
    ctx = ExitStack()
    with ctx:
        st = Stage(nc, ctx, "f",
                   pe="sim down up0 up1 g0 g1 g2 g3 out var",
                   act="s down sg0 ey ea ex sg1 sqo ln rs",
                   dve="xs top ix ixf hm0 best rep sel hm1 row z rz tau ne thr xw far far2 rest "
                       + " ".join(f"m{c} f{c} l{c}" for c in range(TILES)) + " w norm",
                   pool="pairs ey ea rel far0 far1 keep nt " + " ".join(f"v{c}" for c in range(TILES)))
        PE, A_, V_, P_, pX = st.PE, st.ACT, st.DVE, st.POOL, st.pX
        CHD = TILES * PKH
        W = {n: st.sb(n, s) for n, s in dict(wg=[128, DCD], wu=[128, DCD], bg=[128, BLK], bu=[128, BLK], wdT=[128, DCD],
                                             bd=[128, 1], downT=[128, NEXP],
                                             upT=[128, NEXP]).items()}
        km, wd, up, cb = st.sb("km", [128, 512]), st.sb("wd", [128, DCD]), st.sb("up", [128, NEXP]), st.sb("cb", [128, 1])
        xs = st.two("xs", [128, CH])
        S_ = st.two("S", [128, 2, CHD, NK])
        T_ = st.two("T", [128, 2, CHD, TOPK])
        ixu, ixf = st.two("ixu", [128, CHD, TOPK], U32), st.two("ixf", [128, CHD, TOPK])
        pairs, sel = st.two("pairs", [128, CHD, 64]), st.two("sel", [128, CHD, 64])
        best = st.two("best", [128, CHD, TOPK])
        ey, ea = st.two("ey", [128, CHD, NK]), st.two("ea", [128, CHD, ROWS])
        far = st.two("far", [128, CHD, 64])
        ne = far
        row, z, tau, thr = (st.two(n, s) for n, s in (("row", [128, CHD, 8]), ("z", [128, CHD]), ("tau", [128, CHD, 8]),
                                                      ("thr", [128, CHD, ROWS])))
        outr, rest = st.two("outr", [128, CHD, 8]), st.two("rest", [128, TILES])
        val = [st.two(f"val{k}_", [128, PKH, NEXP]) for k in range(2)]
        reach = st.sb("reach", [128, PKH, NEXP])
        flat = reach[:].rearrange("p h e -> p (h e)")
        wqT, keysT = flat[0:64, 0:1024], flat[0:64, 1024:1024 + 8 * NK]
        act_e = st.two("act_e", [128, BLK, CH])
        sg, hm = st.two("sg", [128, 2, CH]), st.two("hm", [128, BLK, CH])
        sq, rs = ([t[:, k, :] for t in sg] for k in range(2))
        ld = g["in"]
        g8 = lambda t: t.rearrange("p g (i j) -> p g i j", i=8)

        with nc.Block() as block:
            @block.sync
            def _(sp):
                load_weights(sp, W, ld, st.s_w)
                sp.dma_start(wqT, ld["wqT"]).then_inc(st.s_w, 16)
                sp.dma_start(keysT, ld["keysT"]).then_inc(st.s_w, 16)
            wready = 16 * (len(W) + 2)

            @block.gpsimd
            def _(pool):
                def body(it, first):
                    for u in range(2):
                        await_(pool, V_, u, it, "top")
                        sx, sy = T_[u][:, 0, :, :], T_[u][:, 1, :, :]
                        P_.done(pool.tensor_tensor(g8(pairs[u][:]), sx.unsqueeze(3).to_broadcast([128, CHD, 8, 8]),
                                                   sy.unsqueeze(2).to_broadcast([128, CHD, 8, 8]), ALU.add), u, "pairs")
                        P_.done(pool.tensor_tensor(ey[u][:], S_[u][:, 1, :, :], sy[:, :, 0:1].to_broadcast([128, CHD, NK]),
                                                   ALU.subtract), u, "ey")
                        P_.done(pool.tensor_tensor(ea[u][:], S_[u][:, 0, :, 0:ROWS],
                                                   sx[:, :, 0:1].to_broadcast([128, CHD, ROWS]), ALU.subtract), u, "ea")
                    for u in range(2):
                        await_(pool, V_, u, it, "sel")
                        P_.done(pool.tensor_tensor(pairs[u][:], pairs[u][:], best[u][:, :, 0:1].to_broadcast([128, CHD, 64]),
                                                   ALU.subtract), u, "rel")
                        P_.done(pool.tensor_scalar(far[u][:], sel[u][:], -BIG, BIG, ALU.mult, ALU.add), u, "far0")
                        await_(pool, P_, u, it, "far0")
                        P_.done(pool.tensor_tensor(g8(far[u][:]), g8(far[u][:]),
                                                   T_[u][:, 1, :, :].unsqueeze(2).to_broadcast([128, CHD, 8, 8]),
                                                   ALU.add), u, "far1")
                        await_(pool, A_, u, it, "ex")
                        P_.done(pool.tensor_tensor(pairs[u][:], pairs[u][:], sel[u][:], ALU.mult), u, "keep")
                    for u in range(2):
                        await_(pool, V_, u, it, "ne")
                        P_.done(pool.tensor_tensor(g8(ne[u][:]), g8(ne[u][:]),
                                                   tau[u][:].unsqueeze(2).to_broadcast([128, CHD, 8, 8]), ALU.add), u, "nt")
                    for c in range(TILES):
                        for u in range(2):
                            if c == 0:
                                await_(pool, V_, u, it, "xw")
                                await_(pool, A_, u, it, "ey")
                            if c >= 2:
                                await_(pool, PE, u, it, f"g{c - 2}")
                            elif not first:
                                await_(pool, PE, u, it - 1, f"g{c + 2}")
                            t = slice(c * PKH, (c + 1) * PKH)
                            P_.done(pool.tensor_tensor(val[c % 2][u][:].rearrange("p h (a b) -> p h a b", a=ROWS),
                                                       ey[u][:, t, :].unsqueeze(2).to_broadcast([128, PKH, ROWS, NK]),
                                                       ea[u][:, t, :].unsqueeze(3).to_broadcast([128, PKH, ROWS, NK]),
                                                       ALU.mult), u, f"v{c}")
                over_pairs(pool, body)

            @block.tensor
            def _(pe):
                pe.wait_ge(st.s_w, wready)
                for k in range(8):
                    pe.matmul(pX[0][:, 0, k * NK:(k + 1) * NK], wqT[:, k * 128:(k + 1) * 128], keysT[:, k * NK:(k + 1) * NK], start=True, stop=True)
                centred_rows(pe, pX[0][:, 1, :], W["wdT"], BLK, g["cen"][:])
                centred_rows(pe, pX[0][:, 2, :], W["upT"], BLK, g["cen"][:])
                pe.matmul(pX[0][:, 3, 0:1], g["cen"][:], W["bd"][:], start=True, stop=True).then_inc(st.s_prep, 1)
                pe.wait_ge(st.s_copied, 1)

                def up_proj(u, k, step):
                    for j in range(2):
                        b = 2 * k + j
                        pe.matmul(pX[u][:, j, :], W["wg"][:, b * 128:(b + 1) * 128], xs[u][:], start=True, stop=True)
                        mm = pe.matmul(pX[u][:, 2 + j, :], W["wu"][:, b * 128:(b + 1) * 128], xs[u][:], start=True, stop=True)
                    PE.done(mm, u, step)

                def body(it, first):
                    for u in range(2):
                        await_(pe, V_, u, it, "xs")
                        for c in range(TILES):
                            mm = pe.matmul(pX[u][:, c, :], xs[u][:, c * 128:(c + 1) * 128], km[:], start=True, stop=True)
                        PE.done(mm, u, "sim")
                    for u in range(2):
                        await_(pe, A_, u, it, "s")
                        for b in range(BLK):
                            mm = pe.matmul(pX[u][:, b, :], W["downT"][:, b * 128:(b + 1) * 128], xs[u][:], start=True, stop=True)
                        PE.done(mm, u, "down")
                    for u in range(2):
                        await_(pe, A_, u, it, "down")
                        up_proj(u, 0, "up0")
                    for u in range(2):
                        await_(pe, V_, u, it, "hm0")
                        up_proj(u, 1, "up1")
                    for c in range(TILES):
                        for u in range(2):
                            if c == 0:
                                await_(pe, V_, u, it, "hm1")
                            await_(pe, V_, u, it, f"l{c}")
                            for b in range(BLK):
                                for h in range(PKH):
                                    mm = pe.matmul(pX[u][:, b, c * 128:(c + 1) * 128],
                                                   val[c % 2][u][:, h, b * 128:(b + 1) * 128], g["eye"][:],
                                                   start=(h == 0), stop=(h == PKH - 1))
                            PE.done(mm, u, f"g{c}")
                    for u in range(2):
                        await_(pe, V_, u, it, "w")
                        pe.matmul(pX[u][:, 0, :], g["cen"][:], xs[u][:], start=True, stop=False)
                        for b in range(BLK):
                            pe.matmul(pX[u][:, 0, :], wd[:, b * 128:(b + 1) * 128], hm[u][:, b, :], start=False, stop=False)
                        for b in range(BLK):
                            mm = pe.matmul(pX[u][:, 0, :], up[:, b * 128:(b + 1) * 128], act_e[u][:, b, :], start=False,
                                           stop=(b == BLK - 1))
                        PE.done(mm, u, "out")
                    for u in range(2):
                        await_(pe, A_, u, it, "sqo")
                        PE.done(pe.matmul(pX[u][:, 1, :], g["avg"][:], sq[u][:], start=True, stop=True), u, "var")
                over_pairs(pe, body)

            @block.scalar
            def _(act):
                act.wait_ge(st.s_prep, 1)
                for k, t in enumerate((km, wd, up)):
                    act.activation(t[:], pX[0][:, k, :], ACT.Copy)
                act.activation(cb[:], pX[0][:, 3, 0:1], ACT.Copy).then_inc(st.s_copied, 1)

                def gate(u, k, step):
                    for j in range(2):
                        a = act.activation(sg[u][:, j, :], pX[u][:, j, :], ACT.Silu, bias=W["bg"][:, 2 * k + j:2 * k + j + 1])
                    A_.done(a, u, step)

                def body(it, first):
                    for u in range(2):
                        await_(act, PE, u, it, "sim")
                        A_.done(act.activation(S_[u][:].rearrange("p s (c h) k -> p c s (h k)", c=TILES),
                                               pX[u][:].rearrange("p c (s n) -> p c s n", s=2), ACT.Copy), u, "s")
                    for u in range(2):
                        await_(act, PE, u, it, "down")
                        A_.done(act.activation(act_e[u][:], pX[u][:], ACT.Silu), u, "down")
                    for u in range(2):
                        await_(act, PE, u, it, "up0")
                        gate(u, 0, "sg0")
                    for u in range(2):
                        await_(act, P_, u, it, "ea")
                        A_.done(act.activation(ey[u][:], ey[u][:], ACT.Exp), u, "ey")
                        A_.done(act.activation(ea[u][:], ea[u][:], ACT.Exp), u, "ea")
                    for u in range(2):
                        await_(act, P_, u, it, "rel")
                        A_.done(act.activation(pairs[u][:], pairs[u][:], ACT.Exp), u, "ex")
                    for u in range(2):
                        await_(act, PE, u, it, "up1")
                        gate(u, 1, "sg1")
                    for u in range(2):
                        await_(act, PE, u, it, "out")
                        A_.done(act.activation(sq[u][:], pX[u][:, 0, :], ACT.Square, bias=cb[:]), u, "sqo")
                    for u in range(2):
                        await_(act, PE, u, it, "var")
                        rsqrt_steps(act, st, g, it, u, pX[u][:, 1, :], rs[u][:])
                over_pairs(act, body)

            @block.vector
            def _(dve):
                def hidden(it, u, k):
                    await_(dve, A_, u, it, f"sg{k}")
                    for j in range(2):
                        b = 2 * k + j
                        a = dve.scalar_tensor_tensor(hm[u][:, b, :], pX[u][:, 2 + j, :], W["bu"][:, b:b + 1], sg[u][:, j, :],
                                                     ALU.add, ALU.mult)
                    V_.done(a, u, f"hm{k}")

                def body(it, first):
                    for u in range(2):
                        take_input(dve, st, g, xs, it, u, first)
                    for u in range(2):
                        await_(dve, A_, u, it, "s")
                        st.carry(dve)
                        for s in range(2):
                            for k in range(CHD):
                                a = dve.max(T_[u][:, s, k, :], S_[u][:, s, k, :])
                        V_.done(a, u, "top")
                        await_(dve, V_, u, it, "top")
                        st.carry(dve)
                        for k in range(CHD):
                            a = dve.max_index(ixu[u][:, k, :], T_[u][:, 0, k, :], S_[u][:, 0, k, :])
                        V_.done(a, u, "ix")
                        await_(dve, V_, u, it, "ix")
                        V_.done(dve.tensor_copy(ixf[u][:], ixu[u][:]), u, "ixf")
                    for u in range(2):
                        hidden(it, u, 0)
                    for u in range(2):
                        await_(dve, P_, u, it, "pairs")
                        st.carry(dve)
                        for k in range(CHD):
                            a = dve.max(best[u][:, k, :], pairs[u][:, k, :])
                        V_.done(a, u, "best")
                        await_(dve, V_, u, it, "best")
                        st.carry(dve)
                        for k in range(CHD):
                            a = dve.match_replace(sel[u][:, k, :], best[u][:, k, :], pairs[u][:, k, :], -3e38)
                        V_.done(a, u, "rep")
                        await_(dve, V_, u, it, "rep")
                        V_.done(dve.tensor_tensor(sel[u][:], sel[u][:], pairs[u][:], ALU.is_lt), u, "sel")
                    for u in range(2):
                        hidden(it, u, 1)
                    for u in range(2):
                        await_(dve, P_, u, it, "keep")
                        V_.done(dve.tensor_reduce(row[u][:], g8(pairs[u][:]), AX, ALU.add), u, "row")
                        await_(dve, V_, u, it, "row")
                        V_.done(dve.tensor_reduce(z[u][:], row[u][:], AX, ALU.add), u, "z")
                        await_(dve, V_, u, it, "z")
                        V_.done(dve.reciprocal(z[u][:], z[u][:]), u, "rz")
                        await_(dve, P_, u, it, "far1")
                        V_.done(dve.tensor_reduce(tau[u][:], g8(far[u][:]), AX, ALU.min), u, "tau")
                        await_(dve, V_, u, it, "tau")
                        for a_ in range(ROWS):
                            a = dve.tensor_scalar(g8(ne[u][:])[:, :, a_, :], ixf[u][:], float(a_), BIG, ALU.not_equal, ALU.mult)
                        V_.done(a, u, "ne")
                    for u in range(2):
                        await_(dve, P_, u, it, "nt")
                        V_.done(dve.tensor_reduce(thr[u][:], g8(ne[u][:]), AX, ALU.min), u, "thr")
                        await_(dve, A_, u, it, "ea")
                        zb = z[u][:].unsqueeze(2).to_broadcast([128, CHD, 8])
                        V_.done(dve.tensor_tensor(ea[u][:], ea[u][:], zb, ALU.mult), u, "xw")
                        V_.done(dve.scalar_tensor_tensor(outr[u][:], ixf[u][:], float(ROWS), row[u][:], ALU.is_ge, ALU.mult),
                                u, "far")
                        await_(dve, V_, u, it, "far")
                        V_.done(dve.tensor_tensor(outr[u][:], outr[u][:], zb, ALU.mult), u, "far2")
                        await_(dve, V_, u, it, "far2")
                        V_.done(dve.tensor_reduce(rest[u][:], outr[u][:].rearrange("p (c h) i -> p c (h i)", c=TILES),
                                                  AX, ALU.add), u, "rest")
                    for c in range(TILES):
                        for u in range(2):
                            t = slice(c * PKH, (c + 1) * PKH)
                            v = val[c % 2][u]
                            if u == 1:
                                await_(dve, V_, 0, it, f"f{c}")
                            elif c > 0:
                                await_(dve, V_, 1, it, f"f{c - 1}")
                            elif not first:
                                await_(dve, V_, 1, it - 1, f"f{TILES - 1}")
                            V_.done(dve.tensor_tensor(reach[:].rearrange("p h (a b) -> p h a b", a=ROWS),
                                                      S_[u][:, 1, t, :].unsqueeze(2).to_broadcast([128, PKH, ROWS, NK]),
                                                      thr[u][:, t, :].unsqueeze(3).to_broadcast([128, PKH, ROWS, NK]),
                                                      ALU.is_ge), u, f"m{c}")
                            await_(dve, V_, u, it, f"m{c}")
                            await_(dve, P_, u, it, f"v{c}")
                            V_.done(dve.tensor_tensor(v[:], reach[:], v[:], ALU.mult), u, f"f{c}")
                            await_(dve, V_, u, it, f"f{c}")
                            last = v[:, PKH - 1, NEXP - 1:NEXP]
                            V_.done(dve.tensor_tensor(last, last, rest[u][:, c:c + 1], ALU.add), u, f"l{c}")
                    for u in range(2):
                        await_(dve, PE, u, it, f"g{TILES - 1}")
                        V_.done(dve.tensor_tensor(act_e[u][:], pX[u][:], act_e[u][:], ALU.mult), u, "w")
                    for u in range(2):
                        await_(dve, A_, u, it, "rs")
                        V_.done(dve.scalar_tensor_tensor(g["resid"][:, cols(it * 2 + u)], pX[u][:, 0, :], cb[:],
                                                         rs[u][:], ALU.add, ALU.mult), u, "norm")
                dve.wait_ge(st.s_w, wready)
                dve.wait_ge(st.s_copied, 1)
                over_pairs(dve, body)


def gated_scan(nc, g):
    ctx = ExitStack()
    with ctx:
        st = Stage(nc, ctx, "r", pe="ms uv lam out var", act="sqi lni rsi uz lam sqo ln rs",
                   dve="xs h one in zero scan gate norm", pool="")
        PE, A_, V_, P_, pX = st.PE, st.ACT, st.DVE, st.POOL, st.pX
        W = {n: st.sb(n, s) for n, s in dict(rnorm=[128, 1], rwin=[128, 4 * 128], rwdt=[128, HALF, INNER], rbdt=[128, HALF],
                                             rwoT=[128, HALF * 128]).items()}
        wo = st.sb("wo", [128, HALF * 128])
        xs, sq, rs, hn = (st.two(n, [128, CH]) for n in ("xs", "sq", "rs", "hn"))
        uz = st.two("uz", [128, 4, CH])
        lam, one, s_ = (st.two(n, [128, HALF, CH]) for n in ("lam", "one", "s"))
        ld = g["in"]

        with nc.Block() as block:
            @block.sync
            def _(sp):
                load_weights(sp, W, ld, st.s_w)

            @block.tensor
            def _(pe):
                pe.wait_ge(st.s_w, 16 * len(W))
                centred_rows(pe, pX[0][:, 0, :], W["rwoT"], HALF, g["cen"][:]).then_inc(st.s_prep, 1)
                pe.wait_ge(st.s_copied, 1)

                def body(it, first):
                    for u in range(2):
                        await_(pe, A_, u, it, "sqi")
                        PE.done(pe.matmul(pX[u][:, 0, :], g["avg"][:], sq[u][:], start=True, stop=True), u, "ms")
                    for u in range(2):
                        await_(pe, V_, u, it, "h")
                        for b in range(4):
                            mm = pe.matmul(pX[u][:, b, :], W["rwin"][:, b * 128:(b + 1) * 128], hn[u][:], start=True, stop=True)
                        PE.done(mm, u, "uv")
                    for u in range(2):
                        await_(pe, A_, u, it, "uz")
                        for h in range(HALF):
                            for k in range(HALF):
                                mm = pe.matmul(pX[u][:, h, :], W["rwdt"][:, k, h * 128:(h + 1) * 128], uz[u][:, k, :],
                                               start=(k == 0), stop=(k == HALF - 1))
                        PE.done(mm, u, "lam")
                    for u in range(2):
                        await_(pe, V_, u, it, "gate")
                        pe.matmul(pX[u][:, 2, :], g["cen2"][:], xs[u][:], start=True, stop=False)
                        for k in range(HALF):
                            mm = pe.matmul(pX[u][:, 2, :], wo[:, k * 128:(k + 1) * 128], s_[u][:, k, :], start=False,
                                           stop=(k == HALF - 1))
                        PE.done(mm, u, "out")
                    for u in range(2):
                        await_(pe, A_, u, it, "sqo")
                        PE.done(pe.matmul(pX[u][:, 3, :], g["avg"][:], sq[u][:], start=True, stop=True), u, "var")
                over_pairs(pe, body)

            @block.scalar
            def _(act):
                act.wait_ge(st.s_prep, 1)
                act.activation(wo[:], pX[0][:, 0, 0:HALF * 128], ACT.Copy).then_inc(st.s_copied, 1)

                def body(it, first):
                    for u in range(2):
                        await_(act, V_, u, it, "xs")
                        A_.done(act.activation(sq[u][:], xs[u][:], ACT.Square), u, "sqi")
                    for u in range(2):
                        await_(act, PE, u, it, "ms")
                        A_.done(act.activation(rs[u][:], pX[u][:, 0, :], ACT.Ln, bias=g["eps"][:]), u, "lni")
                        await_(act, A_, u, it, "lni")
                        A_.done(act.activation(rs[u][:], rs[u][:], ACT.Exp, scale=-0.5), u, "rsi")
                    for u in range(2):
                        await_(act, PE, u, it, "uv")
                        A_.done(act.activation(uz[u][:], pX[u][:], ACT.Silu), u, "uz")
                    for u in range(2):
                        await_(act, PE, u, it, "lam")
                        for h in range(HALF):
                            a = act.activation(lam[u][:, h, :], pX[u][:, h, :], ACT.Sigmoid, bias=W["rbdt"][:, h:h + 1])
                        A_.done(a, u, "lam")
                    for u in range(2):
                        await_(act, PE, u, it, "out")
                        A_.done(act.activation(sq[u][:], pX[u][:, 2, :], ACT.Square), u, "sqo")
                    for u in range(2):
                        await_(act, PE, u, it, "var")
                        rsqrt_steps(act, st, g, it, u, pX[u][:, 3, :], rs[u][:])
                over_pairs(act, body)

            @block.vector
            def _(dve):
                dve.wait_ge(st.s_w, 16 * len(W))
                flat = lambda t: t.rearrange("p h t -> p (h t)")

                def body(it, first):
                    for u in range(2):
                        take_input(dve, st, g, xs, it, u, first)
                    for u in range(2):
                        await_(dve, A_, u, it, "rsi")
                        V_.done(dve.scalar_tensor_tensor(hn[u][:], xs[u][:], W["rnorm"][:], rs[u][:], ALU.mult, ALU.mult),
                                u, "h")
                    for u in range(2):
                        await_(dve, A_, u, it, "lam")
                        V_.done(dve.tensor_scalar(one[u][:], lam[u][:], -1.0, 1.0, ALU.mult, ALU.add), u, "one")
                        await_(dve, V_, u, it, "one")
                        V_.done(dve.tensor_tensor(one[u][:], one[u][:], uz[u][:, 0:HALF, :], ALU.mult), u, "in")
                        V_.done(dve.memset(flat(lam[u][:]).rearrange("p (s t) -> p s t", t=S)[:, :, 0:1], 0.0), u, "zero")
                        await_(dve, V_, u, it, "zero")
                        V_.done(dve.tensor_tensor_scan(flat(s_[u][:]), flat(lam[u][:]), flat(one[u][:]), 0.0, ALU.mult,
                                                       ALU.add), u, "scan")
                        await_(dve, V_, u, it, "scan")
                        V_.done(dve.tensor_tensor(s_[u][:], s_[u][:], uz[u][:, HALF:4, :], ALU.mult), u, "gate")
                    for u in range(2):
                        await_(dve, A_, u, it, "rs")
                        V_.done(dve.tensor_tensor(g["resid"][:, cols(it * 2 + u)], pX[u][:, 2, :], rs[u][:], ALU.mult),
                                u, "norm")
                over_pairs(dve, body)


def context_experts(nc, g):
    ctx = ExitStack()
    with ctx:
        st = Stage(nc, ctx, "e", pe="x1 out cen var", act="gelu sqo ln rs", dve="xs h add norm", pool="")
        PE, A_, V_, P_, pX = st.PE, st.ACT, st.DVE, st.POOL, st.pX
        xs, xr, sq, rs, cT = (st.two(n, [128, CH]) for n in ("xs", "xr", "sq", "rs", "cT"))
        cr = st.two("cr", [128, SEQ // 2, 128])
        hT = st.two("hT", [128, SEQ // 2, S])
        s_c = [st.sem(f"ctx{u}") for u in range(2)]
        ld = g["in"]

        with nc.Block() as block:
            @block.sync
            def _(sp):
                def load(c, u):
                    sp.dma_start(cT[u][:], ld["ctxT"][:, cols(c)]).then_inc(s_c[u], 16)
                    sp.dma_start(cr[u][:], ld["ctxrow"][:, bass.ds(c * (SEQ // 2), SEQ // 2), :]).then_inc(s_c[u], 16)
                for u in range(2):
                    load(u, u)
                with sp.Fori(0, NCH // 2 - 1) as it:
                    for u in range(2):
                        await_(sp, PE, u, it, "out")
                        load(it * 2 + 2 + u, u)

            @block.tensor
            def _(pe):
                def body(it, first):
                    for u in range(2):
                        pe.wait_ge(s_c[u], (it + 1) * 32)
                        await_(pe, V_, u, it, "xs")
                        for b in range(SEQ):
                            r, pair = b % 2, b // 2
                            mm = pe.matmul(pX[u][r * S:(r + 1) * S, 0, pair * S:(pair + 1) * S], cT[u][:, b * S:(b + 1) * S],
                                           xs[u][:, b * S:(b + 1) * S], start=True, stop=True)
                        PE.done(mm, u, "x1")
                    for u in range(2):
                        await_(pe, V_, u, it, "h")
                        for b in range(SEQ):
                            r, pair = b % 2, b // 2
                            mm = pe.matmul(pX[u][:, 1 + r, pair * S:(pair + 1) * S], cr[u][r * S:(r + 1) * S, pair, :],
                                           hT[u][r * S:(r + 1) * S, pair, :], start=True, stop=True)
                        PE.done(mm, u, "out")
                    for u in range(2):
                        await_(pe, V_, u, it, "add")
                        PE.done(pe.matmul(pX[u][:, 3, :], g["cen"][:], xr[u][:], start=True, stop=True), u, "cen")
                    for u in range(2):
                        await_(pe, A_, u, it, "sqo")
                        PE.done(pe.matmul(pX[u][:, 0, :], g["avg"][:], sq[u][:], start=True, stop=True), u, "var")
                over_pairs(pe, body)

            @block.scalar
            def _(act):
                def body(it, first):
                    for u in range(2):
                        await_(act, PE, u, it, "x1")
                        A_.done(act.activation(hT[u][:].rearrange("p a t -> p (a t)"), pX[u][:, 0, 0:CH // 2],
                                               ACT.Gelu_apprx_tanh), u, "gelu")
                    for u in range(2):
                        await_(act, PE, u, it, "cen")
                        A_.done(act.activation(sq[u][:], pX[u][:, 3, :], ACT.Square), u, "sqo")
                    for u in range(2):
                        await_(act, PE, u, it, "var")
                        rsqrt_steps(act, st, g, it, u, pX[u][:, 0, :], rs[u][:])
                over_pairs(act, body)

            @block.vector
            def _(dve):
                def body(it, first):
                    for u in range(2):
                        take_input(dve, st, g, xs, it, u, first)
                    for u in range(2):
                        await_(dve, A_, u, it, "gelu")
                        h = hT[u][:].rearrange("p a t -> p (a t)")
                        V_.done(dve.tensor_tensor(h, h, pX[u][:, 0, 0:CH // 2], ALU.mult), u, "h")
                    for u in range(2):
                        await_(dve, PE, u, it, "out")
                        V_.done(dve.tensor_tensor(
                            xr[u][:].rearrange("p (a r t) -> p r a t", r=2, t=S),
                            xs[u][:].rearrange("p (a r t) -> p r a t", r=2, t=S),
                            pX[u][:, 1:3, 0:CH // 2].rearrange("p r (a t) -> p r a t", t=S), ALU.add), u, "add")
                    for u in range(2):
                        await_(dve, A_, u, it, "rs")
                        V_.done(dve.tensor_tensor(g["resid"][:, cols(it * 2 + u)], pX[u][:, 3, :], rs[u][:], ALU.mult),
                                u, "norm")
                over_pairs(dve, body)


def moe(nc, g):
    ALLX = EXPERTS + 1
    ctx = ExitStack()
    with ctx:
        st = Stage(nc, ctx, "g",
                   pe="lg cwT " + " ".join(f"ab{e} ac{e}" for e in range(ALLX)) + " var",
                   act="le hi cwf " + " ".join(f"sa{e}" for e in range(ALLX)) + " sqo ln rs",
                   dve="xs lmax lsub ls lr p top ix ixf eq0 eq1 eqs cw r1 mid lo hid0 "
                       + " ".join(f"g{e} hid{e}" for e in range(1, ALLX)) + " norm",
                   pool="")
        PE, A_, V_, P_, pX = st.PE, st.ACT, st.DVE, st.POOL, st.pX
        W = {n: st.sb(n, s) for n, s in dict(gw=[128, EXPERTS], gb=[1, EXPERTS], one1=[1, 128], iota8=[128, EXPERTS],
                                             w1=[128, ALLX, 2 * FFN], b1=[128, ALLX, 2], w2T=[128, ALLX * FFN],
                                             rb2T=[128, EXPERTS], sb2=[128, 1]).items()}
        w2, rb2, cb = st.sb("w2", [128, ALLX * 128]), st.sb("rb2", [EXPERTS, 128]), st.sb("cb", [128, 1])
        xs, sq, rs, sa, hid, res = (st.two(n, [128, CH]) for n in ("xs", "sq", "rs", "sa", "hid", "res"))
        lg, eq = st.two("lg", [128, TILES, 8]), st.two("eq", [128, 2, TILES, 8])
        lm, top, ixu, ixf = (st.two("lm", [128, TILES]), st.two("top", [128, TILES, 8]),
                             st.two("ixu", [128, TILES, 8], U32), st.two("ixf", [128, TILES, 8]))
        cw3 = st.two("cw3", [128, TILES, 3, 32])
        parts, r1, cwf = st.two("parts", [96, CH], BF16), st.two("r1", [64, CH]), st.two("cwf", [EXPERTS, CH])
        s_out = [st.sem(f"out{u}") for u in range(2)]
        s_zero = st.sem("zero")
        ld = g["in"]

        with nc.Block() as block:
            @block.sync
            def _(sp):
                load_weights(sp, W, ld, st.s_w)
                with sp.Fori(0, NCH // 2) as it:
                    for u in range(2):
                        await_(sp, V_, u, it, "norm")
                        sp.dma_start(g["out"][:, cols(it * 2 + u)], res[u][:]).then_inc(s_out[u], 16)
                for u in range(2):
                    sp.wait_ge(s_out[u], 16 * (NCH // 2))

            @block.tensor
            def _(pe):
                pe.wait_ge(st.s_w, 16 * len(W))
                for b in range(3):
                    n = min(4, ALLX - 4 * b)
                    centred_rows(pe, pX[0][:, b, :], W["w2T"][:, 512 * b:], n, g["cen"][:])
                pe.matmul(pX[0][0:EXPERTS, 3, 0:128], W["rb2T"][:], g["cen"][:], start=True, stop=True)
                pe.matmul(pX[0][:, 3, 128:129], g["cen"][:], W["sb2"][:], start=True, stop=True).then_inc(st.s_prep, 1)
                pe.wait_ge(st.s_copied, 1)

                def up(u, e):
                    for k in range(2):
                        mm = pe.matmul(pX[u][:, k, :], W["w1"][:, e, k * FFN:(k + 1) * FFN], xs[u][:], start=True, stop=True)
                    if e:
                        mm = pe.matmul(pX[u][:, 3, :], g["sel"][:, e - 1, :], parts[u][:], start=True, stop=True)
                    PE.done(mm, u, f"ab{e}")

                def body(it, first):
                    for u in range(2):
                        await_(pe, V_, u, it, "xs")
                        for c in range(TILES):
                            o = pX[u][:, 3, c * 8:(c + 1) * 8]
                            pe.matmul(o, xs[u][:, c * 128:(c + 1) * 128], W["gw"][:], start=True, stop=False)
                            mm = pe.matmul(o, W["one1"][:], W["gb"][:], start=False, stop=True)
                        PE.done(mm, u, "lg")
                    for u in range(2):
                        await_(pe, V_, u, it, "cw")
                        for c in range(TILES):
                            mm = pe.matmul(pX[u][0:96, 3, c * 128:(c + 1) * 128],
                                           cw3[u][:, c, :, :].rearrange("p r e -> p (r e)"), g["eye"][:], start=True, stop=True)
                        PE.done(mm, u, "cwT")
                    for e in range(ALLX):
                        for u in range(2):
                            if e == 0:
                                pe.wait_ge(st.s_w, 16 * len(W))
                            elif e == 1:
                                await_(pe, V_, u, it, "lo")
                                await_(pe, A_, u, it, "cwf")
                                await_(pe, V_, u, it, "hid0")
                            else:
                                await_(pe, V_, u, it, f"hid{e - 1}")
                            up(u, e)
                            if e == 0:
                                pe.matmul(pX[u][:, 2, :], g["cen"][:], xs[u][:], start=True, stop=False)
                        for u in range(2):
                            await_(pe, V_, u, it, f"hid{e}")
                            mm = pe.matmul(pX[u][:, 2, :], w2[:, e * 128:(e + 1) * 128], hid[u][:], start=False, stop=False)
                            if e == EXPERTS:
                                mm = pe.matmul(pX[u][:, 2, :], rb2[:], cwf[u][:], start=False, stop=True)
                            PE.done(mm, u, f"ac{e}")
                    for u in range(2):
                        await_(pe, A_, u, it, "sqo")
                        PE.done(pe.matmul(pX[u][:, 0, :], g["avg"][:], sq[u][:], start=True, stop=True), u, "var")
                over_pairs(pe, body)

            @block.scalar
            def _(act):
                act.wait_ge(st.s_prep, 1)
                act.activation(w2[:], pX[0][:, 0:3, :].rearrange("p b n -> p (b n)")[:, 0:ALLX * 128], ACT.Copy)
                act.activation(rb2[:], pX[0][0:EXPERTS, 3, 0:128], ACT.Copy)
                act.activation(cb[:], pX[0][:, 3, 128:129], ACT.Copy).then_inc(st.s_copied, 1)

                def body(it, first):
                    for u in range(2):
                        await_(act, V_, u, it, "lsub")
                        A_.done(act.activation(lg[u][:], lg[u][:], ACT.Exp), u, "le")
                    for u in range(2):
                        await_(act, PE, u, it, "cwT")
                        A_.done(act.activation(parts[u][:], pX[u][0:96, 3, :], ACT.Copy), u, "hi")
                        A_.done(act.activation(cwf[u][:], pX[u][0:EXPERTS, 3, :], ACT.Copy), u, "cwf")
                    for e in range(ALLX):
                        for u in range(2):
                            await_(act, PE, u, it, f"ab{e}")
                            A_.done(act.activation(sa[u][:], pX[u][:, 0, :], ACT.Silu, bias=W["b1"][:, e, 0:1]), u, f"sa{e}")
                    for u in range(2):
                        await_(act, PE, u, it, f"ac{EXPERTS}")
                        A_.done(act.activation(sq[u][:], pX[u][:, 2, :], ACT.Square, bias=cb[:]), u, "sqo")
                    for u in range(2):
                        await_(act, PE, u, it, "var")
                        rsqrt_steps(act, st, g, it, u, pX[u][:, 0, :], rs[u][:])
                over_pairs(act, body)

            @block.vector
            def _(dve):
                for u in range(2):
                    dve.memset(cw3[u][:], 0.0).then_inc(s_zero, 1)
                dve.wait_ge(s_zero, 2)
                dve.wait_ge(st.s_w, 16 * len(W))
                wide = lambda t: t.unsqueeze(2).to_broadcast([128, TILES, 8])

                def body(it, first):
                    for u in range(2):
                        take_input(dve, st, g, xs, it, u, first)
                    for u in range(2):
                        await_(dve, PE, u, it, "lg")
                        logits = pX[u][:, 3, 0:TILES * 8].rearrange("p (c e) -> p c e", e=8)
                        V_.done(dve.tensor_reduce(lm[u][:], logits, AX, ALU.max), u, "lmax")
                        await_(dve, V_, u, it, "lmax")
                        V_.done(dve.tensor_tensor(lg[u][:], logits, wide(lm[u][:]), ALU.subtract), u, "lsub")
                    for u in range(2):
                        await_(dve, A_, u, it, "le")
                        V_.done(dve.tensor_reduce(lm[u][:], lg[u][:], AX, ALU.add), u, "ls")
                        await_(dve, V_, u, it, "ls")
                        V_.done(dve.reciprocal(lm[u][:], lm[u][:]), u, "lr")
                        await_(dve, V_, u, it, "lr")
                        V_.done(dve.tensor_tensor(lg[u][:], lg[u][:], wide(lm[u][:]), ALU.mult), u, "p")
                        await_(dve, V_, u, it, "p")
                        st.carry(dve)
                        for c in range(TILES):
                            a = dve.max(top[u][:, c, :], lg[u][:, c, :])
                        V_.done(a, u, "top")
                        await_(dve, V_, u, it, "top")
                        st.carry(dve)
                        for c in range(TILES):
                            a = dve.max_index(ixu[u][:, c, :], top[u][:, c, :], lg[u][:, c, :])
                        V_.done(a, u, "ix")
                        await_(dve, V_, u, it, "ix")
                        V_.done(dve.tensor_copy(ixf[u][:], ixu[u][:]), u, "ixf")
                        await_(dve, V_, u, it, "ixf")
                        for k in range(2):
                            V_.done(dve.tensor_tensor(eq[u][:, k, :, :], W["iota8"][:, None, :].to_broadcast([128, TILES, 8]),
                                                      ixf[u][:, :, k:k + 1].to_broadcast([128, TILES, 8]), ALU.is_equal),
                                    u, f"eq{k}")
                        await_(dve, V_, u, it, "eq1")
                        V_.done(dve.tensor_tensor(eq[u][:, 0, :, :], eq[u][:, 0, :, :], eq[u][:, 1, :, :], ALU.add), u, "eqs")
                        await_(dve, V_, u, it, "eqs")
                        V_.done(dve.tensor_tensor(cw3[u][:, :, :, 0:8],
                                                  lg[u][:].unsqueeze(2).to_broadcast([128, TILES, 3, 8]),
                                                  eq[u][:, 0, :, :].unsqueeze(2).to_broadcast([128, TILES, 3, 8]),
                                                  ALU.mult), u, "cw")
                    for u in range(2):
                        await_(dve, A_, u, it, "cwf")
                        V_.done(dve.tensor_tensor(r1[u][:], pX[u][0:64, 3, :], parts[u][0:64, :], ALU.subtract), u, "r1")
                        await_(dve, V_, u, it, "r1")
                        V_.done(dve.tensor_copy(parts[u][0:64, :], r1[u][:]), u, "mid")
                        await_(dve, V_, u, it, "mid")
                        V_.done(dve.tensor_tensor(parts[u][0:32, :], r1[u][0:32, :], parts[u][0:32, :], ALU.subtract), u, "lo")
                    for e in range(ALLX):
                        for u in range(2):
                            await_(dve, A_, u, it, f"sa{e}")
                            if e:
                                await_(dve, PE, u, it, f"ac{e - 1}")
                            elif not first:
                                await_(dve, PE, u, it - 1, f"ac{EXPERTS}")
                            a = dve.scalar_tensor_tensor(hid[u][:], pX[u][:, 1, :], W["b1"][:, e, 1:2], sa[u][:], ALU.add,
                                                         ALU.mult)
                            if e:
                                V_.done(a, u, f"g{e}")
                                await_(dve, V_, u, it, f"g{e}")
                                a = dve.tensor_tensor(hid[u][:], hid[u][:], pX[u][:, 3, :], ALU.mult)
                            V_.done(a, u, f"hid{e}")
                    for u in range(2):
                        await_(dve, A_, u, it, "rs")
                        if not first:
                            dve.wait_ge(s_out[u], it * 16)
                        V_.done(dve.scalar_tensor_tensor(res[u][:], pX[u][:, 2, :], cb[:], rs[u][:], ALU.add, ALU.mult),
                                u, "norm")
                over_pairs(dve, body)


STAGES = [mamba, cross, experts, gated_scan, context_experts, moe]



def build(nc, ld, out, stages=None):
    g = {"in": ld, "out": out}
    ctx = ExitStack()
    with ctx:
        sb = lambda n, s, d=F32: ctx.enter_context(nc.sbuf_tensor(n, s, d))
        g["resid"] = sb("resid", [128, TOK])
        g["cen"] = sb("cen", [128, 128])
        g["cen2"] = sb("cen2", [128, 128])
        g["avg"] = sb("avg", [128, 128])
        g["avgh"] = sb("avgh", [128, 128])
        g["eye"] = sb("eye", [128, 128])
        self_ = sb("sel_f", [96, 128])
        g["sel"] = sb("sel", [96, 2 * NSTATE, 128], BF16)
        g["eps"] = sb("eps", [128, 1])
        g["s_const"] = ctx.enter_context(nc.semaphore("s_const"))
        with nc.Block() as block:
            @block.sync
            def _(sp):
                for n, t in (("cen", g["cen"]), ("avg", g["avg"]), ("avgh", g["avgh"]), ("eye", g["eye"])):
                    sp.dma_start(t[:], ld[n]).then_inc(g["s_const"], 16)
                sp.dma_start(self_[:, 0:32], ld["mod32"]).then_inc(g["s_const"], 16)

            @block.vector
            def _(dve):
                dve.memset(g["eps"][:], EPS).then_inc(g["s_const"], 1)
                dve.wait_ge(g["s_const"], 81)
                dve.tensor_scalar(g["cen2"][:], g["cen"][:], 2.0, None, ALU.mult).then_inc(g["s_const"], 1)
                dve.tensor_copy(g["sel"][:], self_[:, 0:32].unsqueeze(2).to_broadcast([96, 32, 128]))\
                   .then_inc(g["s_const"], 1)
        g["const_ready"] = 83
        for stage in (stages or STAGES):
            stage(nc, g)
        if stages and stages[-1] is not moe:
            s = ctx.enter_context(nc.semaphore("dbg"))
            with nc.Block() as block:
                @block.sync
                def _(sp):
                    sp.dma_start(out, g["resid"][:]).then_inc(s, 16)
                    sp.wait_ge(s, 16)


def layout(x):
    f = lambda a: np.ascontiguousarray(a)
    eye = np.eye(128, dtype=np.float32)
    column = lambda v: v.reshape(-1, 1)
    halves = lambda v: f(v.reshape(HALF, 128).T)
    xp = x["L0_attn_x_proj_w"].T.reshape(HALF, 128, 96).transpose(1, 0, 2)
    a = {
        "xT": x["x"].reshape(TOK, D).T,
        "cen": eye - np.float32(1 / D), "avg": np.full((128, 128), 1 / D, np.float32), "eye": eye,
        "avgh": np.kron(np.eye(2, dtype=np.float32), np.full((64, 64), 1 / 64, np.float32)),
        "mod32": np.tile(np.eye(32, dtype=np.float32), (3, 1)),
        "win": x["L0_attn_in_proj_w"].T,
        "convw": np.broadcast_to(x["L0_attn_conv_w"].T[None], (128, KCONV, INNER)),
        "convb": halves(x["L0_attn_conv_b"]),
        "xproj": np.concatenate([xp[:, :, 0:64]] + [xp[:, :, 64:96]] * 3, axis=2),
        "dtproj": x["L0_attn_dt_proj_w"].T,
        "dtb": halves(x["L0_attn_dt_proj_b"]),
        "alog": x["L0_attn_A_log"].reshape(HALF, 128, NSTATE).transpose(1, 0, 2),
        "dpar": halves(x["L0_attn_D_param"]),
        "woT": x["L0_attn_out_proj_w"],
        "ctxT": x["ctx_1024"].reshape(TOK, D).T,
        "mask": x["mask_BxS2_bk0"].reshape(B // 2, 2, S).transpose(1, 0, 2).reshape(2, B // 2 * S),
        "xwq": x["L0_xattn_W_q"], "xwkv": x["L0_xattn_W_kv"], "xwoT": x["L0_xattn_W_out"].T,
        "xbo": column(x["L0_xattn_b_out"]),
        "gx": column(x["L0_xattn_ln_x_g"]), "bx": column(x["L0_xattn_ln_x_b"]),
        "gl": column(x["L0_xattn_ln_l_g"]), "bl": column(x["L0_xattn_ln_l_b"]),
        "gq": column(np.tile(x["L0_xattn_q_gamma"], 2)), "gk": column(np.tile(x["L0_xattn_k_gamma"], 2)),
        "wg": x["L0_ffn_Wg"], "wu": x["L0_ffn_Wu"], "bg": x["L0_ffn_bg"].reshape(BLK, 128).T,
        "bu": x["L0_ffn_bu"].reshape(BLK, 128).T, "wdT": x["L0_ffn_Wd"].T, "bd": column(x["L0_ffn_bd"]),
        "wqT": x["L0_ffn_Wq"].T.reshape(8, 64, 128).transpose(1, 0, 2).reshape(64, 8 * 128),
        "keysT": x["L0_ffn_keys"].transpose(3, 2, 0, 1).reshape(64, 8 * NK),
        "downT": x["L0_ffn_down_embed"].T, "upT": x["L0_ffn_up_embed"].T,
        "rnorm": column(x["L1_attn_w_norm"]), "rwin": x["L1_attn_W_in"].T,
        "rwdt": x["L1_attn_W_dt"].T.reshape(HALF, 128, INNER).transpose(1, 0, 2),
        "rbdt": halves(x["L1_attn_b_dt"]), "rwoT": x["L1_attn_W_out"],
        "ctxrow": x["ctx_1024"].reshape(B // 2, 2 * S, D).transpose(1, 0, 2),
        "gw": x["L1_ffn_gate_w"], "gb": x["L1_ffn_gate_b"].reshape(1, EXPERTS), "one1": np.ones((1, 128), np.float32),
        "iota8": np.tile(np.arange(EXPERTS, dtype=np.float32), (128, 1)),
        "w1": np.concatenate([x["L1_ffn_sw1"], x["L1_ffn_rw1"]]).transpose(1, 0, 2),
        "b1": np.concatenate([x["L1_ffn_sb1"], x["L1_ffn_rb1"]]).reshape(EXPERTS + 1, 2, FFN).transpose(2, 0, 1),
        "w2T": np.concatenate([x["L1_ffn_sw2"], x["L1_ffn_rw2"]]).transpose(2, 0, 1).reshape(D, (EXPERTS + 1) * FFN),
        "rb2T": x["L1_ffn_rb2"].T, "sb2": x["L1_ffn_sb2"].T,
    }
    return {k: f(v) for k, v in a.items()}


def kernel(**inputs):
    from concourse import bacc
    from concourse.bass_utils import run_bass_kernel_spmd

    nc = bacc.Bacc("TRN2", target_bir_lowering=False, num_devices=1)
    arrays = layout({k: np.asarray(v) for k, v in inputs.items()})
    ld = {k: nc.dram_tensor("in_" + k, a.shape, mybir.dt.from_np(a.dtype), kind="ExternalInput").ap()
          for k, a in arrays.items()}
    out = nc.dram_tensor("out", (D, TOK), F32, kind="ExternalOutput").ap()
    build(nc, ld, out)
    r = run_bass_kernel_spmd(nc, [{"in_" + k: a for k, a in arrays.items()}], core_ids=[0])
    return np.ascontiguousarray(r.results[0]["out"].T).reshape(B, S, D)
```

```python
from contextlib import ExitStack

import numpy as np
import concourse.bass as bass
from concourse import mybir

F32 = mybir.dt.float32
BF16 = mybir.dt.bfloat16
U8 = mybir.dt.uint8
U32 = mybir.dt.uint32
ALU = mybir.AluOpType
ACT = mybir.ActivationFunctionType
AX = mybir.AxisListType.X

D = 128
B, S = 128, 64
TOK = B * S
CH = 512
NCH = TOK // CH
SEQ = CH // S
TILES = CH // 128
EPS = 1e-5
BIG = 1e30

INNER = 256
HALF = INNER // 128
NSTATE, KCONV, RANK = 16, 4, 64
PAIRS = NSTATE // 2
AT_U, AT_Z, AT_HI, AT_SP = 3, 3, 5, 6

HEADS, HD = 2, 64

DCD = 512
BLK = DCD // 128
PKH, NK, TOPK = 4, 64, 8
NEXP = 512
ROWS = NEXP // NK

EXPERTS, FFN = 8, 128


def wait(eng, sem, value):
    if isinstance(value, int) and value <= 0:
        return
    eng.wait_ge(sem, value)


class Progress:

    def __init__(self, sems, steps):
        self.sems, self.steps, self.at = sems, steps, {}

    def value(self, it, step):
        return it * len(self.steps) + self.steps.index(step) + 1

    def done(self, ins, u, step):
        k = self.at.get(u, 0)
        assert self.steps[k % len(self.steps)] == step, (self.steps[k % len(self.steps)], step)
        self.at[u] = k + 1
        ins.then_inc(self.sems[u], 1)


def await_(eng, prog, u, it, step):
    if isinstance(it, int) and it < 0:
        return
    eng.wait_ge(prog.sems[u], prog.value(it, step))


def cols(i):
    return bass.ds(i * CH, CH)


def mamba(nc, g):
    ctx = ExitStack()
    with ctx:
        sb = lambda n, s, d=F32: ctx.enter_context(nc.sbuf_tensor(n, s, d))
        ps = lambda n, s: ctx.enter_context(nc.psum_tensor(n, s, F32))
        sem = lambda n: ctx.enter_context(nc.semaphore(n))
        W = {n: sb("m_" + n, s) for n, s in dict(
            win=[128, 4 * 128], convw=[128, KCONV, INNER], convb=[128, HALF], xproj=[128, HALF, 64 + 96],
            dtproj=[RANK, INNER], dtb=[128, HALF], alog=[128, HALF, NSTATE], dpar=[128, HALF],
            woT=[128, HALF * 128]).items()}
        wconv = sb("wconv", [128, KCONV, INNER])
        nega = sb("nega", [128, HALF, NSTATE])
        wout = sb("wout_c", [128, HALF, 128])
        xin = [sb(f"xin{q}", [128, CH]) for q in range(2)]
        xre = sb("xre", [128, CH])
        u = [sb(f"u{q}", [128, HALF, CH]) for q in range(2)]
        z = [sb(f"z{q}", [128, HALF, CH]) for q in range(2)]
        dt = [sb(f"dt{q}", [128, HALF, CH]) for q in range(2)]
        dtu = [sb(f"dtu{q}", [128, HALF, CH]) for q in range(2)]
        parts = [sb(f"parts{q}", [96, CH], BF16) for q in range(2)]
        dtin = sb("dtin", [RANK, CH])
        r1 = sb("r1", [64, CH])
        ab = sb("ab", [128, HALF, CH])
        rl = sb("rl", [128, HALF, CH])
        ex = sb("ex", [128, HALF, CH])
        ln = sb("ln", [128, HALF, CH])
        wm1 = sb("wm1", [128, HALF, CH])
        bs = [sb(f"bs{k}", [128, 2, CH]) for k in range(2)]
        dA = [sb(f"dA{k}", [128, 2, CH]) for k in range(4)]
        dbu = [sb(f"dbu{k}", [128, 2, CH]) for k in range(4)]
        hs = [sb(f"hs{k}", [128, 2, CH]) for k in range(2)]
        hc = [sb(f"hc{k}", [128, 2, CH]) for k in range(2)]
        yd = sb("yd", [128, HALF, CH])
        sq = sb("m_sq", [128, CH])
        rs = sb("m_rs", [128, CH])
        pB = ps("pB", [128, 2, CH])
        pC = ps("pC", [128, 2, CH])
        pY = ps("pY", [128, HALF, CH])
        mA = ps("mA", [128, CH])
        mB = ps("mB", [128, CH])

        s_w, s_wprep, s_wp, s_neg = sem("m_w"), sem("m_wprep"), sem("m_wp"), sem("m_neg")
        s_xin = [sem(f"s_xin{q}") for q in range(2)]
        s_B, s_C, s_ysum, s_xre = sem("s_B"), sem("s_C"), sem("s_ysum"), sem("s_xre")
        s_conv, s_res, s_xdbl, s_dtp, s_xc, s_var = (sem("s_" + n) for n in "conv res xdbl dtp xc var".split())
        s_bs, s_dA, s_u, s_z, s_hi, s_ab, s_ex, s_ln, s_sq, s_lnv, s_rs = (sem("s_" + n) for n in "bs dA u z hi ab ex ln sq lnv rs".split())
        s_dbu, s_t = sem("s_dbu"), sem("s_t")
        s_scan, s_hc, s_r1, s_mid, s_lo, s_wm1, s_c, s_dt, s_dtu, s_yd, s_yz, s_x1 = (
            sem("s_" + n) for n in "scan hc r1 mid lo wm1 c dt dtu yd yz x1".split())

        ld = g["in"]
        seqs = lambda ap: ap.rearrange("p (s t) -> p s t", t=S)

        def over_chunks(eng, body):
            for i in range(2):
                body(i, i % 2, i == 0, False)
            with eng.Fori(1, NCH // 2 - 1) as ib:
                for q in range(2):
                    body(ib * 2 + q, q, False, False)
            for i in range(NCH - 2, NCH):
                body(i, i % 2, False, i == NCH - 1)

        with nc.Block() as block:
            @block.sync
            def _(sp):
                for n in W:
                    sp.dma_start(W[n][:], ld[n]).then_inc(s_w, 16)
                sp.dma_start(xin[0][:], ld["xT"][:, 0:CH]).then_inc(s_xin[0], 16)

                def body(i, q, first, last):
                    if not last:
                        wait(sp, s_res, i)
                        sp.dma_start(xin[1 - q][:], ld["xT"][:, cols(i + 1)]).then_inc(s_xin[1 - q], 16)
                    wait(sp, s_xc, i)
                    sp.dma_start(xre[:], ld["xT"][:, cols(i)]).then_inc(s_xre, 16)

                over_chunks(sp, body)

            @block.tensor
            def _(pe):
                pe.wait_ge(s_w, 16 * len(W))
                pe.wait_ge(g["s_const"], g["const_ready"])
                for h in range(HALF):
                    mm = pe.matmul(mA[:, h * 128:(h + 1) * 128], W["woT"][:, h * 128:(h + 1) * 128], g["cen"][:],
                                   start=True, stop=True)
                mm.then_inc(s_wprep, 1)
                pe.wait_ge(s_wp, 1 + KCONV)

                def conv(n, q, h, xin_count):
                    if h == 0:
                        pe.wait_ge(s_xin[q], xin_count)
                        wait(pe, s_x1, n - 2)
                    m = (mA, mB)[h]
                    x3 = seqs(xin[q][:])
                    for k in reversed(range(KCONV)):
                        sh = KCONV - 1 - k
                        mm = pe.matmul(seqs(m[:])[:, :, sh:S], wconv[:, k, h * 128:(h + 1) * 128],
                                       x3[:, :, 0:S - sh], start=(sh == 0), stop=(k == 0))
                    mm.then_inc(s_conv, 1)

                def res(n, q):
                    pe.wait_ge(s_u, n + 1)
                    for h, m in ((0, mA), (1, mB)):
                        mm = pe.matmul(m[:], W["win"][:, INNER + h * 128:INNER + (h + 1) * 128], xin[q][:],
                                       start=True, stop=True)
                    mm.then_inc(s_res, 1)

                def xdbl(n, q):
                    pe.wait_ge(s_z, n + 1)
                    for h in range(HALF):
                        pe.matmul(mA[0:96, :], W["xproj"][:, h, RANK:RANK + 96], u[q][:, h, :],
                                  start=(h == 0), stop=(h == HALF - 1))
                    for h in range(HALF):
                        mm = pe.matmul(mB[0:RANK, :], W["xproj"][:, h, 0:RANK], u[q][:, h, :],
                                       start=(h == 0), stop=(h == HALF - 1))
                    mm.then_inc(s_xdbl, 1)

                def dtp(n, q):
                    pe.wait_ge(s_hi, n + 1)
                    pe.wait_ge(s_r1, n + 1)
                    for h, m in ((0, mA), (1, mB)):
                        mm = pe.matmul(m[:], W["dtproj"][:, h * 128:(h + 1) * 128], dtin[:], start=True, stop=True)
                    mm.then_inc(s_dtp, 1)

                def spread(row, m, q, done):
                    for j in range(2):
                        mm = pe.matmul(m[:, j, :], g["sel"][:, row + j, :], parts[q][:], start=True, stop=True)
                    mm.then_inc(done, 1)

                def centre(n):
                    pe.wait_ge(s_xre, 16 * (n + 1))
                    pe.wait_ge(s_yz, n + 1)
                    pe.matmul(mA[:], g["cen"][:], xre[:], start=True, stop=False)
                    for h in range(HALF):
                        mm = pe.matmul(mA[:], wout[:, h, :], yd[:, h, :], start=False, stop=(h == HALF - 1))
                    mm.then_inc(s_xc, 1)

                def variance(n):
                    pe.wait_ge(s_sq, n + 1)
                    pe.matmul(mB[:], g["avg"][:], sq[:], start=True, stop=True).then_inc(s_var, 1)

                def body(i, q, first, last):
                    xin_count = 16 if first else ((i + 1 - (1 - q)) // 2 + 1) * 16
                    for p in range(PAIRS):
                        P = i * PAIRS + p

                        def between():
                            if p < PAIRS - 2 or not last:
                                if p == PAIRS - 2:
                                    pe.wait_ge(s_lo, i + 2)
                                pe.wait_ge(s_bs, P + 2)
                                spread(2 * ((p + 2) % PAIRS), pB, q if p < PAIRS - 2 else 1 - q, s_B)
                            if not last and p < 2:
                                conv(i + 1, 1 - q, p, xin_count)
                            if not last and p == 2:
                                res(i + 1, 1 - q)
                            if not last and p == 3:
                                xdbl(i + 1, 1 - q)
                            if not last and p == 4:
                                dtp(i + 1, 1 - q)
                            if not first and p == 5:
                                if not last:
                                    pe.wait_ge(s_ab, i + 2)
                                centre(i - 1)
                            if not first and p == 6:
                                variance(i - 1)

                        if p == 0:
                            between()
                            wait(pe, s_yd, i)
                        for h in range(HALF):
                            pe.wait_ge(s_hc, P * 2 + h + 1)
                            if h == 1 and (p < PAIRS - 1 or not last):
                                spread(NSTATE + 2 * ((p + 1) % PAIRS), pC, q if p < PAIRS - 1 else 1 - q, s_C)
                            for j in range(2):
                                mm = pe.matmul(pY[:, h, :], g["eye"][:], hc[h][:, j, :], start=(p == 0 and j == 0),
                                               stop=(p == PAIRS - 1 and j == 1))
                            mm.then_inc(s_ysum, 1)
                            if h == 0 and p:
                                between()

                for h in range(HALF):
                    conv(0, 0, h, 16)
                res(0, 0)
                xdbl(0, 0)
                dtp(0, 0)
                pe.wait_ge(s_lo, 1)
                spread(0, pB, 0, s_B)
                spread(NSTATE, pC, 0, s_C)
                pe.wait_ge(s_bs, 1)
                spread(2, pB, 0, s_B)
                over_chunks(pe, body)
                centre(NCH - 1)
                variance(NCH - 1)

            @block.scalar
            def _(act):
                act.wait_ge(s_w, 16 * len(W))
                act.activation(nega[:], W["alog"][:], ACT.Exp).then_inc(s_neg, 1)
                act.wait_ge(s_wprep, 1)
                act.activation(wout[:], mA[:, 0:HALF * 128].rearrange("p (h n) -> p h n", h=HALF), ACT.Copy)\
                   .then_inc(s_wp, 1)

                def drive(n, q):
                    wait(act, s_yz, n - 1)
                    for h, m in ((0, mA), (1, mB)):
                        act.wait_ge(s_conv, 2 * n + h + 1)
                        a = act.activation(u[q][:, h, :], m[:], ACT.Silu, bias=W["convb"][:, h:h + 1])
                    a.then_inc(s_u, 1)

                def gate(n, q):
                    act.wait_ge(s_res, n + 1)
                    for h, m in ((0, mA), (1, mB)):
                        a = act.activation(z[q][:, h, :], m[:], ACT.Silu)
                    a.then_inc(s_z, 1)

                def high(n, q):
                    act.wait_ge(s_xdbl, n + 1)
                    wait(act, s_C, (n - 1) * PAIRS)
                    act.activation(parts[q][:], mA[0:96, :], ACT.Copy)
                    wait(act, s_dtp, n)
                    act.activation(dtin[:], mB[0:RANK, :], ACT.Copy).then_inc(s_hi, 1)

                def softplus(n):
                    act.wait_ge(s_dtp, n + 1)
                    wait(act, s_dtu, n)
                    for h, m in ((0, mA), (1, mB)):
                        act.activation(ab[:, h, :], m[:], ACT.Abs, bias=W["dtb"][:, h:h + 1])
                        a = act.activation(rl[:, h, :], m[:], ACT.Relu, bias=W["dtb"][:, h:h + 1])
                    a.then_inc(s_ab, 1)
                    act.wait_ge(s_ab, n + 1)
                    act.activation(ex[:], ab[:], ACT.Exp, scale=-1.0).then_inc(s_ex, 1)
                    act.wait_ge(s_ex, n + 1)
                    act.activation(ln[:], ex[:], ACT.Ln, bias=1.0).then_inc(s_ln, 1)

                def squares(n):
                    act.wait_ge(s_xc, n + 1)
                    wait(act, s_var, n)
                    act.activation(sq[:], mA[:], ACT.Square).then_inc(s_sq, 1)

                def rsqrt(n):
                    act.wait_ge(s_var, n + 1)
                    wait(act, s_x1, n)
                    act.activation(rs[:], mB[:], ACT.Ln, bias=g["eps"][:]).then_inc(s_lnv, 1)
                    act.wait_ge(s_lnv, n + 1)
                    act.activation(rs[:], rs[:], ACT.Exp, scale=-0.5).then_inc(s_rs, 1)

                def body(i, q, first, last):
                    for p in range(PAIRS):
                        act.wait_ge(s_B, i * PAIRS + p + 1)
                        wait(act, s_dbu, (i * PAIRS + p) * 2 - 2)
                        act.activation(bs[p % 2][:], pB[:], ACT.Copy).then_inc(s_bs, 1)
                        if p == 0:
                            act.wait_ge(s_dt, i + 1)
                        for h in range(HALF):
                            k = (p * 2 + h) % 4
                            wait(act, s_scan, (i * PAIRS + p) * 2 + h - 3)
                            for j in range(2):
                                a = act.activation(seqs(dA[k][:, j, :])[:, :, 1:S], seqs(dt[q][:, h, :])[:, :, 1:S],
                                                   ACT.Exp, scale=nega[:, h, 2 * p + j:2 * p + j + 1])
                            a.then_inc(s_dA, 1)
                        if not last and p == AT_U:
                            drive(i + 1, 1 - q)
                        if not last and p == AT_Z:
                            gate(i + 1, 1 - q)
                        if not last and p == AT_HI:
                            high(i + 1, 1 - q)
                        if not last and p == AT_SP:
                            softplus(i + 1)
                        if not first and p == PAIRS - 1:
                            squares(i - 1)
                            rsqrt(i - 1)

                act.wait_ge(s_neg, 2)
                drive(0, 0)
                gate(0, 0)
                high(0, 0)
                softplus(0)
                over_chunks(act, body)
                squares(NCH - 1)
                rsqrt(NCH - 1)

            @block.gpsimd
            def _(pool):
                def relu_ln(n):
                    pool.wait_ge(s_ln, n + 1)
                    pool.tensor_tensor(ln[:], ln[:], rl[:], ALU.add).then_inc(s_t, 1)

                def body(i, q, first, last):
                    for p in range(PAIRS):
                        if p == 0:
                            pool.wait_ge(s_dtu, i + 1)
                        if not last and p == PAIRS - 1:
                            relu_ln(i + 1)
                        pool.wait_ge(s_bs, i * PAIRS + p + 1)
                        for h in range(HALF):
                            k = (p * 2 + h) % 4
                            wait(pool, s_scan, (i * PAIRS + p) * 2 + h - 3)
                            pool.tensor_tensor(dbu[k][:], dtu[q][:, h, None, :].to_broadcast([128, 2, CH]), bs[p % 2][:],
                                               ALU.mult).then_inc(s_dbu, 1)

                relu_ln(0)
                over_chunks(pool, body)

            @block.vector
            def _(dve):
                dve.wait_ge(s_w, 16 * len(W))
                for k in range(KCONV):
                    dve.tensor_tensor(wconv[:, k, :], W["win"][:, 0:INNER], W["convw"][:, k, :], ALU.mult)\
                       .then_inc(s_wp, 1)
                for k in range(4):
                    for j in range(2):
                        dve.memset(seqs(dA[k][:, j, :])[:, :, 0:1], 0.0)
                dve.wait_ge(s_neg, 1)
                dve.tensor_scalar(nega[:], nega[:], -1.0, None, ALU.mult).then_inc(s_neg, 1)

                def remainders(n, q):
                    dve.wait_ge(s_hi, n + 1)
                    dve.tensor_tensor(r1[:], mA[0:64, :], parts[q][0:64, :], ALU.subtract).then_inc(s_r1, 1)
                    dve.wait_ge(s_r1, n + 1)
                    dve.tensor_copy(parts[q][0:64, :], r1[:]).then_inc(s_mid, 1)
                    dve.wait_ge(s_mid, n + 1)
                    dve.tensor_tensor(parts[q][0:32, :], r1[0:32, :], parts[q][0:32, :], ALU.subtract).then_inc(s_lo, 1)

                def correction(n):
                    dve.wait_ge(s_ex, n + 1)
                    dve.tensor_scalar(wm1[:], ex[:], 1.0, -1.0, ALU.add, ALU.add).then_inc(s_wm1, 1)
                    dve.wait_ge(s_wm1, n + 1)
                    dve.tensor_tensor(wm1[:], ex[:], wm1[:], ALU.subtract).then_inc(s_c, 1)

                def step(n, q):
                    dve.wait_ge(s_c, n + 1)
                    dve.wait_ge(s_t, n + 1)
                    wait(dve, s_dA, (n - 1) * PAIRS * 2)
                    wait(dve, s_dbu, (n - 1) * PAIRS * 2)
                    dve.tensor_tensor(dt[q][:], wm1[:], ln[:], ALU.add).then_inc(s_dt, 1)
                    dve.wait_ge(s_dt, n + 1)
                    dve.tensor_tensor(dtu[q][:], dt[q][:], u[q][:], ALU.mult).then_inc(s_dtu, 1)

                def skip(n, q):
                    dve.wait_ge(s_ysum, (n + 1) * PAIRS * 2)
                    wait(dve, s_xc, n)
                    for h in range(HALF):
                        a = dve.scalar_tensor_tensor(yd[:, h, :], u[q][:, h, :], W["dpar"][:, h:h + 1], pY[:, h, :],
                                                     ALU.mult, ALU.add)
                    a.then_inc(s_yd, 1)

                def gated(n, q):
                    dve.wait_ge(s_yd, n + 1)
                    dve.tensor_tensor(yd[:], yd[:], z[q][:], ALU.mult).then_inc(s_yz, 1)

                def normed(n):
                    dve.wait_ge(s_rs, n + 1)
                    dve.tensor_tensor(g["resid"][:, cols(n)], mA[:], rs[:], ALU.mult).then_inc(s_x1, 1)

                def body(i, q, first, last):
                    for p in range(PAIRS):
                        for h in range(HALF):
                            k, n = (p * 2 + h) % 4, (i * PAIRS + p) * 2 + h
                            dve.wait_ge(s_dA, n + 1)
                            dve.wait_ge(s_dbu, n + 1)
                            wait(dve, s_hc, n - 1)
                            dve.tensor_tensor_scan(hs[h][:].rearrange("p j t -> p (j t)"),
                                                   dA[k][:].rearrange("p j t -> p (j t)"),
                                                   dbu[k][:].rearrange("p j t -> p (j t)"), 0.0, ALU.mult, ALU.add)\
                               .then_inc(s_scan, 1)
                            if not first and p == 0 and h == 0:
                                skip(i - 1, 1 - q)
                            dve.wait_ge(s_scan, n + 1)
                            dve.wait_ge(s_C, i * PAIRS + p + 1)
                            wait(dve, s_ysum, n - 1)
                            dve.tensor_tensor(hc[h][:], hs[h][:], pC[:], ALU.mult).then_inc(s_hc, 1)
                            if h == 1:
                                continue
                            if not first and p == 1:
                                gated(i - 1, 1 - q)
                            if not last and p == 4:
                                remainders(i + 1, 1 - q)
                            if not last and p == 5:
                                correction(i + 1)
                            if not last and p == 6:
                                step(i + 1, 1 - q)
                            if not first and p == PAIRS - 1:
                                normed(i - 1)

                remainders(0, 0)
                correction(0)
                step(0, 0)
                over_chunks(dve, body)
                skip(NCH - 1, (NCH - 1) % 2)
                gated(NCH - 1, (NCH - 1) % 2)
                normed(NCH - 1)


class Stage:

    def __init__(self, nc, ctx, tag, pe, act, dve, pool):
        self.nc, self.ctx, self.tag = nc, ctx, tag
        self.pX = [ctx.enter_context(nc.psum_tensor(f"{tag}_ps{u}", [128, 4, CH], F32)) for u in range(2)]
        streams = lambda e: [self.sem(f"{e}{u}") for u in range(2)]
        count = lambda e, steps: Progress(streams(e) if steps else [], steps.split())
        self.PE, self.ACT, self.DVE, self.POOL = count("pe", pe), count("act", act), count("dve", dve), count("pool", pool)
        self.ticks, self.n_ticks = self.sb("ticks", [128, 96]), 0
        self.s_w, self.s_prep, self.s_copied = self.sem("w"), self.sem("prep"), self.sem("copied")

    def carry(self, dve):
        dve.memset(self.ticks[:, self.n_ticks:self.n_ticks + 1], 0.0)
        self.n_ticks += 1

    def sem(self, n):
        return self.ctx.enter_context(self.nc.semaphore(f"{self.tag}_{n}"))

    def sb(self, n, s, d=F32):
        return self.ctx.enter_context(self.nc.sbuf_tensor(f"{self.tag}_{n}", s, d))

    def two(self, n, s, d=F32):
        return [self.sb(f"{n}{u}", s, d) for u in range(2)]


def over_slots(eng, slot):
    for n in range(4):
        slot(n // 2, n % 2, "ABC"[:n + 1])
    with eng.Fori(2, NCH // 2) as it:
        for u in range(2):
            slot(it, u, "ABC")
    slot(NCH // 2, 0, "BC")
    slot(NCH // 2, 1, "C")


def other(it, u):
    return (0, it) if u == 1 else (1, it - 1)


def over_pairs(eng, body):
    body(0, True)
    with eng.Fori(1, NCH // 2) as it:
        body(it, False)


def load_weights(eng, W, ld, sem):
    for n in W:
        eng.dma_start(W[n][:], ld[n]).then_inc(sem, 16)


def centred_rows(pe, psum, wT, blocks, cen):
    for b in range(blocks):
        mm = pe.matmul(psum[:, b * 128:(b + 1) * 128], wT[:, b * 128:(b + 1) * 128], cen, start=True, stop=True)
    return mm


def take_input(dve, st, g, xs, it, u, first):
    if not first:
        await_(dve, st.DVE, u, it - 1, "norm")
    st.DVE.done(dve.tensor_scalar(xs[u][:], g["resid"][:, cols(it * 2 + u)], 1.0, 0.0, ALU.mult, ALU.add), u, "xs")


def rsqrt_steps(act, st, g, it, u, src, rs):
    st.ACT.done(act.activation(rs, src, ACT.Ln, bias=g["eps"][:]), u, "ln")
    await_(act, st.ACT, u, it, "ln")
    st.ACT.done(act.activation(rs, rs, ACT.Exp, scale=-0.5), u, "rs")


def cross(nc, g):
    ctx = ExitStack()
    with ctx:
        st = Stage(nc, ctx, "x",
                   pe="cen var qk ms v sim pT av out vout",
                   act="sq lnc rsc sqk gq gk lnk rsk vs exp pT av sqo ln rs",
                   dve="xs hat affine guard qn mb mask max sub sum rec pn norm",
                   pool="")
        PE, A_, V_, P_, pX = st.PE, st.ACT, st.DVE, st.POOL, st.pX
        W = {n: st.sb(n, s) for n, s in dict(xwq=[128, 128], xwkv=[128, 256], xwoT=[128, 128], xbo=[128, 1], gx=[128, 1],
                                             bx=[128, 1], gl=[128, 1], bl=[128, 1], gq=[128, 1], gk=[128, 1]).items()}
        mask = st.sb("mask", [128, B // 2 * S], U8)
        wo, cb, gqs = st.sb("wo", [128, 128]), st.sb("cb", [128, 1]), st.sb("gqs", [128, 1])
        cin, xs = st.two("cin", [128, CH]), st.two("xs", [128, CH])
        sq, rs = st.two("sq", [128, 3, CH]), st.two("rs", [128, 3, CH])
        cn = st.two("cn", [128, 2, CH])
        qk = st.two("qk", [128, 3, CH])
        qn, kn = st.two("qn", [128, CH]), st.two("kn", [128, SEQ, 2, S])
        vs = st.two("vs", [128, SEQ, 128])
        mb = st.two("mb", [128, SEQ // 2, S])
        mx, sm = st.two("mx", [128, SEQ]), st.two("sm", [128, SEQ])
        pr, pT = st.two("pr", [128, SEQ, 128]), st.two("pT", [128, 2, CH])
        ao = st.two("ao", [128, CH])
        s_cin = [st.sem(f"cin{u}") for u in range(2)]
        ld = g["in"]

        with nc.Block() as block:
            @block.sync
            def _(sp):
                for u in range(2):
                    sp.dma_start(cin[u][:], ld["ctxT"][:, cols(u)]).then_inc(s_cin[u], 16)
                load_weights(sp, W, ld, st.s_w)
                for r in range(2):
                    sp.dma_start(mask[r * S:(r + 1) * S, :],
                                 ld["mask"][r:r + 1, :].to_broadcast([S, B // 2 * S])).then_inc(st.s_w, 16)
                with sp.Fori(0, NCH // 2 - 1) as it:
                    for u in range(2):
                        await_(sp, PE, u, it, "cen")
                        sp.dma_start(cin[u][:], ld["ctxT"][:, cols(it * 2 + 2 + u)]).then_inc(s_cin[u], 16)
            wready = 16 * (len(W) + 2)

            @block.tensor
            def _(pe):
                pe.wait_ge(st.s_w, wready)
                centred_rows(pe, pX[0][:, 0, :], W["xwoT"], 1, g["cen"][:])
                pe.matmul(pX[0][:, 0, 128:129], g["cen"][:], W["xbo"][:], start=True, stop=True).then_inc(st.s_prep, 1)
                pe.wait_ge(st.s_copied, 2)

                def body(it, first):
                    for u in range(2):
                        pe.wait_ge(s_cin[u], (it + 1) * 16)
                        await_(pe, V_, u, it, "xs")
                        pe.matmul(pX[u][:, 0, :], g["cen"][:], cin[u][:], start=True, stop=True)
                        PE.done(pe.matmul(pX[u][:, 1, :], g["cen"][:], xs[u][:], start=True, stop=True), u, "cen")
                    for u in range(2):
                        await_(pe, A_, u, it, "sq")
                        for k in range(2):
                            mm = pe.matmul(pX[u][:, 2 + k, :], g["avg"][:], sq[u][:, k, :], start=True, stop=True)
                        PE.done(mm, u, "var")
                    for u in range(2):
                        await_(pe, V_, u, it, "affine")
                        pe.matmul(pX[u][:, 0, :], W["xwq"][:], cn[u][:, 1, :], start=True, stop=True)
                        for k in range(2):
                            mm = pe.matmul(pX[u][:, 1 + k, :], W["xwkv"][:, 0:128], cn[u][:, k, :], start=True, stop=True)
                        PE.done(mm, u, "qk")
                    for u in range(2):
                        await_(pe, A_, u, it, "gk")
                        for k in range(3):
                            mm = pe.matmul(pX[u][:, k, :], g["avgh"][:], sq[u][:, k, :], start=True, stop=True)
                        PE.done(mm, u, "ms")
                    for u in range(2):
                        await_(pe, V_, u, it, "qn")
                        for b in range(SEQ):
                            for k in range(2):
                                mm = pe.matmul(pX[u][k * S:(k + 1) * S, 2 + b // 4, (b % 4) * 128:(b % 4 + 1) * 128],
                                               cn[u][:, k, b * S:(b + 1) * S], W["xwkv"][:, 128:256],
                                               start=True, stop=True)
                        PE.done(mm, u, "v")
                    for u in range(2):
                        for h in range(HEADS):
                            for b in range(SEQ):
                                r, pair = b % 2, b // 2
                                mm = pe.matmul(pX[u][r * S:(r + 1) * S, h, pair * 128:(pair + 1) * 128],
                                               qn[u][h * HD:(h + 1) * HD, b * S:(b + 1) * S],
                                               kn[u][h * HD:(h + 1) * HD, b, :, :].rearrange("p k t -> p (k t)"),
                                               start=True, stop=True)
                        PE.done(mm, u, "sim")
                    for u in range(2):
                        await_(pe, V_, u, it, "pn")
                        for k in range(SEQ):
                            mm = pe.transpose(pX[u][:, k // 4, (k % 4) * 128:(k % 4 + 1) * 128], pr[u][:, k, :],
                                              g["eye"][:])
                        PE.done(mm, u, "pT")
                    for u in range(2):
                        await_(pe, A_, u, it, "pT")
                        await_(pe, A_, u, it, "vs")
                        for b in range(SEQ):
                            for h in range(HEADS):
                                mm = pe.matmul(pX[u][h * HD:(h + 1) * HD, 2, b * S:(b + 1) * S],
                                               vs[u][:, b, h * HD:(h + 1) * HD],
                                               pT[u][:, h, b * S:(b + 1) * S], start=True, stop=True)
                        PE.done(mm, u, "av")
                    for u in range(2):
                        await_(pe, A_, u, it, "av")
                        pe.matmul(pX[u][:, 3, :], g["cen"][:], xs[u][:], start=True, stop=False)
                        PE.done(pe.matmul(pX[u][:, 3, :], wo[:], ao[u][:], start=False, stop=True), u, "out")
                    for u in range(2):
                        await_(pe, A_, u, it, "sqo")
                        PE.done(pe.matmul(pX[u][:, 0, :], g["avg"][:], sq[u][:, 0, :], start=True, stop=True), u, "vout")
                over_pairs(pe, body)

            @block.scalar
            def _(act):
                act.wait_ge(st.s_prep, 1)
                act.activation(wo[:], pX[0][:, 0, 0:128], ACT.Copy)
                act.activation(cb[:], pX[0][:, 0, 128:129], ACT.Copy).then_inc(st.s_copied, 1)

                def body(it, first):
                    for u in range(2):
                        await_(act, PE, u, it, "cen")
                        A_.done(act.activation(sq[u][:, 0:2, :], pX[u][:, 0:2, :], ACT.Square), u, "sq")
                    for u in range(2):
                        await_(act, PE, u, it, "var")
                        A_.done(act.activation(rs[u][:, 0:2, :], pX[u][:, 2:4, :], ACT.Ln, bias=g["eps"][:]), u, "lnc")
                        await_(act, A_, u, it, "lnc")
                        A_.done(act.activation(rs[u][:, 0:2, :], rs[u][:, 0:2, :], ACT.Exp, scale=-0.5), u, "rsc")
                    for u in range(2):
                        await_(act, PE, u, it, "qk")
                        A_.done(act.activation(sq[u][:], pX[u][:, 0:3, :], ACT.Square), u, "sqk")
                        A_.done(act.activation(qk[u][:, 0, :], pX[u][:, 0, :], ACT.Copy, scale=gqs[:]), u, "gq")
                        A_.done(act.activation(qk[u][:, 1:3, :], pX[u][:, 1:3, :], ACT.Copy, scale=W["gk"][:]), u, "gk")
                    for u in range(2):
                        await_(act, V_, u, it, "guard")
                        A_.done(act.activation(rs[u][:], rs[u][:], ACT.Ln), u, "lnk")
                        await_(act, A_, u, it, "lnk")
                        A_.done(act.activation(rs[u][:], rs[u][:], ACT.Exp, scale=-0.5), u, "rsk")
                    for u in range(2):
                        await_(act, PE, u, it, "v")
                        A_.done(act.activation(vs[u][:].rearrange("p (k b) d -> p k (b d)", k=2), pX[u][:, 2:4, :], ACT.Copy), u, "vs")
                    for u in range(2):
                        await_(act, V_, u, it, "sub")
                        A_.done(act.activation(pr[u][:], pr[u][:], ACT.Exp), u, "exp")
                    for u in range(2):
                        await_(act, PE, u, it, "pT")
                        A_.done(act.activation(pT[u][:], pX[u][:, 0:2, :], ACT.Copy), u, "pT")
                    for u in range(2):
                        await_(act, PE, u, it, "av")
                        A_.done(act.activation(ao[u][:], pX[u][:, 2, :], ACT.Copy), u, "av")
                    for u in range(2):
                        await_(act, PE, u, it, "out")
                        A_.done(act.activation(sq[u][:, 0, :], pX[u][:, 3, :], ACT.Square, bias=cb[:]), u, "sqo")
                    for u in range(2):
                        await_(act, PE, u, it, "vout")
                        rsqrt_steps(act, st, g, it, u, pX[u][:, 0, :], rs[u][:, 0, :])
                over_pairs(act, body)

            @block.vector
            def _(dve):
                dve.wait_ge(st.s_w, wready)
                dve.tensor_scalar(gqs[:], W["gq"][:], HD ** -0.5, None, ALU.mult).then_inc(st.s_copied, 1)

                def body(it, first):
                    for u in range(2):
                        take_input(dve, st, g, xs, it, u, first)
                    for u in range(2):
                        await_(dve, A_, u, it, "rsc")
                        V_.done(dve.tensor_tensor(cn[u][:], pX[u][:, 0:2, :], rs[u][:, 0:2, :], ALU.mult), u, "hat")
                        await_(dve, V_, u, it, "hat")
                        dve.tensor_scalar(cn[u][:, 0, :], cn[u][:, 0, :], W["gx"][:], W["bx"][:], ALU.mult, ALU.add)
                        V_.done(dve.tensor_scalar(cn[u][:, 1, :], cn[u][:, 1, :], W["gl"][:], W["bl"][:], ALU.mult,
                                                  ALU.add), u, "affine")
                    for u in range(2):
                        await_(dve, PE, u, it, "ms")
                        V_.done(dve.tensor_scalar(rs[u][:], pX[u][:, 0:3, :], 1e-16, None, ALU.max), u, "guard")
                    for u in range(2):
                        await_(dve, A_, u, it, "rsk")
                        dve.tensor_tensor(qn[u][:], qk[u][:, 0, :], rs[u][:, 0, :], ALU.mult)
                        V_.done(dve.tensor_tensor(kn[u][:].rearrange("p b k t -> p k b t"),
                                                  qk[u][:, 1:3, :].rearrange("p k (b t) -> p k b t", b=SEQ),
                                                  rs[u][:, 1:3, :].rearrange("p k (b t) -> p k b t", b=SEQ),
                                                  ALU.mult), u, "qn")
                    for u in range(2):
                        n = SEQ // 2 * S
                        V_.done(dve.tensor_scalar(mb[u][:].rearrange("p a t -> p (a t)"), mask[:, bass.ds((it * 2 + u) * n, n)],
                                                  -1.0, BIG, ALU.add, ALU.mult), u, "mb")
                        await_(dve, PE, u, it, "sim")
                        await_(dve, V_, u, it, "mb")
                        keys = pX[u][:, 0:2, :].rearrange("p h (a k t) -> p h a k t", k=2, t=S)[:, :, :, 0, :]
                        V_.done(dve.tensor_tensor(keys, keys, mb[u][:, None, :, :].to_broadcast([128, 2, SEQ // 2, S]),
                                                  ALU.add), u, "mask")
                        await_(dve, V_, u, it, "mask")
                        sim = pX[u][:, 0:2, :].rearrange("p h (a k) -> p (h a) k", k=128)
                        V_.done(dve.tensor_reduce(mx[u][:], sim, AX, ALU.max), u, "max")
                        await_(dve, V_, u, it, "max")
                        V_.done(dve.tensor_tensor(pr[u][:], sim, mx[u][:].unsqueeze(2).to_broadcast([128, SEQ, 128]),
                                                  ALU.subtract), u, "sub")
                    for u in range(2):
                        await_(dve, A_, u, it, "exp")
                        V_.done(dve.tensor_reduce(sm[u][:], pr[u][:], AX, ALU.add), u, "sum")
                        await_(dve, V_, u, it, "sum")
                        V_.done(dve.reciprocal(sm[u][:], sm[u][:]), u, "rec")
                        await_(dve, V_, u, it, "rec")
                        V_.done(dve.tensor_tensor(pr[u][:], pr[u][:], sm[u][:].unsqueeze(2).to_broadcast([128, SEQ, 128]),
                                                  ALU.mult), u, "pn")
                    for u in range(2):
                        await_(dve, A_, u, it, "rs")
                        V_.done(dve.scalar_tensor_tensor(g["resid"][:, cols(it * 2 + u)], pX[u][:, 3, :], cb[:],
                                                         rs[u][:, 0, :], ALU.add, ALU.mult), u, "norm")
                over_pairs(dve, body)


def experts(nc, g):
    ctx = ExitStack()
    with ctx:
        st = Stage(nc, ctx, "f",
                   pe="sim down up0 up1 g0 g1 g2 g3 out var",
                   act="s down sg0 ey ea ex sg1 sqo ln rs",
                   dve="xs top ix ixf best rep hm0 sel hm1 row z rz xw tau ne far far2 rest thr "
                       + " ".join(f"m{c} f{c} l{c}" for c in range(TILES)) + " w0 w norm",
                   pool="pairs ey ea rel far0 far1 keep v0 nt v1 v2 v3")
        PE, A_, V_, P_, pX = st.PE, st.ACT, st.DVE, st.POOL, st.pX
        CHD = TILES * PKH
        W = {n: st.sb(n, s) for n, s in dict(wg=[128, DCD], wu=[128, DCD], bg=[128, BLK], bu=[128, BLK], wdT=[128, DCD],
                                             bd=[128, 1], downT=[128, NEXP],
                                             upT=[128, NEXP]).items()}
        km, wd, up, cb = st.sb("km", [128, 512]), st.sb("wd", [128, DCD]), st.sb("up", [128, NEXP]), st.sb("cb", [128, 1])
        xs = st.two("xs", [128, CH])
        S_ = st.two("S", [128, 2, CHD, NK])
        T_ = st.two("T", [128, 2, CHD, TOPK])
        ixu, ixf = st.two("ixu", [128, CHD, TOPK], U32), st.two("ixf", [128, CHD, TOPK])
        pairs, sel = st.two("pairs", [128, CHD, 64]), st.two("sel", [128, CHD, 64])
        best = st.two("best", [128, CHD, TOPK])
        ey, ea = st.two("ey", [128, CHD, NK]), st.two("ea", [128, CHD, ROWS])
        far = st.two("far", [128, CHD, 64])
        ne = far
        row, z, tau, thr = (st.two(n, s) for n, s in (("row", [128, CHD, 8]), ("z", [128, CHD]), ("tau", [128, CHD, 8]),
                                                      ("thr", [128, CHD, ROWS])))
        outr, rest = st.two("outr", [128, CHD, 8]), st.two("rest", [128, TILES])
        val = [st.sb(f"val{c}", [128, PKH, NEXP]) for c in range(TILES)]
        reach = st.sb("reach", [128, PKH, NEXP])
        flat = val[0][:].rearrange("p h e -> p (h e)")
        wqT, keysT = flat[0:64, 0:1024], flat[0:64, 1024:1024 + 8 * NK]
        act_e = st.two("act_e", [128, BLK, CH])
        sg, hm = st.two("sg", [128, 2, CH]), st.two("hm", [128, BLK, CH])
        sq, rs = ([t[:, k, :] for t in sg] for k in range(2))
        ld = g["in"]
        g8 = lambda t: t.rearrange("p g (i j) -> p g i j", i=8)

        with nc.Block() as block:
            @block.sync
            def _(sp):
                load_weights(sp, W, ld, st.s_w)
                sp.dma_start(wqT, ld["wqT"]).then_inc(st.s_w, 16)
                sp.dma_start(keysT, ld["keysT"]).then_inc(st.s_w, 16)
            wready = 16 * (len(W) + 2)

            @block.gpsimd
            def _(pool):
                def first_scores(it, u):
                    await_(pool, V_, u, it, "top")
                    sx, sy = T_[u][:, 0, :, :], T_[u][:, 1, :, :]
                    P_.done(pool.tensor_tensor(g8(pairs[u][:]), sx.unsqueeze(3).to_broadcast([128, CHD, 8, 8]),
                                               sy.unsqueeze(2).to_broadcast([128, CHD, 8, 8]), ALU.add), u, "pairs")
                    P_.done(pool.tensor_tensor(ey[u][:], S_[u][:, 1, :, :], sy[:, :, 0:1].to_broadcast([128, CHD, NK]),
                                               ALU.subtract), u, "ey")
                    P_.done(pool.tensor_tensor(ea[u][:], S_[u][:, 0, :, 0:ROWS],
                                               sx[:, :, 0:1].to_broadcast([128, CHD, ROWS]), ALU.subtract), u, "ea")

                def chosen(it, u):
                    await_(pool, V_, u, it, "sel")
                    P_.done(pool.tensor_tensor(pairs[u][:], pairs[u][:], best[u][:, :, 0:1].to_broadcast([128, CHD, 64]),
                                               ALU.subtract), u, "rel")
                    P_.done(pool.tensor_scalar(far[u][:], sel[u][:], -BIG, BIG, ALU.mult, ALU.add), u, "far0")
                    await_(pool, P_, u, it, "far0")
                    P_.done(pool.tensor_tensor(g8(far[u][:]), g8(far[u][:]),
                                               T_[u][:, 1, :, :].unsqueeze(2).to_broadcast([128, CHD, 8, 8]),
                                               ALU.add), u, "far1")
                    await_(pool, A_, u, it, "ex")
                    P_.done(pool.tensor_tensor(pairs[u][:], pairs[u][:], sel[u][:], ALU.mult), u, "keep")

                def add_tau(it, u):
                    await_(pool, V_, u, it, "ne")
                    P_.done(pool.tensor_tensor(g8(ne[u][:]), g8(ne[u][:]),
                                               tau[u][:].unsqueeze(2).to_broadcast([128, CHD, 8, 8]), ALU.add), u, "nt")

                def weights(it, u, c):
                    if c == 0:
                        await_(pool, V_, u, it, "xw")
                        await_(pool, A_, u, it, "ey")
                    v, jt = other(it, u)
                    await_(pool, PE, v, jt, f"g{c}")
                    t = slice(c * PKH, (c + 1) * PKH)
                    P_.done(pool.tensor_tensor(val[c][:].rearrange("p h (a b) -> p h a b", a=ROWS),
                                               ey[u][:, t, :].unsqueeze(2).to_broadcast([128, PKH, ROWS, NK]),
                                               ea[u][:, t, :].unsqueeze(3).to_broadcast([128, PKH, ROWS, NK]),
                                               ALU.mult), u, f"v{c}")

                def slot(it, u, parts):
                    v, jt = other(it, u)
                    A, Bm = "A" in parts, "B" in parts
                    if Bm:
                        weights(jt, v, 1)
                        weights(jt, v, 2)
                    if A:
                        first_scores(it, u)
                    if Bm:
                        weights(jt, v, 3)
                    if A:
                        chosen(it, u)
                        weights(it, u, 0)
                        add_tau(it, u)
                over_slots(pool, slot)

            @block.tensor
            def _(pe):
                pe.wait_ge(st.s_w, wready)
                for k in range(8):
                    pe.matmul(pX[0][:, 0, k * NK:(k + 1) * NK], wqT[:, k * 128:(k + 1) * 128], keysT[:, k * NK:(k + 1) * NK], start=True, stop=True)
                centred_rows(pe, pX[0][:, 1, :], W["wdT"], BLK, g["cen"][:])
                centred_rows(pe, pX[0][:, 2, :], W["upT"], BLK, g["cen"][:])
                pe.matmul(pX[0][:, 3, 0:1], g["cen"][:], W["bd"][:], start=True, stop=True).then_inc(st.s_prep, 1)
                pe.wait_ge(st.s_copied, 1)

                def up_proj(u, k, step):
                    for j in range(2):
                        b = 2 * k + j
                        pe.matmul(pX[u][:, j, :], W["wg"][:, b * 128:(b + 1) * 128], xs[u][:], start=True, stop=True)
                        mm = pe.matmul(pX[u][:, 2 + j, :], W["wu"][:, b * 128:(b + 1) * 128], xs[u][:], start=True, stop=True)
                    PE.done(mm, u, step)

                def scores(it, u):
                    await_(pe, V_, u, it, "xs")
                    for c in range(TILES):
                        mm = pe.matmul(pX[u][:, c, :], xs[u][:, c * 128:(c + 1) * 128], km[:], start=True, stop=True)
                    PE.done(mm, u, "sim")

                def down(it, u):
                    await_(pe, A_, u, it, "s")
                    for b in range(BLK):
                        mm = pe.matmul(pX[u][:, b, :], W["downT"][:, b * 128:(b + 1) * 128], xs[u][:], start=True, stop=True)
                    PE.done(mm, u, "down")

                def tile(it, u, c):
                    if c == 0:
                        await_(pe, V_, u, it, "hm1")
                    await_(pe, V_, u, it, f"l{c}")
                    for b in range(BLK):
                        for h in range(PKH):
                            mm = pe.matmul(pX[u][:, b, c * 128:(c + 1) * 128], val[c][:, h, b * 128:(b + 1) * 128],
                                           g["eye"][:], start=(h == 0), stop=(h == PKH - 1))
                    PE.done(mm, u, f"g{c}")

                def out(it, u):
                    await_(pe, V_, u, it, "w0")
                    pe.matmul(pX[u][:, 0, :], g["cen"][:], xs[u][:], start=True, stop=False)
                    for b in range(BLK):
                        pe.matmul(pX[u][:, 0, :], wd[:, b * 128:(b + 1) * 128], hm[u][:, b, :], start=False, stop=False)
                    await_(pe, V_, u, it, "w")
                    for b in range(BLK):
                        mm = pe.matmul(pX[u][:, 0, :], up[:, b * 128:(b + 1) * 128], act_e[u][:, b, :], start=False,
                                       stop=(b == BLK - 1))
                    PE.done(mm, u, "out")

                def slot(it, u, parts):
                    v, jt = other(it, u)
                    A, Bm, Cn = "A" in parts, "B" in parts, "C" in parts
                    if Cn:
                        await_(pe, A_, u, it - 1, "sqo")
                        PE.done(pe.matmul(pX[u][:, 1, :], g["avg"][:], sq[u][:], start=True, stop=True), u, "var")
                    if A:
                        scores(it, u)
                    if Bm:
                        tile(jt, v, 0)
                    if A:
                        down(it, u)
                    if Bm:
                        tile(jt, v, 1)
                    if A:
                        await_(pe, A_, u, it, "down")
                        up_proj(u, 0, "up0")
                    if Bm:
                        tile(jt, v, 2)
                    if A:
                        await_(pe, V_, u, it, "hm0")
                        up_proj(u, 1, "up1")
                    if Bm:
                        tile(jt, v, 3)
                        out(jt, v)
                over_slots(pe, slot)

            @block.scalar
            def _(act):
                act.wait_ge(st.s_prep, 1)
                for k, t in enumerate((km, wd, up)):
                    act.activation(t[:], pX[0][:, k, :], ACT.Copy)
                act.activation(cb[:], pX[0][:, 3, 0:1], ACT.Copy).then_inc(st.s_copied, 1)

                def gate(u, k, step):
                    for j in range(2):
                        a = act.activation(sg[u][:, j, :], pX[u][:, j, :], ACT.Silu, bias=W["bg"][:, 2 * k + j:2 * k + j + 1])
                    A_.done(a, u, step)

                def slot(it, u, parts):
                    if "C" in parts:
                        await_(act, PE, u, it - 1, "var")
                        rsqrt_steps(act, st, g, it - 1, u, pX[u][:, 1, :], rs[u][:])
                    if "A" in parts:
                        await_(act, PE, u, it, "sim")
                        A_.done(act.activation(S_[u][:].rearrange("p s (c h) k -> p c s (h k)", c=TILES),
                                               pX[u][:].rearrange("p c (s n) -> p c s n", s=2), ACT.Copy), u, "s")
                        await_(act, PE, u, it, "down")
                        A_.done(act.activation(act_e[u][:], pX[u][:], ACT.Silu), u, "down")
                        await_(act, PE, u, it, "up0")
                        gate(u, 0, "sg0")
                        await_(act, P_, u, it, "ea")
                        A_.done(act.activation(ey[u][:], ey[u][:], ACT.Exp), u, "ey")
                        A_.done(act.activation(ea[u][:], ea[u][:], ACT.Exp), u, "ea")
                        await_(act, P_, u, it, "rel")
                        A_.done(act.activation(pairs[u][:], pairs[u][:], ACT.Exp), u, "ex")
                        await_(act, PE, u, it, "up1")
                        gate(u, 1, "sg1")
                    if "B" in parts:
                        v, jt = other(it, u)
                        await_(act, PE, v, jt, "out")
                        A_.done(act.activation(sq[v][:], pX[v][:, 0, :], ACT.Square, bias=cb[:]), v, "sqo")
                over_slots(act, slot)

            @block.vector
            def _(dve):
                def hidden(it, u, k):
                    await_(dve, A_, u, it, f"sg{k}")
                    for j in range(2):
                        b = 2 * k + j
                        a = dve.scalar_tensor_tensor(hm[u][:, b, :], pX[u][:, 2 + j, :], W["bu"][:, b:b + 1], sg[u][:, j, :],
                                                     ALU.add, ALU.mult)
                    V_.done(a, u, f"hm{k}")

                def best_keys(it, u):
                    await_(dve, A_, u, it, "s")
                    st.carry(dve)
                    for s in range(2):
                        for k in range(CHD):
                            a = dve.max(T_[u][:, s, k, :], S_[u][:, s, k, :])
                    V_.done(a, u, "top")
                    await_(dve, V_, u, it, "top")
                    st.carry(dve)
                    for k in range(CHD):
                        a = dve.max_index(ixu[u][:, k, :], T_[u][:, 0, k, :], S_[u][:, 0, k, :])
                    V_.done(a, u, "ix")
                    await_(dve, V_, u, it, "ix")
                    V_.done(dve.tensor_copy(ixf[u][:], ixu[u][:]), u, "ixf")

                def best_pairs(it, u):
                    await_(dve, P_, u, it, "pairs")
                    st.carry(dve)
                    for k in range(CHD):
                        a = dve.max(best[u][:, k, :], pairs[u][:, k, :])
                    V_.done(a, u, "best")
                    await_(dve, V_, u, it, "best")
                    st.carry(dve)
                    for k in range(CHD):
                        a = dve.match_replace(sel[u][:, k, :], best[u][:, k, :], pairs[u][:, k, :], -3e38)
                    V_.done(a, u, "rep")
                    hidden(it, u, 0)
                    await_(dve, V_, u, it, "rep")
                    V_.done(dve.tensor_tensor(sel[u][:], sel[u][:], pairs[u][:], ALU.is_lt), u, "sel")

                def ranks(it, u):
                    await_(dve, P_, u, it, "keep")
                    V_.done(dve.tensor_reduce(row[u][:], g8(pairs[u][:]), AX, ALU.add), u, "row")
                    await_(dve, V_, u, it, "row")
                    V_.done(dve.tensor_reduce(z[u][:], row[u][:], AX, ALU.add), u, "z")
                    await_(dve, V_, u, it, "z")
                    V_.done(dve.reciprocal(z[u][:], z[u][:]), u, "rz")
                    await_(dve, V_, u, it, "rz")
                    await_(dve, A_, u, it, "ea")
                    zb = z[u][:].unsqueeze(2).to_broadcast([128, CHD, 8])
                    V_.done(dve.tensor_tensor(ea[u][:], ea[u][:], zb, ALU.mult), u, "xw")

                def positions(it, u):
                    await_(dve, P_, u, it, "far1")
                    V_.done(dve.tensor_reduce(tau[u][:], g8(far[u][:]), AX, ALU.min), u, "tau")
                    await_(dve, V_, u, it, "tau")
                    for a_ in range(ROWS):
                        a = dve.tensor_scalar(g8(ne[u][:])[:, :, a_, :], ixf[u][:], float(a_), BIG, ALU.not_equal, ALU.mult)
                    V_.done(a, u, "ne")
                    zb = z[u][:].unsqueeze(2).to_broadcast([128, CHD, 8])
                    V_.done(dve.scalar_tensor_tensor(outr[u][:], ixf[u][:], float(ROWS), row[u][:], ALU.is_ge, ALU.mult),
                            u, "far")
                    await_(dve, V_, u, it, "far")
                    V_.done(dve.tensor_tensor(outr[u][:], outr[u][:], zb, ALU.mult), u, "far2")
                    await_(dve, V_, u, it, "far2")
                    V_.done(dve.tensor_reduce(rest[u][:], outr[u][:].rearrange("p (c h) i -> p c (h i)", c=TILES),
                                              AX, ALU.add), u, "rest")

                def thresholds(it, u):
                    await_(dve, P_, u, it, "nt")
                    V_.done(dve.tensor_reduce(thr[u][:], g8(ne[u][:]), AX, ALU.min), u, "thr")

                def tile(it, u, c):
                    if c == 0:
                        await_(dve, V_, u, it, "thr")
                        v, jt = other(it, u)
                        await_(dve, V_, v, jt, f"l{TILES - 1}")
                    else:
                        await_(dve, V_, u, it, f"l{c - 1}")
                    t = slice(c * PKH, (c + 1) * PKH)
                    V_.done(dve.tensor_tensor(reach[:].rearrange("p h (a b) -> p h a b", a=ROWS),
                                              S_[u][:, 1, t, :].unsqueeze(2).to_broadcast([128, PKH, ROWS, NK]),
                                              thr[u][:, t, :].unsqueeze(3).to_broadcast([128, PKH, ROWS, NK]),
                                              ALU.is_ge), u, f"m{c}")
                    await_(dve, V_, u, it, f"m{c}")
                    await_(dve, P_, u, it, f"v{c}")
                    V_.done(dve.tensor_tensor(val[c][:], reach[:], val[c][:], ALU.mult), u, f"f{c}")
                    await_(dve, V_, u, it, f"f{c}")
                    last = val[c][:, PKH - 1, NEXP - 1:NEXP]
                    V_.done(dve.tensor_tensor(last, last, rest[u][:, c:c + 1], ALU.add), u, f"l{c}")

                def slot(it, u, parts):
                    v, jt = other(it, u)
                    A, Bm, Cn = "A" in parts, "B" in parts, "C" in parts
                    if Bm:
                        tile(jt, v, 0)
                    if Cn:
                        await_(dve, A_, u, it - 1, "rs")
                        V_.done(dve.scalar_tensor_tensor(g["resid"][:, cols(it * 2 - 2 + u)], pX[u][:, 0, :], cb[:],
                                                         rs[u][:], ALU.add, ALU.mult), u, "norm")
                    if A:
                        take_input(dve, st, g, xs, it, u, it == 0 if isinstance(it, int) else False)
                    if Bm:
                        tile(jt, v, 1)
                        tile(jt, v, 2)
                    if A:
                        best_keys(it, u)
                        best_pairs(it, u)
                    if Bm:
                        tile(jt, v, 3)
                    if A:
                        hidden(it, u, 1)
                        ranks(it, u)
                    if Bm:
                        await_(dve, PE, v, jt, f"g{TILES - 1}")
                        for step, t in (("w0", slice(0, 1)), ("w", slice(1, BLK))):
                            V_.done(dve.tensor_tensor(act_e[v][:, t, :], pX[v][:, t, :], act_e[v][:, t, :], ALU.mult), v, step)
                    if A:
                        positions(it, u)
                        thresholds(it, u)
                dve.wait_ge(st.s_w, wready)
                dve.wait_ge(st.s_copied, 1)
                over_slots(dve, slot)


def gated_scan(nc, g):
    ctx = ExitStack()
    with ctx:
        st = Stage(nc, ctx, "r", pe="ms uv lam out var", act="sqi lni rsi uz lam sqo ln rs",
                   dve="xs h one in zero scan gate norm", pool="")
        PE, A_, V_, P_, pX = st.PE, st.ACT, st.DVE, st.POOL, st.pX
        W = {n: st.sb(n, s) for n, s in dict(rnorm=[128, 1], rwin=[128, 4 * 128], rwdt=[128, HALF, INNER], rbdt=[128, HALF],
                                             rwoT=[128, HALF * 128]).items()}
        wo = st.sb("wo", [128, HALF * 128])
        xs, sq, rs, hn = (st.two(n, [128, CH]) for n in ("xs", "sq", "rs", "hn"))
        uz = st.two("uz", [128, 4, CH])
        lam, one, s_ = (st.two(n, [128, HALF, CH]) for n in ("lam", "one", "s"))
        ld = g["in"]

        with nc.Block() as block:
            @block.sync
            def _(sp):
                load_weights(sp, W, ld, st.s_w)

            @block.tensor
            def _(pe):
                pe.wait_ge(st.s_w, 16 * len(W))
                centred_rows(pe, pX[0][:, 0, :], W["rwoT"], HALF, g["cen"][:]).then_inc(st.s_prep, 1)
                pe.wait_ge(st.s_copied, 1)

                def body(it, first):
                    for u in range(2):
                        await_(pe, A_, u, it, "sqi")
                        PE.done(pe.matmul(pX[u][:, 0, :], g["avg"][:], sq[u][:], start=True, stop=True), u, "ms")
                    for u in range(2):
                        await_(pe, V_, u, it, "h")
                        for b in range(4):
                            mm = pe.matmul(pX[u][:, b, :], W["rwin"][:, b * 128:(b + 1) * 128], hn[u][:], start=True, stop=True)
                        PE.done(mm, u, "uv")
                    for u in range(2):
                        await_(pe, A_, u, it, "uz")
                        for h in range(HALF):
                            for k in range(HALF):
                                mm = pe.matmul(pX[u][:, h, :], W["rwdt"][:, k, h * 128:(h + 1) * 128], uz[u][:, k, :],
                                               start=(k == 0), stop=(k == HALF - 1))
                        PE.done(mm, u, "lam")
                    for u in range(2):
                        await_(pe, V_, u, it, "gate")
                        pe.matmul(pX[u][:, 2, :], g["cen2"][:], xs[u][:], start=True, stop=False)
                        for k in range(HALF):
                            mm = pe.matmul(pX[u][:, 2, :], wo[:, k * 128:(k + 1) * 128], s_[u][:, k, :], start=False,
                                           stop=(k == HALF - 1))
                        PE.done(mm, u, "out")
                    for u in range(2):
                        await_(pe, A_, u, it, "sqo")
                        PE.done(pe.matmul(pX[u][:, 3, :], g["avg"][:], sq[u][:], start=True, stop=True), u, "var")
                over_pairs(pe, body)

            @block.scalar
            def _(act):
                act.wait_ge(st.s_prep, 1)
                act.activation(wo[:], pX[0][:, 0, 0:HALF * 128], ACT.Copy).then_inc(st.s_copied, 1)

                def body(it, first):
                    for u in range(2):
                        await_(act, V_, u, it, "xs")
                        A_.done(act.activation(sq[u][:], xs[u][:], ACT.Square), u, "sqi")
                    for u in range(2):
                        await_(act, PE, u, it, "ms")
                        A_.done(act.activation(rs[u][:], pX[u][:, 0, :], ACT.Ln, bias=g["eps"][:]), u, "lni")
                        await_(act, A_, u, it, "lni")
                        A_.done(act.activation(rs[u][:], rs[u][:], ACT.Exp, scale=-0.5), u, "rsi")
                    for u in range(2):
                        await_(act, PE, u, it, "uv")
                        A_.done(act.activation(uz[u][:], pX[u][:], ACT.Silu), u, "uz")
                    for u in range(2):
                        await_(act, PE, u, it, "lam")
                        for h in range(HALF):
                            a = act.activation(lam[u][:, h, :], pX[u][:, h, :], ACT.Sigmoid, bias=W["rbdt"][:, h:h + 1])
                        A_.done(a, u, "lam")
                    for u in range(2):
                        await_(act, PE, u, it, "out")
                        A_.done(act.activation(sq[u][:], pX[u][:, 2, :], ACT.Square), u, "sqo")
                    for u in range(2):
                        await_(act, PE, u, it, "var")
                        rsqrt_steps(act, st, g, it, u, pX[u][:, 3, :], rs[u][:])
                over_pairs(act, body)

            @block.vector
            def _(dve):
                dve.wait_ge(st.s_w, 16 * len(W))
                flat = lambda t: t.rearrange("p h t -> p (h t)")

                def body(it, first):
                    for u in range(2):
                        take_input(dve, st, g, xs, it, u, first)
                    for u in range(2):
                        await_(dve, A_, u, it, "rsi")
                        V_.done(dve.scalar_tensor_tensor(hn[u][:], xs[u][:], W["rnorm"][:], rs[u][:], ALU.mult, ALU.mult),
                                u, "h")
                    for u in range(2):
                        await_(dve, A_, u, it, "lam")
                        V_.done(dve.tensor_scalar(one[u][:], lam[u][:], -1.0, 1.0, ALU.mult, ALU.add), u, "one")
                        await_(dve, V_, u, it, "one")
                        V_.done(dve.tensor_tensor(one[u][:], one[u][:], uz[u][:, 0:HALF, :], ALU.mult), u, "in")
                        V_.done(dve.memset(flat(lam[u][:]).rearrange("p (s t) -> p s t", t=S)[:, :, 0:1], 0.0), u, "zero")
                        await_(dve, V_, u, it, "zero")
                        V_.done(dve.tensor_tensor_scan(flat(s_[u][:]), flat(lam[u][:]), flat(one[u][:]), 0.0, ALU.mult,
                                                       ALU.add), u, "scan")
                        await_(dve, V_, u, it, "scan")
                        V_.done(dve.tensor_tensor(s_[u][:], s_[u][:], uz[u][:, HALF:4, :], ALU.mult), u, "gate")
                    for u in range(2):
                        await_(dve, A_, u, it, "rs")
                        V_.done(dve.tensor_tensor(g["resid"][:, cols(it * 2 + u)], pX[u][:, 2, :], rs[u][:], ALU.mult),
                                u, "norm")
                over_pairs(dve, body)


def context_experts(nc, g):
    ctx = ExitStack()
    with ctx:
        st = Stage(nc, ctx, "e", pe="x1 out cen var", act="gelu sqo ln rs", dve="xs h add norm", pool="")
        PE, A_, V_, P_, pX = st.PE, st.ACT, st.DVE, st.POOL, st.pX
        xs, xr, sq, rs, cT = (st.two(n, [128, CH]) for n in ("xs", "xr", "sq", "rs", "cT"))
        cr = st.two("cr", [128, SEQ // 2, 128])
        hT = st.two("hT", [128, SEQ // 2, S])
        s_c = [st.sem(f"ctx{u}") for u in range(2)]
        ld = g["in"]

        with nc.Block() as block:
            @block.sync
            def _(sp):
                def load(c, u):
                    sp.dma_start(cT[u][:], ld["ctxT"][:, cols(c)]).then_inc(s_c[u], 16)
                    sp.dma_start(cr[u][:], ld["ctxrow"][:, bass.ds(c * (SEQ // 2), SEQ // 2), :]).then_inc(s_c[u], 16)
                for u in range(2):
                    load(u, u)
                with sp.Fori(0, NCH // 2 - 1) as it:
                    for u in range(2):
                        await_(sp, PE, u, it, "out")
                        load(it * 2 + 2 + u, u)

            @block.tensor
            def _(pe):
                def body(it, first):
                    for u in range(2):
                        pe.wait_ge(s_c[u], (it + 1) * 32)
                        await_(pe, V_, u, it, "xs")
                        for b in range(SEQ):
                            r, pair = b % 2, b // 2
                            mm = pe.matmul(pX[u][r * S:(r + 1) * S, 0, pair * S:(pair + 1) * S], cT[u][:, b * S:(b + 1) * S],
                                           xs[u][:, b * S:(b + 1) * S], start=True, stop=True)
                        PE.done(mm, u, "x1")
                    for u in range(2):
                        await_(pe, V_, u, it, "h")
                        for b in range(SEQ):
                            r, pair = b % 2, b // 2
                            mm = pe.matmul(pX[u][:, 1 + r, pair * S:(pair + 1) * S], cr[u][r * S:(r + 1) * S, pair, :],
                                           hT[u][r * S:(r + 1) * S, pair, :], start=True, stop=True)
                        PE.done(mm, u, "out")
                    for u in range(2):
                        await_(pe, V_, u, it, "add")
                        PE.done(pe.matmul(pX[u][:, 3, :], g["cen"][:], xr[u][:], start=True, stop=True), u, "cen")
                    for u in range(2):
                        await_(pe, A_, u, it, "sqo")
                        PE.done(pe.matmul(pX[u][:, 0, :], g["avg"][:], sq[u][:], start=True, stop=True), u, "var")
                over_pairs(pe, body)

            @block.scalar
            def _(act):
                def body(it, first):
                    for u in range(2):
                        await_(act, PE, u, it, "x1")
                        A_.done(act.activation(hT[u][:].rearrange("p a t -> p (a t)"), pX[u][:, 0, 0:CH // 2],
                                               ACT.Gelu_apprx_tanh), u, "gelu")
                    for u in range(2):
                        await_(act, PE, u, it, "cen")
                        A_.done(act.activation(sq[u][:], pX[u][:, 3, :], ACT.Square), u, "sqo")
                    for u in range(2):
                        await_(act, PE, u, it, "var")
                        rsqrt_steps(act, st, g, it, u, pX[u][:, 0, :], rs[u][:])
                over_pairs(act, body)

            @block.vector
            def _(dve):
                def body(it, first):
                    for u in range(2):
                        take_input(dve, st, g, xs, it, u, first)
                    for u in range(2):
                        await_(dve, A_, u, it, "gelu")
                        h = hT[u][:].rearrange("p a t -> p (a t)")
                        V_.done(dve.tensor_tensor(h, h, pX[u][:, 0, 0:CH // 2], ALU.mult), u, "h")
                    for u in range(2):
                        await_(dve, PE, u, it, "out")
                        V_.done(dve.tensor_tensor(
                            xr[u][:].rearrange("p (a r t) -> p r a t", r=2, t=S),
                            xs[u][:].rearrange("p (a r t) -> p r a t", r=2, t=S),
                            pX[u][:, 1:3, 0:CH // 2].rearrange("p r (a t) -> p r a t", t=S), ALU.add), u, "add")
                    for u in range(2):
                        await_(dve, A_, u, it, "rs")
                        V_.done(dve.tensor_tensor(g["resid"][:, cols(it * 2 + u)], pX[u][:, 3, :], rs[u][:], ALU.mult),
                                u, "norm")
                over_pairs(dve, body)


def moe(nc, g):
    ALLX = EXPERTS + 1
    ctx = ExitStack()
    with ctx:
        st = Stage(nc, ctx, "g",
                   pe="lg cwT a0 b0 " + " ".join(f"a{e} b{e} ac{e - 1}" for e in range(1, ALLX)) + f" ac{EXPERTS}",
                   act="le hi cwf " + " ".join(f"sa{e}" for e in range(ALLX)),
                   dve="xs lmax lsub ls lr p top ix ixf eq0 eq1 eqs cw r1 mid lo hid0 "
                       + " ".join(f"g{e} hid{e}" for e in range(1, ALLX)),
                   pool="")
        PE, A_, V_, P_, pX = st.PE, st.ACT, st.DVE, st.POOL, st.pX
        TAIL, VAR, NORM = (Progress([st.sem(f"{n}{u}") for u in range(2)], steps.split())
                           for n, steps in (("tail", "sqo xo ln rs"), ("var", "var"), ("norm", "norm")))
        AB = [pX[0][:, 0:2, :], pX[0][:, 2:4, :]]
        SP = [pX[1][:, 0, :], pX[1][:, 1, :]]
        ACC, MISC = pX[1][:, 2, :], pX[1][:, 3, :]
        AT_CW = 5
        side = lambda u, e: (u + e) % 2
        W = {n: st.sb(n, s) for n, s in dict(gw=[128, EXPERTS], gb=[1, EXPERTS], one1=[1, 128], iota8=[128, EXPERTS],
                                             w1=[128, ALLX, 2 * FFN], b1=[128, ALLX, 2], w2T=[128, ALLX * FFN],
                                             rb2T=[128, EXPERTS], sb2=[128, 1]).items()}
        w2, rb2, cb = st.sb("w2", [128, ALLX * 128]), st.sb("rb2", [EXPERTS, 128]), st.sb("cb", [128, 1])
        xs, sq, rs, xo, sa, hid, res = (st.two(n, [128, CH]) for n in ("xs", "sq", "rs", "xo", "sa", "hid", "res"))
        lg, eq = st.two("lg", [128, TILES, 8]), st.two("eq", [128, 2, TILES, 8])
        lm, top, ixu, ixf = (st.two("lm", [128, TILES]), st.two("top", [128, TILES, 8]),
                             st.two("ixu", [128, TILES, 8], U32), st.two("ixf", [128, TILES, 8]))
        cw3 = st.two("cw3", [128, TILES, 3, 32])
        parts, r1, cwf = st.two("parts", [96, CH], BF16), st.two("r1", [64, CH]), st.two("cwf", [EXPERTS, CH])
        s_out = [st.sem(f"out{u}") for u in range(2)]
        s_zero = st.sem("zero")
        ld = g["in"]

        with nc.Block() as block:
            @block.sync
            def _(sp):
                load_weights(sp, W, ld, st.s_w)
                with sp.Fori(0, NCH // 2) as it:
                    for u in range(2):
                        await_(sp, NORM, u, it, "norm")
                        sp.dma_start(g["out"][:, cols(it * 2 + u)], res[u][:]).then_inc(s_out[u], 16)
                for u in range(2):
                    sp.wait_ge(s_out[u], 16 * (NCH // 2))

            @block.tensor
            def _(pe):
                pe.wait_ge(st.s_w, 16 * len(W))
                for b in range(3):
                    n = min(4, ALLX - 4 * b)
                    centred_rows(pe, pX[0][:, b, :], W["w2T"][:, 512 * b:], n, g["cen"][:])
                pe.matmul(pX[0][0:EXPERTS, 3, 0:128], W["rb2T"][:], g["cen"][:], start=True, stop=True)
                pe.matmul(pX[0][:, 3, 128:129], g["cen"][:], W["sb2"][:], start=True, stop=True).then_inc(st.s_prep, 1)
                pe.wait_ge(st.s_copied, 1)

                def up(it, u, e):
                    v, jt = other(it, u)
                    k = side(u, e)
                    if e == 0:
                        await_(pe, V_, v, jt, f"hid{EXPERTS - 1}")
                    elif e == 1:
                        await_(pe, V_, v, jt, f"hid{EXPERTS}")
                        await_(pe, V_, u, it, "lo")
                    else:
                        await_(pe, V_, u, it, f"hid{e - 2}")
                        if e == 2:
                            await_(pe, TAIL, v, jt, "ln")
                    for j, n in enumerate("ab"):
                        mm = pe.matmul(AB[k][:, j, :], W["w1"][:, e, j * FFN:(j + 1) * FFN], xs[u][:], start=True, stop=True)
                        if e and n == "b":
                            mm = pe.matmul(SP[k], g["sel"][:, e - 1, :], parts[u][:], start=True, stop=True)
                        PE.done(mm, u, f"{n}{e}")

                def add(it, u, e):
                    if e == 0:
                        v, jt = other(it, u)
                        await_(pe, TAIL, v, jt, "xo")
                        pe.matmul(ACC, g["cen"][:], xs[u][:], start=True, stop=False)
                    await_(pe, V_, u, it, f"hid{e}")
                    mm = pe.matmul(ACC, w2[:, e * 128:(e + 1) * 128], hid[side(u, e)][:], start=False, stop=False)
                    if e == EXPERTS:
                        mm = pe.matmul(ACC, rb2[:], cwf[u][:], start=False, stop=True)
                    PE.done(mm, u, f"ac{e}")

                def slot(it, u, what):
                    v, jt = other(it, u)
                    for e in range(1, ALLX):
                        if "B" in what:
                            up(jt, v, e)
                        if "C" in what and e == 1:
                            await_(pe, TAIL, u, it - 1, "sqo")
                            await_(pe, V_, u, it - 1, f"hid{EXPERTS}")
                            VAR.done(pe.matmul(SP[side(v, 0)], g["avg"][:], sq[u][:], start=True, stop=True), u, "var")
                        if "A" in what and e == 1:
                            await_(pe, V_, v, jt, "lo")
                            await_(pe, V_, u, it, "xs")
                            for c in range(TILES):
                                o = MISC[:, c * 8:(c + 1) * 8]
                                pe.matmul(o, xs[u][:, c * 128:(c + 1) * 128], W["gw"][:], start=True, stop=False)
                                mm = pe.matmul(o, W["one1"][:], W["gb"][:], start=False, stop=True)
                            PE.done(mm, u, "lg")
                        if "A" in what and e == AT_CW:
                            await_(pe, V_, u, it, "cw")
                            for c in range(TILES):
                                mm = pe.matmul(MISC[0:96, c * 128:(c + 1) * 128],
                                               cw3[u][:, c, :, :].rearrange("p r e -> p (r e)"), g["eye"][:], start=True, stop=True)
                            PE.done(mm, u, "cwT")
                        if "B" in what:
                            add(jt, v, e - 1)
                    if "A" in what:
                        up(it, u, 0)
                    if "B" in what:
                        add(jt, v, EXPERTS)
                over_slots(pe, slot)

            @block.scalar
            def _(act):
                act.wait_ge(st.s_prep, 1)
                act.activation(w2[:], pX[0][:, 0:3, :].rearrange("p b n -> p (b n)")[:, 0:ALLX * 128], ACT.Copy)
                act.activation(rb2[:], pX[0][0:EXPERTS, 3, 0:128], ACT.Copy)
                act.activation(cb[:], pX[0][:, 3, 128:129], ACT.Copy).then_inc(st.s_copied, 1)

                act.wait_ge(st.s_copied, 1)

                def expert(it, u, e):
                    await_(act, PE, u, it, f"a{e}")
                    k = side(u, e)
                    A_.done(act.activation(sa[k][:], AB[k][:, 0, :], ACT.Silu, bias=W["b1"][:, e, 0:1]), u, f"sa{e}")

                def slot(it, u, what):
                    v, jt = other(it, u)
                    for e in range(ALLX):
                        if "B" in what:
                            expert(jt, v, e)
                        if "C" in what and e == 0:
                            await_(act, PE, u, it - 1, f"ac{EXPERTS}")
                            TAIL.done(act.activation(sq[u][:], ACC, ACT.Square, bias=cb[:]), u, "sqo")
                            TAIL.done(act.activation(xo[u][:], ACC, ACT.Identity, bias=cb[:]), u, "xo")
                        if "C" in what and e == 1:
                            await_(act, VAR, u, it - 1, "var")
                            TAIL.done(act.activation(rs[u][:], SP[side(v, 0)], ACT.Ln, bias=g["eps"][:]), u, "ln")
                            await_(act, TAIL, u, it - 1, "ln")
                            TAIL.done(act.activation(rs[u][:], rs[u][:], ACT.Exp, scale=-0.5), u, "rs")
                        if "A" in what and e == 1:
                            await_(act, V_, u, it, "lsub")
                            A_.done(act.activation(lg[u][:], lg[u][:], ACT.Exp), u, "le")
                        if "A" in what and e == AT_CW:
                            await_(act, PE, u, it, "cwT")
                            A_.done(act.activation(parts[u][:], MISC[0:96, :], ACT.Copy), u, "hi")
                            A_.done(act.activation(cwf[u][:], MISC[0:EXPERTS, :], ACT.Copy), u, "cwf")
                over_slots(act, slot)

            @block.vector
            def _(dve):
                for u in range(2):
                    dve.memset(cw3[u][:], 0.0).then_inc(s_zero, 1)
                dve.wait_ge(s_zero, 2)
                dve.wait_ge(st.s_w, 16 * len(W))
                wide = lambda t: t.unsqueeze(2).to_broadcast([128, TILES, 8])

                def hidden(it, u, e):
                    k = side(u, e)
                    v, jt = other(it, u)
                    await_(dve, PE, u, it, f"b{e}")
                    await_(dve, A_, u, it, f"sa{e}")
                    if e < 2:
                        await_(dve, PE, v, jt, f"ac{EXPERTS - 1 + e}")
                    else:
                        await_(dve, PE, u, it, f"ac{e - 2}")
                    a = dve.scalar_tensor_tensor(hid[k][:], AB[k][:, 1, :], W["b1"][:, e, 1:2], sa[k][:], ALU.add,
                                                 ALU.mult)
                    if e:
                        V_.done(a, u, f"g{e}")
                        await_(dve, V_, u, it, f"g{e}")
                        a = dve.tensor_tensor(hid[k][:], hid[k][:], SP[k], ALU.mult)
                    V_.done(a, u, f"hid{e}")

                def routing(it, u, e):
                    if e == 0:
                        await_(dve, PE, u, it, "lg")
                        logits = MISC[:, 0:TILES * 8].rearrange("p (c e) -> p c e", e=8)
                        V_.done(dve.tensor_reduce(lm[u][:], logits, AX, ALU.max), u, "lmax")
                        await_(dve, V_, u, it, "lmax")
                        V_.done(dve.tensor_tensor(lg[u][:], logits, wide(lm[u][:]), ALU.subtract), u, "lsub")
                    if e == 2:
                        await_(dve, A_, u, it, "le")
                        V_.done(dve.tensor_reduce(lm[u][:], lg[u][:], AX, ALU.add), u, "ls")
                        await_(dve, V_, u, it, "ls")
                        V_.done(dve.reciprocal(lm[u][:], lm[u][:]), u, "lr")
                        await_(dve, V_, u, it, "lr")
                        V_.done(dve.tensor_tensor(lg[u][:], lg[u][:], wide(lm[u][:]), ALU.mult), u, "p")
                        await_(dve, V_, u, it, "p")
                        st.carry(dve)
                        for c in range(TILES):
                            a = dve.max(top[u][:, c, :], lg[u][:, c, :])
                        V_.done(a, u, "top")
                        await_(dve, V_, u, it, "top")
                        st.carry(dve)
                        for c in range(TILES):
                            a = dve.max_index(ixu[u][:, c, :], top[u][:, c, :], lg[u][:, c, :])
                        V_.done(a, u, "ix")
                    if e == 3:
                        await_(dve, V_, u, it, "ix")
                        V_.done(dve.tensor_copy(ixf[u][:], ixu[u][:]), u, "ixf")
                        await_(dve, V_, u, it, "ixf")
                        for k in range(2):
                            V_.done(dve.tensor_tensor(eq[u][:, k, :, :], W["iota8"][:, None, :].to_broadcast([128, TILES, 8]),
                                                      ixf[u][:, :, k:k + 1].to_broadcast([128, TILES, 8]), ALU.is_equal),
                                    u, f"eq{k}")
                        await_(dve, V_, u, it, "eq1")
                        V_.done(dve.tensor_tensor(eq[u][:, 0, :, :], eq[u][:, 0, :, :], eq[u][:, 1, :, :], ALU.add), u, "eqs")
                        await_(dve, V_, u, it, "eqs")
                        V_.done(dve.tensor_tensor(cw3[u][:, :, :, 0:8],
                                                  lg[u][:].unsqueeze(2).to_broadcast([128, TILES, 3, 8]),
                                                  eq[u][:, 0, :, :].unsqueeze(2).to_broadcast([128, TILES, 3, 8]),
                                                  ALU.mult), u, "cw")
                    if e == AT_CW:
                        await_(dve, A_, u, it, "cwf")
                        V_.done(dve.tensor_tensor(r1[u][:], MISC[0:64, :], parts[u][0:64, :], ALU.subtract), u, "r1")
                        await_(dve, V_, u, it, "r1")
                        V_.done(dve.tensor_copy(parts[u][0:64, :], r1[u][:]), u, "mid")
                        await_(dve, V_, u, it, "mid")
                        V_.done(dve.tensor_tensor(parts[u][0:32, :], r1[u][0:32, :], parts[u][0:32, :], ALU.subtract), u, "lo")

                def slot(it, u, what):
                    v, jt = other(it, u)
                    if "A" in what:
                        await_(dve, PE, u, it - 1, f"ac{EXPERTS}")
                        V_.done(dve.tensor_scalar(xs[u][:], g["resid"][:, cols(it * 2 + u)], 1.0, 0.0, ALU.mult, ALU.add), u, "xs")
                    for e in range(ALLX):
                        if "B" in what:
                            hidden(jt, v, e)
                        if "A" in what:
                            routing(it, u, e)
                        if "C" in what and e == 3:
                            await_(dve, TAIL, u, it - 1, "rs")
                            if not isinstance(it, int) or it > 1:
                                dve.wait_ge(s_out[u], (it - 1) * 16)
                            NORM.done(dve.tensor_tensor(res[u][:], xo[u][:], rs[u][:], ALU.mult), u, "norm")
                over_slots(dve, slot)


STAGES = [mamba, cross, experts, gated_scan, context_experts, moe]



def build(nc, ld, out, stages=None):
    g = {"in": ld, "out": out}
    ctx = ExitStack()
    with ctx:
        sb = lambda n, s, d=F32: ctx.enter_context(nc.sbuf_tensor(n, s, d))
        g["resid"] = sb("resid", [128, TOK])
        g["cen"] = sb("cen", [128, 128])
        g["cen2"] = sb("cen2", [128, 128])
        g["avg"] = sb("avg", [128, 128])
        g["avgh"] = sb("avgh", [128, 128])
        g["eye"] = sb("eye", [128, 128])
        self_ = sb("sel_f", [96, 128])
        g["sel"] = sb("sel", [96, 2 * NSTATE, 128], BF16)
        g["eps"] = sb("eps", [128, 1])
        g["s_const"] = ctx.enter_context(nc.semaphore("s_const"))
        with nc.Block() as block:
            @block.sync
            def _(sp):
                for n, t in (("cen", g["cen"]), ("avg", g["avg"]), ("avgh", g["avgh"]), ("eye", g["eye"])):
                    sp.dma_start(t[:], ld[n]).then_inc(g["s_const"], 16)
                sp.dma_start(self_[:, 0:32], ld["mod32"]).then_inc(g["s_const"], 16)

            @block.vector
            def _(dve):
                dve.memset(g["eps"][:], EPS).then_inc(g["s_const"], 1)
                dve.wait_ge(g["s_const"], 81)
                dve.tensor_scalar(g["cen2"][:], g["cen"][:], 2.0, None, ALU.mult).then_inc(g["s_const"], 1)
                dve.tensor_copy(g["sel"][:], self_[:, 0:32].unsqueeze(2).to_broadcast([96, 32, 128]))\
                   .then_inc(g["s_const"], 1)
        g["const_ready"] = 83
        for stage in (stages or STAGES):
            stage(nc, g)
        if stages and stages[-1] is not moe:
            s = ctx.enter_context(nc.semaphore("dbg"))
            with nc.Block() as block:
                @block.sync
                def _(sp):
                    sp.dma_start(out, g["resid"][:]).then_inc(s, 16)
                    sp.wait_ge(s, 16)


def layout(x):
    f = lambda a: np.ascontiguousarray(a)
    eye = np.eye(128, dtype=np.float32)
    column = lambda v: v.reshape(-1, 1)
    halves = lambda v: f(v.reshape(HALF, 128).T)
    xp = x["L0_attn_x_proj_w"].T.reshape(HALF, 128, 96).transpose(1, 0, 2)
    a = {
        "xT": x["x"].reshape(TOK, D).T,
        "cen": eye - np.float32(1 / D), "avg": np.full((128, 128), 1 / D, np.float32), "eye": eye,
        "avgh": np.kron(np.eye(2, dtype=np.float32), np.full((64, 64), 1 / 64, np.float32)),
        "mod32": np.tile(np.eye(32, dtype=np.float32), (3, 1)),
        "win": x["L0_attn_in_proj_w"].T,
        "convw": np.broadcast_to(x["L0_attn_conv_w"].T[None], (128, KCONV, INNER)),
        "convb": halves(x["L0_attn_conv_b"]),
        "xproj": np.concatenate([xp[:, :, 0:64]] + [xp[:, :, 64:96]] * 3, axis=2),
        "dtproj": x["L0_attn_dt_proj_w"].T,
        "dtb": halves(x["L0_attn_dt_proj_b"]),
        "alog": x["L0_attn_A_log"].reshape(HALF, 128, NSTATE).transpose(1, 0, 2),
        "dpar": halves(x["L0_attn_D_param"]),
        "woT": x["L0_attn_out_proj_w"],
        "ctxT": x["ctx_1024"].reshape(TOK, D).T,
        "mask": x["mask_BxS2_bk0"].reshape(B // 2, 2, S).transpose(1, 0, 2).reshape(2, B // 2 * S),
        "xwq": x["L0_xattn_W_q"], "xwkv": x["L0_xattn_W_kv"], "xwoT": x["L0_xattn_W_out"].T,
        "xbo": column(x["L0_xattn_b_out"]),
        "gx": column(x["L0_xattn_ln_x_g"]), "bx": column(x["L0_xattn_ln_x_b"]),
        "gl": column(x["L0_xattn_ln_l_g"]), "bl": column(x["L0_xattn_ln_l_b"]),
        "gq": column(np.tile(x["L0_xattn_q_gamma"], 2)), "gk": column(np.tile(x["L0_xattn_k_gamma"], 2)),
        "wg": x["L0_ffn_Wg"], "wu": x["L0_ffn_Wu"], "bg": x["L0_ffn_bg"].reshape(BLK, 128).T,
        "bu": x["L0_ffn_bu"].reshape(BLK, 128).T, "wdT": x["L0_ffn_Wd"].T, "bd": column(x["L0_ffn_bd"]),
        "wqT": x["L0_ffn_Wq"].T.reshape(8, 64, 128).transpose(1, 0, 2).reshape(64, 8 * 128),
        "keysT": x["L0_ffn_keys"].transpose(3, 2, 0, 1).reshape(64, 8 * NK),
        "downT": x["L0_ffn_down_embed"].T, "upT": x["L0_ffn_up_embed"].T,
        "rnorm": column(x["L1_attn_w_norm"]), "rwin": x["L1_attn_W_in"].T,
        "rwdt": x["L1_attn_W_dt"].T.reshape(HALF, 128, INNER).transpose(1, 0, 2),
        "rbdt": halves(x["L1_attn_b_dt"]), "rwoT": x["L1_attn_W_out"],
        "ctxrow": x["ctx_1024"].reshape(B // 2, 2 * S, D).transpose(1, 0, 2),
        "gw": x["L1_ffn_gate_w"], "gb": x["L1_ffn_gate_b"].reshape(1, EXPERTS), "one1": np.ones((1, 128), np.float32),
        "iota8": np.tile(np.arange(EXPERTS, dtype=np.float32), (128, 1)),
        "w1": np.concatenate([x["L1_ffn_sw1"], x["L1_ffn_rw1"]]).transpose(1, 0, 2),
        "b1": np.concatenate([x["L1_ffn_sb1"], x["L1_ffn_rb1"]]).reshape(EXPERTS + 1, 2, FFN).transpose(2, 0, 1),
        "w2T": np.concatenate([x["L1_ffn_sw2"], x["L1_ffn_rw2"]]).transpose(2, 0, 1).reshape(D, (EXPERTS + 1) * FFN),
        "rb2T": x["L1_ffn_rb2"].T, "sb2": x["L1_ffn_sb2"].T,
    }
    return {k: f(v) for k, v in a.items()}


def kernel(**inputs):
    from concourse import bacc
    from concourse.bass_utils import run_bass_kernel_spmd

    nc = bacc.Bacc("TRN2", target_bir_lowering=False, num_devices=1)
    arrays = layout({k: np.asarray(v) for k, v in inputs.items()})
    ld = {k: nc.dram_tensor("in_" + k, a.shape, mybir.dt.from_np(a.dtype), kind="ExternalInput").ap()
          for k, a in arrays.items()}
    out = nc.dram_tensor("out", (D, TOK), F32, kind="ExternalOutput").ap()
    build(nc, ld, out)
    r = run_bass_kernel_spmd(nc, [{"in_" + k: a for k, a in arrays.items()}], core_ids=[0])
    return np.ascontiguousarray(r.results[0]["out"].T).reshape(B, S, D)
```

```python
from contextlib import ExitStack

import numpy as np
import concourse.bass as bass
from concourse import mybir

F32 = mybir.dt.float32
BF16 = mybir.dt.bfloat16
U8 = mybir.dt.uint8
U32 = mybir.dt.uint32
ALU = mybir.AluOpType
ACT = mybir.ActivationFunctionType
AX = mybir.AxisListType.X

D = 128
B, S = 128, 64
TOK = B * S
CH = 512
NCH = TOK // CH
SEQ = CH // S
TILES = CH // 128
EPS = 1e-5
BIG = 1e30

INNER = 256
HALF = INNER // 128
NSTATE, KCONV, RANK = 16, 4, 64
PAIRS = NSTATE // 2
AT_U, AT_Z, AT_HI, AT_SP = 3, 3, 4, 6

HEADS, HD = 2, 64

DCD = 512
BLK = DCD // 128
PKH, NK, TOPK = 4, 64, 8
NEXP = 512
ROWS = NEXP // NK

EXPERTS, FFN = 8, 128


def wait(eng, sem, value):
    if isinstance(value, int) and value <= 0:
        return
    eng.wait_ge(sem, value)


class Progress:

    def __init__(self, sems, steps):
        self.sems, self.steps, self.at = sems, steps, {}

    def value(self, it, step):
        return it * len(self.steps) + self.steps.index(step) + 1

    def done(self, ins, u, step):
        k = self.at.get(u, 0)
        assert self.steps[k % len(self.steps)] == step, (self.steps[k % len(self.steps)], step)
        self.at[u] = k + 1
        ins.then_inc(self.sems[u], 1)


def await_(eng, prog, u, it, step):
    if isinstance(it, int) and it < 0:
        return
    eng.wait_ge(prog.sems[u], prog.value(it, step))


def cols(i):
    return bass.ds(i * CH, CH)


def mamba(nc, g):
    ctx = ExitStack()
    with ctx:
        sb = lambda n, s, d=F32: ctx.enter_context(nc.sbuf_tensor(n, s, d))
        ps = lambda n, s: ctx.enter_context(nc.psum_tensor(n, s, F32))
        sem = lambda n: ctx.enter_context(nc.semaphore(n))
        W = {n: sb("m_" + n, s) for n, s in dict(
            win=[128, 4 * 128], convw=[128, KCONV, INNER], convb=[128, HALF], xproj=[128, HALF, 128], dtb=[128, HALF], alog=[128, HALF, NSTATE], dpar=[128, HALF],
            woT=[128, HALF * 128]).items()}
        dtproj = sb("m_dtproj", [128, INNER])
        wconv = sb("wconv", [128, KCONV, INNER])
        nega = sb("nega", [128, HALF, NSTATE])
        wout = sb("wout_c", [128, HALF, 128])
        xin = [sb(f"xin{q}", [128, CH]) for q in range(2)]
        xre = sb("xre", [128, CH])
        u = [sb(f"u{q}", [128, HALF, CH]) for q in range(2)]
        z = [sb(f"z{q}", [128, HALF, CH]) for q in range(2)]
        dt = [sb(f"dt{q}", [128, HALF, CH]) for q in range(2)]
        dtu = [sb(f"dtu{q}", [128, HALF, CH]) for q in range(2)]
        parts = [sb(f"parts{q}", [96, CH], BF16) for q in range(2)]
        dtin = sb("dtin", [128, CH])
        r1 = sb("r1", [64, CH])
        ab = sb("ab", [128, HALF, CH])
        rl = sb("rl", [128, HALF, CH])
        ex = sb("ex", [128, HALF, CH])
        ln = sb("ln", [128, HALF, CH])
        wm1 = sb("wm1", [128, HALF, CH])
        bs = [sb(f"bs{k}", [128, 2, CH]) for k in range(2)]
        dA = [sb(f"dA{k}", [128, 2, CH]) for k in range(4)]
        dbu = [sb(f"dbu{k}", [128, 2, CH]) for k in range(4)]
        hs = [sb(f"hs{k}", [128, 2, CH]) for k in range(2)]
        hc = [sb(f"hc{k}", [128, 2, CH]) for k in range(2)]
        yd = sb("yd", [128, HALF, CH])
        sq = sb("m_sq", [128, CH])
        rs = sb("m_rs", [128, CH])
        pB = ps("pB", [128, 2, CH])
        pC = ps("pC", [128, 2, CH])
        pY = ps("pY", [128, HALF, CH])
        mA = ps("mA", [128, CH])
        mB = ps("mB", [128, CH])

        s_w, s_wprep, s_wp, s_neg = sem("m_w"), sem("m_wprep"), sem("m_wp"), sem("m_neg")
        s_xin = [sem(f"s_xin{q}") for q in range(2)]
        s_B, s_C, s_ysum, s_xre = sem("s_B"), sem("s_C"), sem("s_ysum"), sem("s_xre")
        s_conv, s_res, s_xdbl, s_dtp, s_xc, s_var = (sem("s_" + n) for n in "conv res xdbl dtp xc var".split())
        s_bs, s_dA, s_u, s_z, s_hi, s_ab, s_ex, s_ln, s_sq, s_lnv, s_rs = (sem("s_" + n) for n in "bs dA u z hi ab ex ln sq lnv rs".split())
        s_dbu, s_t = sem("s_dbu"), sem("s_t")
        s_scan, s_hc, s_r1, s_mid, s_lo, s_wm1, s_c, s_dt, s_dtu, s_yd, s_yz, s_x1 = (
            sem("s_" + n) for n in "scan hc r1 mid lo wm1 c dt dtu yd yz x1".split())

        ld = g["in"]
        wready = 16 * (len(W) + 1)
        seqs = lambda ap: ap.rearrange("p (s t) -> p s t", t=S)

        def over_chunks(eng, body):
            for i in range(2):
                body(i, i % 2, i == 0, False)
            with eng.Fori(1, NCH // 2 - 1) as ib:
                for q in range(2):
                    body(ib * 2 + q, q, False, False)
            for i in range(NCH - 2, NCH):
                body(i, i % 2, False, i == NCH - 1)

        with nc.Block() as block:
            @block.sync
            def _(sp):
                for n in W:
                    sp.dma_start(W[n][:], ld[n]).then_inc(s_w, 16)
                sp.dma_start(dtproj[RANK:128, :], ld["dtproj"]).then_inc(s_w, 16)
                sp.dma_start(xin[0][:], ld["xT"][:, 0:CH]).then_inc(s_xin[0], 16)
                for later in ("cross", "experts"):
                    g["w"][later].load(sp, ld)

                def body(i, q, first, last):
                    if not last:
                        wait(sp, s_res, i)
                        sp.dma_start(xin[1 - q][:], ld["xT"][:, cols(i + 1)]).then_inc(s_xin[1 - q], 16)
                    wait(sp, s_xc, i)
                    sp.dma_start(xre[:], ld["xT"][:, cols(i)]).then_inc(s_xre, 16)

                over_chunks(sp, body)

            @block.tensor
            def _(pe):
                pe.wait_ge(s_w, wready)
                pe.wait_ge(g["s_const"], g["const_ready"])
                for h in range(HALF):
                    mm = pe.matmul(mA[:, h * 128:(h + 1) * 128], W["woT"][:, h * 128:(h + 1) * 128], g["cen"][:],
                                   start=True, stop=True)
                mm.then_inc(s_wprep, 1)
                pe.wait_ge(s_wp, 1 + KCONV)

                def conv(n, q, h, xin_count):
                    if h == 0:
                        pe.wait_ge(s_xin[q], xin_count)
                        wait(pe, s_x1, n - 2)
                    m = (mA, mB)[h]
                    x3 = seqs(xin[q][:])
                    for k in reversed(range(KCONV)):
                        sh = KCONV - 1 - k
                        mm = pe.matmul(seqs(m[:])[:, :, sh:S], wconv[:, k, h * 128:(h + 1) * 128],
                                       x3[:, :, 0:S - sh], start=(sh == 0), stop=(k == 0))
                    mm.then_inc(s_conv, 1)

                def res(n, q):
                    pe.wait_ge(s_u, n + 1)
                    for h, m in ((0, mA), (1, mB)):
                        mm = pe.matmul(m[:], W["win"][:, INNER + h * 128:INNER + (h + 1) * 128], xin[q][:],
                                       start=True, stop=True)
                    mm.then_inc(s_res, 1)

                def xdbl(n, q):
                    pe.wait_ge(s_z, n + 1)
                    for h in range(HALF):
                        mm = pe.matmul(mA[:], W["xproj"][:, h, :], u[q][:, h, :], start=(h == 0), stop=(h == HALF - 1))
                    mm.then_inc(s_xdbl, 1)

                def dtp(n, q):
                    pe.wait_ge(s_hi, n + 1)
                    pe.wait_ge(s_r1, n + 1)
                    for h, m in ((0, mA), (1, mB)):
                        mm = pe.matmul(m[:], dtproj[RANK:128, h * 128:(h + 1) * 128], dtin[RANK:128, :], start=True, stop=True)
                    mm.then_inc(s_dtp, 1)

                def spread(row, m, q, done):
                    for j in range(2):
                        mm = pe.matmul(m[:, j, :], g["sel"][:, row + j, :], parts[q][:], start=True, stop=True)
                    mm.then_inc(done, 1)

                def centre(n):
                    pe.wait_ge(s_xre, 16 * (n + 1))
                    pe.wait_ge(s_yz, n + 1)
                    pe.matmul(mA[:], g["cen"][:], xre[:], start=True, stop=False)
                    for h in range(HALF):
                        mm = pe.matmul(mA[:], wout[:, h, :], yd[:, h, :], start=False, stop=(h == HALF - 1))
                    mm.then_inc(s_xc, 1)

                def variance(n):
                    pe.wait_ge(s_sq, n + 1)
                    pe.matmul(mB[:], g["avg"][:], sq[:], start=True, stop=True).then_inc(s_var, 1)

                def body(i, q, first, last):
                    xin_count = 16 if first else ((i + 1 - (1 - q)) // 2 + 1) * 16
                    for p in range(PAIRS):
                        P = i * PAIRS + p

                        def between():
                            if p < PAIRS - 2 or not last:
                                if p == PAIRS - 2:
                                    pe.wait_ge(s_lo, i + 2)
                                pe.wait_ge(s_bs, P + 2)
                                spread(2 * ((p + 2) % PAIRS), pB, q if p < PAIRS - 2 else 1 - q, s_B)
                            if not last and p < 2:
                                conv(i + 1, 1 - q, p, xin_count)
                            if not last and p == 2:
                                res(i + 1, 1 - q)
                            if not last and p == 3:
                                xdbl(i + 1, 1 - q)
                            if not last and p == 4:
                                dtp(i + 1, 1 - q)
                            if not first and p == 5:
                                if not last:
                                    pe.wait_ge(s_ab, i + 2)
                                centre(i - 1)
                            if not first and p == 6:
                                variance(i - 1)

                        if p == 0:
                            between()
                            wait(pe, s_yd, i)
                        for h in range(HALF):
                            pe.wait_ge(s_hc, P * 2 + h + 1)
                            if h == 1 and (p < PAIRS - 1 or not last):
                                spread(NSTATE + 2 * ((p + 1) % PAIRS), pC, q if p < PAIRS - 1 else 1 - q, s_C)
                            for j in range(2):
                                mm = pe.matmul(pY[:, h, :], g["eye"][:], hc[h][:, j, :], start=(p == 0 and j == 0),
                                               stop=(p == PAIRS - 1 and j == 1))
                            mm.then_inc(s_ysum, 1)
                            if h == 0 and p:
                                between()

                for h in range(HALF):
                    conv(0, 0, h, 16)
                res(0, 0)
                xdbl(0, 0)
                dtp(0, 0)
                pe.wait_ge(s_lo, 1)
                spread(0, pB, 0, s_B)
                spread(NSTATE, pC, 0, s_C)
                pe.wait_ge(s_bs, 1)
                spread(2, pB, 0, s_B)
                over_chunks(pe, body)
                centre(NCH - 1)
                variance(NCH - 1)

            @block.scalar
            def _(act):
                act.wait_ge(s_w, wready)
                act.activation(nega[:], W["alog"][:], ACT.Exp).then_inc(s_neg, 1)
                act.wait_ge(s_wprep, 1)
                act.activation(wout[:], mA[:, 0:HALF * 128].rearrange("p (h n) -> p h n", h=HALF), ACT.Copy)\
                   .then_inc(s_wp, 1)

                def drive(n, q):
                    wait(act, s_yz, n - 1)
                    for h, m in ((0, mA), (1, mB)):
                        act.wait_ge(s_conv, 2 * n + h + 1)
                        a = act.activation(u[q][:, h, :], m[:], ACT.Silu, bias=W["convb"][:, h:h + 1])
                    a.then_inc(s_u, 1)

                def gate(n, q):
                    act.wait_ge(s_res, n + 1)
                    for h, m in ((0, mA), (1, mB)):
                        a = act.activation(z[q][:, h, :], m[:], ACT.Silu)
                    a.then_inc(s_z, 1)

                def high(n, q):
                    act.wait_ge(s_xdbl, n + 1)
                    wait(act, s_C, (n - 1) * PAIRS)
                    act.activation(parts[q][0:64, :], mA[0:64, :], ACT.Copy)
                    act.activation(parts[q][64:96, :], mA[0:32, :], ACT.Copy)
                    wait(act, s_dtp, n)
                    act.activation(dtin[RANK:128, :], mA[RANK:128, :], ACT.Copy).then_inc(s_hi, 1)

                def softplus(n):
                    act.wait_ge(s_dtp, n + 1)
                    wait(act, s_dtu, n)
                    for h, m in ((0, mA), (1, mB)):
                        act.activation(ab[:, h, :], m[:], ACT.Abs, bias=W["dtb"][:, h:h + 1])
                        a = act.activation(rl[:, h, :], m[:], ACT.Relu, bias=W["dtb"][:, h:h + 1])
                    a.then_inc(s_ab, 1)
                    act.wait_ge(s_ab, n + 1)
                    act.activation(ex[:], ab[:], ACT.Exp, scale=-1.0).then_inc(s_ex, 1)
                    act.wait_ge(s_ex, n + 1)
                    act.activation(ln[:], ex[:], ACT.Ln, bias=1.0).then_inc(s_ln, 1)

                def squares(n):
                    act.wait_ge(s_xc, n + 1)
                    wait(act, s_var, n)
                    act.activation(sq[:], mA[:], ACT.Square).then_inc(s_sq, 1)

                def rsqrt(n):
                    act.wait_ge(s_var, n + 1)
                    wait(act, s_x1, n)
                    act.activation(rs[:], mB[:], ACT.Ln, bias=g["eps"][:]).then_inc(s_lnv, 1)
                    act.wait_ge(s_lnv, n + 1)
                    act.activation(rs[:], rs[:], ACT.Exp, scale=-0.5).then_inc(s_rs, 1)

                def body(i, q, first, last):
                    for p in range(PAIRS):
                        act.wait_ge(s_B, i * PAIRS + p + 1)
                        wait(act, s_dbu, (i * PAIRS + p) * 2 - 2)
                        act.activation(bs[p % 2][:], pB[:], ACT.Copy).then_inc(s_bs, 1)
                        if p == 0:
                            act.wait_ge(s_dt, i + 1)
                        for h in range(HALF):
                            k = (p * 2 + h) % 4
                            wait(act, s_scan, (i * PAIRS + p) * 2 + h - 3)
                            for j in range(2):
                                a = act.activation(seqs(dA[k][:, j, :])[:, :, 1:S], seqs(dt[q][:, h, :])[:, :, 1:S],
                                                   ACT.Exp, scale=nega[:, h, 2 * p + j:2 * p + j + 1])
                            a.then_inc(s_dA, 1)
                        if not last and p == AT_U:
                            drive(i + 1, 1 - q)
                        if not last and p == AT_Z:
                            gate(i + 1, 1 - q)
                        if not last and p == AT_HI:
                            high(i + 1, 1 - q)
                        if not last and p == AT_SP:
                            softplus(i + 1)
                        if not first and p == PAIRS - 1:
                            squares(i - 1)
                            rsqrt(i - 1)

                act.wait_ge(s_neg, 2)
                drive(0, 0)
                gate(0, 0)
                high(0, 0)
                softplus(0)
                over_chunks(act, body)
                squares(NCH - 1)
                rsqrt(NCH - 1)

            @block.gpsimd
            def _(pool):
                def add_relu(n):
                    pool.wait_ge(s_c, n + 1)
                    pool.tensor_tensor(wm1[:], wm1[:], rl[:], ALU.add).then_inc(s_t, 1)

                def body(i, q, first, last):
                    for p in range(PAIRS):
                        if p == 0:
                            pool.wait_ge(s_dtu, i + 1)
                        if not last and p == PAIRS - 1:
                            add_relu(i + 1)
                        pool.wait_ge(s_bs, i * PAIRS + p + 1)
                        for h in range(HALF):
                            k = (p * 2 + h) % 4
                            wait(pool, s_scan, (i * PAIRS + p) * 2 + h - 3)
                            pool.tensor_tensor(dbu[k][:], dtu[q][:, h, None, :].to_broadcast([128, 2, CH]), bs[p % 2][:],
                                               ALU.mult).then_inc(s_dbu, 1)

                add_relu(0)
                over_chunks(pool, body)

            @block.vector
            def _(dve):
                dve.wait_ge(s_w, wready)
                for k in range(KCONV):
                    dve.tensor_tensor(wconv[:, k, :], W["win"][:, 0:INNER], W["convw"][:, k, :], ALU.mult)\
                       .then_inc(s_wp, 1)
                for k in range(4):
                    for j in range(2):
                        dve.memset(seqs(dA[k][:, j, :])[:, :, 0:1], 0.0)
                dve.wait_ge(s_neg, 1)
                dve.tensor_scalar(nega[:], nega[:], -1.0, None, ALU.mult).then_inc(s_neg, 1)

                def remainders(n, q):
                    dve.wait_ge(s_hi, n + 1)
                    dve.tensor_tensor(r1[:], mA[0:64, :], parts[q][0:64, :], ALU.subtract).then_inc(s_r1, 1)
                    dve.wait_ge(s_r1, n + 1)
                    dve.tensor_copy(parts[q][0:64, :], r1[:]).then_inc(s_mid, 1)
                    dve.wait_ge(s_mid, n + 1)
                    dve.tensor_tensor(parts[q][0:32, :], r1[0:32, :], parts[q][0:32, :], ALU.subtract).then_inc(s_lo, 1)

                def correction(n):
                    dve.wait_ge(s_ex, n + 1)
                    dve.tensor_scalar(wm1[:], ex[:], 1.0, -1.0, ALU.add, ALU.add).then_inc(s_wm1, 1)
                    dve.wait_ge(s_wm1, n + 1)
                    dve.tensor_tensor(wm1[:], ex[:], wm1[:], ALU.subtract).then_inc(s_c, 1)

                def step(n, q):
                    dve.wait_ge(s_t, n + 1)
                    dve.wait_ge(s_ln, n + 1)
                    wait(dve, s_dA, (n - 1) * PAIRS * 2)
                    wait(dve, s_dbu, (n - 1) * PAIRS * 2)
                    dve.tensor_tensor(dt[q][:], wm1[:], ln[:], ALU.add).then_inc(s_dt, 1)
                    dve.wait_ge(s_dt, n + 1)
                    dve.tensor_tensor(dtu[q][:], dt[q][:], u[q][:], ALU.mult).then_inc(s_dtu, 1)

                def skip(n, q):
                    dve.wait_ge(s_ysum, (n + 1) * PAIRS * 2)
                    wait(dve, s_xc, n)
                    for h in range(HALF):
                        a = dve.scalar_tensor_tensor(yd[:, h, :], u[q][:, h, :], W["dpar"][:, h:h + 1], pY[:, h, :],
                                                     ALU.mult, ALU.add)
                    a.then_inc(s_yd, 1)

                def gated(n, q):
                    dve.wait_ge(s_yd, n + 1)
                    dve.tensor_tensor(yd[:], yd[:], z[q][:], ALU.mult).then_inc(s_yz, 1)

                def normed(n):
                    dve.wait_ge(s_rs, n + 1)
                    dve.tensor_tensor(g["resid"][:, cols(n)], mA[:], rs[:], ALU.mult).then_inc(s_x1, 1)

                def body(i, q, first, last):
                    for p in range(PAIRS):
                        for h in range(HALF):
                            k, n = (p * 2 + h) % 4, (i * PAIRS + p) * 2 + h
                            dve.wait_ge(s_dA, n + 1)
                            dve.wait_ge(s_dbu, n + 1)
                            wait(dve, s_hc, n - 1)
                            dve.tensor_tensor_scan(hs[h][:].rearrange("p j t -> p (j t)"),
                                                   dA[k][:].rearrange("p j t -> p (j t)"),
                                                   dbu[k][:].rearrange("p j t -> p (j t)"), 0.0, ALU.mult, ALU.add)\
                               .then_inc(s_scan, 1)
                            if not first and p == 0 and h == 0:
                                skip(i - 1, 1 - q)
                            dve.wait_ge(s_scan, n + 1)
                            dve.wait_ge(s_C, i * PAIRS + p + 1)
                            wait(dve, s_ysum, n - 1)
                            dve.tensor_tensor(hc[h][:], hs[h][:], pC[:], ALU.mult).then_inc(s_hc, 1)
                            if h == 1:
                                continue
                            if not first and p == 1:
                                gated(i - 1, 1 - q)
                            if not last and p == 4:
                                remainders(i + 1, 1 - q)
                            if not last and p == 5:
                                correction(i + 1)
                            if not last and p == 6:
                                step(i + 1, 1 - q)
                            if not first and p == PAIRS - 1:
                                normed(i - 1)

                remainders(0, 0)
                correction(0)
                step(0, 0)
                over_chunks(dve, body)
                skip(NCH - 1, (NCH - 1) % 2)
                gated(NCH - 1, (NCH - 1) % 2)
                normed(NCH - 1)


class Stage:

    def __init__(self, nc, ctx, tag, pe, act, dve, pool):
        self.nc, self.ctx, self.tag = nc, ctx, tag
        self.pX = [ctx.enter_context(nc.psum_tensor(f"{tag}_ps{u}", [128, 4, CH], F32)) for u in range(2)]
        streams = lambda e: [self.sem(f"{e}{u}") for u in range(2)]
        count = lambda e, steps: Progress(streams(e) if steps else [], steps.split())
        self.PE, self.ACT, self.DVE, self.POOL = count("pe", pe), count("act", act), count("dve", dve), count("pool", pool)
        self.ticks, self.n_ticks = self.sb("ticks", [128, 96]), 0
        self.s_prep, self.s_copied = self.sem("prep"), self.sem("copied")

    def carry(self, dve):
        dve.memset(self.ticks[:, self.n_ticks:self.n_ticks + 1], 0.0)
        self.n_ticks += 1

    def sem(self, n):
        return self.ctx.enter_context(self.nc.semaphore(f"{self.tag}_{n}"))

    def sb(self, n, s, d=F32):
        return self.ctx.enter_context(self.nc.sbuf_tensor(f"{self.tag}_{n}", s, d))

    def two(self, n, s, d=F32):
        return [self.sb(f"{n}{u}", s, d) for u in range(2)]


def over_slots(eng, slot, chunks=NCH):
    for n in range(4):
        slot(n // 2, n % 2, "ABC"[:n + 1])
    with eng.Fori(2, chunks // 2) as it:
        for u in range(2):
            slot(it, u, "ABC")
    slot(chunks // 2, 0, "BC")
    slot(chunks // 2, 1, "C")


def other(it, u):
    return (0, it) if u == 1 else (1, it - 1)


class Weights:

    def __init__(self, nc, ctx, tag, **shapes):
        self.tiles = {n: ctx.enter_context(nc.sbuf_tensor(f"{tag}_{n}", s[0] if isinstance(s, tuple) else s,
                                                          s[1] if isinstance(s, tuple) else F32)) for n, s in shapes.items()}
        self.sem = ctx.enter_context(nc.semaphore(f"{tag}_w"))
        self.ready = 0

    def __getitem__(self, n):
        return self.tiles[n]

    def load(self, eng, ld):
        for n, t in self.tiles.items():
            if n == "mask":
                for r in range(2):
                    eng.dma_start(t[r * S:(r + 1) * S, :], ld[n][r:r + 1, :].to_broadcast([S, B // 2 * S])).then_inc(self.sem, 16)
                    self.ready += 16
            else:
                eng.dma_start(t[:], ld[n]).then_inc(self.sem, 16)
                self.ready += 16


def cross_weights(nc, ctx):
    return Weights(nc, ctx, "xw", xwq=[128, 128], xwkv=[128, 256], xwoT=[128, 128], xbo=[128, 1], gx=[128, 1], bx=[128, 1],
                   gl=[128, 1], bl=[128, 1], gq=[128, 1], gk=[128, 1], mask=([128, B // 2 * S], U8))


def experts_weights(nc, ctx):
    return Weights(nc, ctx, "fw", wqT=[64, 1024], keysT=[64, 8 * NK], wdT=[128, DCD], upT=[128, NEXP], bd=[128, 1],
                   wg=[128, DCD], wu=[128, DCD], bg=[128, BLK], bu=[128, BLK], downT=[128, NEXP])


def gated_weights(nc, ctx):
    return Weights(nc, ctx, "rw", rnorm=[128, 1], rwin=[128, 4 * 128], rwdt=[128, HALF, INNER], rbdt=[128, HALF],
                   rwoT=[128, HALF * 128])


def moe_weights(nc, ctx):
    return Weights(nc, ctx, "gw", gw=[128, EXPERTS], gb=[1, EXPERTS], one1=[1, 128], iota8=[128, EXPERTS],
                   w1=[128, EXPERTS + 1, 2 * FFN], b1=[128, EXPERTS + 1, 2], w2T=[128, (EXPERTS + 1) * FFN],
                   rb2T=[128, EXPERTS], sb2=[128, 1])


def centred_rows(pe, psum, wT, blocks, cen):
    for b in range(blocks):
        mm = pe.matmul(psum[:, b * 128:(b + 1) * 128], wT[:, b * 128:(b + 1) * 128], cen, start=True, stop=True)
    return mm


def take_input(dve, st, g, xs, it, u, first):
    if not first:
        await_(dve, st.DVE, u, it - 1, "norm")
    st.DVE.done(dve.tensor_scalar(xs[u][:], g["resid"][:, cols(it * 2 + u)], 1.0, 0.0, ALU.mult, ALU.add), u, "xs")


def rsqrt_steps(act, st, g, it, u, src, rs):
    st.ACT.done(act.activation(rs, src, ACT.Ln, bias=g["eps"][:]), u, "ln")
    await_(act, st.ACT, u, it, "ln")
    st.ACT.done(act.activation(rs, rs, ACT.Exp, scale=-0.5), u, "rs")


def cross(nc, g):
    ctx = ExitStack()
    with ctx:
        st = Stage(nc, ctx, "x",
                   pe="cenC cenL varC varL kC qk msC ms v sim pT av out vout",
                   act="sqC sqL lnC rsC lnL rsL sqkC gkC sqk gq gk lnkC rskC lnk rsk vs exp pT av sqo ln rs",
                   dve="xs hatC affC hatL affL gdC gd knC qn mb mask max sub sum rec pn norm",
                   pool="")
        PE, A_, V_, P_, pX = st.PE, st.ACT, st.DVE, st.POOL, st.pX
        W = g["w"]["cross"]
        mask = W["mask"]
        wo, cb, gqs = st.sb("wo", [128, 128]), st.sb("cb", [128, 1]), st.sb("gqs", [128, 1])
        cin, xs = st.two("cin", [128, CH]), st.two("xs", [128, CH])
        sq, rs = st.two("sq", [128, 3, CH]), st.two("rs", [128, 3, CH])
        cn = st.two("cn", [128, 2, CH])
        qk = st.two("qk", [128, 3, CH])
        qn, kn = st.two("qn", [128, CH]), st.two("kn", [128, SEQ, 2, S])
        vs = st.two("vs", [128, SEQ, 128])
        mb = st.two("mb", [128, SEQ // 2, S])
        mx, sm = st.two("mx", [128, SEQ]), st.two("sm", [128, SEQ])
        pr, pT = st.two("pr", [128, SEQ, 128]), st.two("pT", [128, 2, CH])
        ao = st.two("ao", [128, CH])
        s_cin = [st.sem(f"cin{u}") for u in range(2)]
        ld = g["in"]

        with nc.Block() as block:
            @block.sync
            def _(sp):
                for u in range(2):
                    sp.dma_start(cin[u][:], ld["ctxT"][:, cols(u)]).then_inc(s_cin[u], 16)
                with sp.Fori(0, NCH // 2 - 1) as it:
                    for u in range(2):
                        await_(sp, PE, u, it, "cenC")
                        sp.dma_start(cin[u][:], ld["ctxT"][:, cols(it * 2 + 2 + u)]).then_inc(s_cin[u], 16)

            @block.tensor
            def _(pe):
                pe.wait_ge(W.sem, W.ready)
                centred_rows(pe, pX[0][:, 0, :], W["xwoT"], 1, g["cen"][:])
                pe.matmul(pX[0][:, 0, 128:129], g["cen"][:], W["xbo"][:], start=True, stop=True).then_inc(st.s_prep, 1)
                pe.wait_ge(st.s_copied, 2)

                def centre(it, u):
                    pe.wait_ge(s_cin[u], (it + 1) * 16)
                    await_(pe, V_, u, it, "xs")
                    PE.done(pe.matmul(pX[u][:, 0, :], g["cen"][:], cin[u][:], start=True, stop=True), u, "cenC")
                    PE.done(pe.matmul(pX[u][:, 1, :], g["cen"][:], xs[u][:], start=True, stop=True), u, "cenL")

                def variances(it, u):
                    for k, n in enumerate("CL"):
                        await_(pe, A_, u, it, "sq" + n)
                        PE.done(pe.matmul(pX[u][:, 2 + k, :], g["avg"][:], sq[u][:, k, :], start=True, stop=True), u, "var" + n)

                def context_keys(it, u):
                    await_(pe, V_, u, it, "affC")
                    PE.done(pe.matmul(pX[u][:, 0, :], W["xwkv"][:, 0:128], cn[u][:, 0, :], start=True, stop=True), u, "kC")

                def queries_keys(it, u):
                    await_(pe, V_, u, it, "affL")
                    pe.matmul(pX[u][:, 2, :], W["xwq"][:], cn[u][:, 1, :], start=True, stop=True)
                    PE.done(pe.matmul(pX[u][:, 3, :], W["xwkv"][:, 0:128], cn[u][:, 1, :], start=True, stop=True), u, "qk")

                def context_norms(it, u):
                    await_(pe, A_, u, it, "sqkC")
                    PE.done(pe.matmul(pX[u][:, 1, :], g["avgh"][:], sq[u][:, 0, :], start=True, stop=True), u, "msC")

                def norms(it, u):
                    await_(pe, A_, u, it, "gq")
                    pe.matmul(pX[u][:, 0, :], g["avgh"][:], sq[u][:, 1, :], start=True, stop=True)
                    PE.done(pe.matmul(pX[u][:, 2, :], g["avgh"][:], sq[u][:, 2, :], start=True, stop=True), u, "ms")

                def value(u, b):
                    for k in range(2):
                        mm = pe.matmul(pX[u][k * S:(k + 1) * S, 2 + b // 4, (b % 4) * 128:(b % 4 + 1) * 128],
                                       cn[u][:, k, b * S:(b + 1) * S], W["xwkv"][:, 128:256], start=True, stop=True)
                    return mm

                def values(it, u):
                    await_(pe, V_, u, it, "gd")
                    await_(pe, A_, u, it, "gk")
                    for b in range(SEQ - 1):
                        value(u, b)

                def scores(it, u):
                    await_(pe, V_, u, it, "qn")
                    PE.done(value(u, SEQ - 1), u, "v")
                    for h in range(HEADS):
                        for b in range(SEQ):
                            r, pair = b % 2, b // 2
                            mm = pe.matmul(pX[u][r * S:(r + 1) * S, h, pair * 128:(pair + 1) * 128],
                                           qn[u][h * HD:(h + 1) * HD, b * S:(b + 1) * S],
                                           kn[u][h * HD:(h + 1) * HD, b, :, :].rearrange("p k t -> p (k t)"),
                                           start=True, stop=True)
                    PE.done(mm, u, "sim")

                def transposed(it, u):
                    await_(pe, V_, u, it, "pn")
                    for k in range(SEQ):
                        mm = pe.transpose(pX[u][:, k // 4, (k % 4) * 128:(k % 4 + 1) * 128], pr[u][:, k, :],
                                          g["eye"][:])
                    PE.done(mm, u, "pT")

                def attend(it, u):
                    await_(pe, A_, u, it, "pT")
                    await_(pe, A_, u, it, "vs")
                    for b in range(SEQ):
                        for h in range(HEADS):
                            mm = pe.matmul(pX[u][h * HD:(h + 1) * HD, 2, b * S:(b + 1) * S],
                                           vs[u][:, b, h * HD:(h + 1) * HD],
                                           pT[u][:, h, b * S:(b + 1) * S], start=True, stop=True)
                    PE.done(mm, u, "av")

                def out(it, u):
                    await_(pe, A_, u, it, "av")
                    pe.matmul(pX[u][:, 3, :], g["cen"][:], xs[u][:], start=True, stop=False)
                    PE.done(pe.matmul(pX[u][:, 3, :], wo[:], ao[u][:], start=False, stop=True), u, "out")

                def variance(it, u):
                    await_(pe, A_, u, it, "sqo")
                    PE.done(pe.matmul(pX[u][:, 0, :], g["avg"][:], sq[u][:, 0, :], start=True, stop=True), u, "vout")

                def slot(it, u, parts):
                    v, jt = other(it, u)
                    A, Bm = "A" in parts, "B" in parts
                    if A:
                        centre(it, u)
                        variances(it, u)
                        context_keys(it, u)
                        queries_keys(it, u)
                    if Bm:
                        transposed(jt, v)
                    if A:
                        context_norms(it, u)
                        norms(it, u)
                    if Bm:
                        attend(jt, v)
                        out(jt, v)
                    if A:
                        values(it, u)
                    if Bm:
                        variance(jt, v)
                    if A:
                        scores(it, u)
                over_slots(pe, slot)

            @block.scalar
            def _(act):
                act.wait_ge(st.s_prep, 1)
                act.activation(wo[:], pX[0][:, 0, 0:128], ACT.Copy)
                act.activation(cb[:], pX[0][:, 0, 128:129], ACT.Copy).then_inc(st.s_copied, 1)

                act.preload_act_table_set("natural_log_exp_and_others")

                def squares(it, u):
                    for k, n in enumerate("CL"):
                        await_(act, PE, u, it, "cen" + n)
                        A_.done(act.activation(sq[u][:, k, :], pX[u][:, k, :], ACT.Square), u, "sq" + n)

                def inverse(it, u, n):
                    k = "CL".index(n)
                    await_(act, PE, u, it, "var" + n)
                    A_.done(act.activation(rs[u][:, k, :], pX[u][:, 2 + k, :], ACT.Ln, bias=g["eps"][:]), u, "ln" + n)
                    await_(act, A_, u, it, "ln" + n)
                    A_.done(act.activation(rs[u][:, k, :], rs[u][:, k, :], ACT.Exp, scale=-0.5), u, "rs" + n)

                def context_copies(it, u):
                    await_(act, PE, u, it, "kC")
                    A_.done(act.activation(sq[u][:, 0, :], pX[u][:, 0, :], ACT.Square), u, "sqkC")
                    A_.done(act.activation(qk[u][:, 0, :], pX[u][:, 0, :], ACT.Copy, scale=W["gk"][:]), u, "gkC")

                def copies(it, u):
                    await_(act, PE, u, it, "qk")
                    A_.done(act.activation(sq[u][:, 1:3, :], pX[u][:, 2:4, :], ACT.Square), u, "sqk")
                    A_.done(act.activation(qk[u][:, 1, :], pX[u][:, 2, :], ACT.Copy, scale=gqs[:]), u, "gq")
                    A_.done(act.activation(qk[u][:, 2, :], pX[u][:, 3, :], ACT.Copy, scale=W["gk"][:]), u, "gk")

                def inverse_norms(it, u, n):
                    t = rs[u][:, 0, :] if n else rs[u][:, 1:3, :]
                    await_(act, V_, u, it, "gd" + n)
                    A_.done(act.activation(t, t, ACT.Ln), u, "lnk" + n)
                    await_(act, A_, u, it, "lnk" + n)
                    A_.done(act.activation(t, t, ACT.Exp, scale=-0.5), u, "rsk" + n)

                def values(it, u):
                    await_(act, PE, u, it, "v")
                    A_.done(act.activation(vs[u][:].rearrange("p (k b) d -> p k (b d)", k=2), pX[u][:, 2:4, :], ACT.Copy), u, "vs")

                def exps(it, u):
                    await_(act, V_, u, it, "sub")
                    A_.done(act.activation(pr[u][:], pr[u][:], ACT.Exp), u, "exp")

                def transposed(it, u):
                    await_(act, PE, u, it, "pT")
                    A_.done(act.activation(pT[u][:], pX[u][:, 0:2, :], ACT.Copy), u, "pT")

                def attended(it, u):
                    await_(act, PE, u, it, "av")
                    A_.done(act.activation(ao[u][:], pX[u][:, 2, :], ACT.Copy), u, "av")

                def out_squares(it, u):
                    await_(act, PE, u, it, "out")
                    A_.done(act.activation(sq[u][:, 0, :], pX[u][:, 3, :], ACT.Square, bias=cb[:]), u, "sqo")

                def out_inverse(it, u):
                    await_(act, PE, u, it, "vout")
                    rsqrt_steps(act, st, g, it, u, pX[u][:, 0, :], rs[u][:, 0, :])

                def slot(it, u, parts):
                    v, jt = other(it, u)
                    A, Bm = "A" in parts, "B" in parts
                    if Bm:
                        values(jt, v)
                    if A:
                        squares(it, u)
                        inverse(it, u, "C")
                        inverse(it, u, "L")
                    if Bm:
                        exps(jt, v)
                    if A:
                        context_copies(it, u)
                        copies(it, u)
                    if Bm:
                        transposed(jt, v)
                    if A:
                        inverse_norms(it, u, "C")
                    if Bm:
                        attended(jt, v)
                    if A:
                        inverse_norms(it, u, "")
                    if Bm:
                        out_squares(jt, v)
                        out_inverse(jt, v)
                over_slots(act, slot)

            @block.vector
            def _(dve):
                dve.wait_ge(W.sem, W.ready)
                dve.tensor_scalar(gqs[:], W["gq"][:], HD ** -0.5, None, ALU.mult).then_inc(st.s_copied, 1)

                def load(it, u):
                    take_input(dve, st, g, xs, it, u, isinstance(it, int) and it == 0)

                def hat(it, u, n):
                    k = "CL".index(n)
                    await_(dve, A_, u, it, "rs" + n)
                    V_.done(dve.tensor_tensor(cn[u][:, k, :], pX[u][:, k, :], rs[u][:, k, :], ALU.mult), u, "hat" + n)
                    await_(dve, V_, u, it, "hat" + n)
                    V_.done(dve.tensor_scalar(cn[u][:, k, :], cn[u][:, k, :], (W["gx"], W["gl"])[k][:], (W["bx"], W["bl"])[k][:],
                                              ALU.mult, ALU.add), u, "aff" + n)

                def guard(it, u):
                    await_(dve, PE, u, it, "msC")
                    V_.done(dve.tensor_scalar(rs[u][:, 0, :], pX[u][:, 1, :], 1e-16, None, ALU.max), u, "gdC")
                    await_(dve, PE, u, it, "ms")
                    V_.done(dve.tensor_scalar(rs[u][:, 1:3, :], pX[u][:, 0:3:2, :], 1e-16, None, ALU.max), u, "gd")

                def normalise(it, u, n):
                    key = lambda t, k: t[u][:, k, :].rearrange("p (b t) -> p b t", b=SEQ)
                    await_(dve, A_, u, it, "rsk" + n)
                    if n:
                        V_.done(dve.tensor_tensor(kn[u][:, :, 0, :], key(qk, 0), key(rs, 0), ALU.mult), u, "knC")
                    else:
                        dve.tensor_tensor(qn[u][:], qk[u][:, 1, :], rs[u][:, 1, :], ALU.mult)
                        V_.done(dve.tensor_tensor(kn[u][:, :, 1, :], key(qk, 2), key(rs, 2), ALU.mult), u, "qn")

                def softmax_in(it, u):
                    n = SEQ // 2 * S
                    V_.done(dve.tensor_scalar(mb[u][:].rearrange("p a t -> p (a t)"), mask[:, bass.ds((it * 2 + u) * n, n)],
                                              -1.0, BIG, ALU.add, ALU.mult), u, "mb")
                    await_(dve, PE, u, it, "sim")
                    await_(dve, V_, u, it, "mb")
                    keys = pX[u][:, 0:2, :].rearrange("p h (a k t) -> p h a k t", k=2, t=S)[:, :, :, 0, :]
                    V_.done(dve.tensor_tensor(keys, keys, mb[u][:, None, :, :].to_broadcast([128, 2, SEQ // 2, S]),
                                              ALU.add), u, "mask")
                    await_(dve, V_, u, it, "mask")
                    sim = pX[u][:, 0:2, :].rearrange("p h (a k) -> p (h a) k", k=128)
                    V_.done(dve.tensor_reduce(mx[u][:], sim, AX, ALU.max), u, "max")
                    await_(dve, V_, u, it, "max")
                    V_.done(dve.tensor_tensor(pr[u][:], sim, mx[u][:].unsqueeze(2).to_broadcast([128, SEQ, 128]),
                                              ALU.subtract), u, "sub")

                def sums(it, u):
                    await_(dve, A_, u, it, "exp")
                    V_.done(dve.tensor_reduce(sm[u][:], pr[u][:], AX, ALU.add), u, "sum")
                    await_(dve, V_, u, it, "sum")
                    V_.done(dve.reciprocal(sm[u][:], sm[u][:]), u, "rec")

                def divide(it, u):
                    await_(dve, V_, u, it, "rec")
                    V_.done(dve.tensor_tensor(pr[u][:], pr[u][:], sm[u][:].unsqueeze(2).to_broadcast([128, SEQ, 128]),
                                              ALU.mult), u, "pn")

                def norm(it, u):
                    await_(dve, A_, u, it, "rs")
                    V_.done(dve.scalar_tensor_tensor(g["resid"][:, cols(it * 2 + u)], pX[u][:, 3, :], cb[:],
                                                     rs[u][:, 0, :], ALU.add, ALU.mult), u, "norm")

                def slot(it, u, parts):
                    v, jt = other(it, u)
                    A, Bm = "A" in parts, "B" in parts
                    if A:
                        load(it, u)
                    if Bm:
                        softmax_in(jt, v)
                    if A:
                        hat(it, u, "C")
                        hat(it, u, "L")
                    if Bm:
                        sums(jt, v)
                        divide(jt, v)
                    if A:
                        guard(it, u)
                        normalise(it, u, "C")
                        normalise(it, u, "")
                    if Bm:
                        norm(jt, v)
                over_slots(dve, slot)


def experts(nc, g):
    ctx = ExitStack()
    with ctx:
        st = Stage(nc, ctx, "f",
                   pe="sim down up0 up1 g0 g1 g2 g3 out var",
                   act="s down sg0 ey ea ex sg1 v1 sqo ln rs",
                   dve="xs top ix ixf best rep hm0 sel hm1 row z rz xw tau ne nt far far2 rest thr "
                       + " ".join(f"m{c} f{c} l{c}" for c in range(TILES)) + " w0 w norm",
                   pool="pairs ey ea rel far0 far1 keep v0 v2 v3")
        PE, A_, V_, P_, pX = st.PE, st.ACT, st.DVE, st.POOL, st.pX
        CHD = TILES * PKH
        W = g["w"]["experts"]
        km, wd, up, cb = st.sb("km", [128, 512]), st.sb("wd", [128, DCD]), st.sb("up", [128, NEXP]), st.sb("cb", [128, 1])
        xs = st.two("xs", [128, CH])
        S_ = st.two("S", [128, 2, CHD, NK])
        T_ = st.two("T", [128, 2, CHD, TOPK])
        ixu, ixf = st.two("ixu", [128, CHD, TOPK], U32), st.two("ixf", [128, CHD, TOPK])
        pairs, sel = st.two("pairs", [128, CHD, 64]), st.two("sel", [128, CHD, 64])
        best = st.two("best", [128, CHD, TOPK])
        ey, ea = st.two("ey", [128, CHD, NK]), st.two("ea", [128, CHD, ROWS])
        far = st.two("far", [128, CHD, 64])
        ne = far
        row, z, tau, thr = (st.two(n, s) for n, s in (("row", [128, CHD, 8]), ("z", [128, CHD]), ("tau", [128, CHD, 8]),
                                                      ("thr", [128, CHD, ROWS])))
        outr, rest = st.two("outr", [128, CHD, 8]), st.two("rest", [128, TILES])
        val = [st.sb(f"val{c}", [128, PKH, NEXP]) for c in range(TILES)]
        reach = st.sb("reach", [128, PKH, NEXP])
        wqT, keysT = W["wqT"], W["keysT"]
        act_e = st.two("act_e", [128, BLK, CH])
        sg, hm = st.two("sg", [128, 2, CH]), st.two("hm", [128, BLK, CH])
        sq, rs = ([t[:, k, :] for t in sg] for k in range(2))
        ld = g["in"]
        g8 = lambda t: t.rearrange("p g (i j) -> p g i j", i=8)

        with nc.Block() as block:
            @block.gpsimd
            def _(pool):
                def first_scores(it, u):
                    await_(pool, V_, u, it, "top")
                    sx, sy = T_[u][:, 0, :, :], T_[u][:, 1, :, :]
                    P_.done(pool.tensor_tensor(g8(pairs[u][:]), sx.unsqueeze(3).to_broadcast([128, CHD, 8, 8]),
                                               sy.unsqueeze(2).to_broadcast([128, CHD, 8, 8]), ALU.add), u, "pairs")
                    P_.done(pool.tensor_tensor(ey[u][:], S_[u][:, 1, :, :], sy[:, :, 0:1].to_broadcast([128, CHD, NK]),
                                               ALU.subtract), u, "ey")
                    P_.done(pool.tensor_tensor(ea[u][:], S_[u][:, 0, :, 0:ROWS],
                                               sx[:, :, 0:1].to_broadcast([128, CHD, ROWS]), ALU.subtract), u, "ea")

                def chosen(it, u):
                    await_(pool, V_, u, it, "sel")
                    P_.done(pool.tensor_tensor(pairs[u][:], pairs[u][:], best[u][:, :, 0:1].to_broadcast([128, CHD, 64]),
                                               ALU.subtract), u, "rel")
                    P_.done(pool.tensor_scalar(far[u][:], sel[u][:], -BIG, BIG, ALU.mult, ALU.add), u, "far0")
                    await_(pool, P_, u, it, "far0")
                    P_.done(pool.tensor_tensor(g8(far[u][:]), g8(far[u][:]),
                                               T_[u][:, 1, :, :].unsqueeze(2).to_broadcast([128, CHD, 8, 8]),
                                               ALU.add), u, "far1")
                    await_(pool, A_, u, it, "ex")
                    P_.done(pool.tensor_tensor(pairs[u][:], pairs[u][:], sel[u][:], ALU.mult), u, "keep")

                def weights(it, u, c):
                    if c == 0:
                        await_(pool, V_, u, it, "xw")
                        await_(pool, A_, u, it, "ey")
                    v, jt = other(it, u)
                    await_(pool, PE, v, jt, f"g{c}")
                    t = slice(c * PKH, (c + 1) * PKH)
                    P_.done(pool.tensor_tensor(val[c][:].rearrange("p h (a b) -> p h a b", a=ROWS),
                                               ey[u][:, t, :].unsqueeze(2).to_broadcast([128, PKH, ROWS, NK]),
                                               ea[u][:, t, :].unsqueeze(3).to_broadcast([128, PKH, ROWS, NK]),
                                               ALU.mult), u, f"v{c}")

                def slot(it, u, parts):
                    v, jt = other(it, u)
                    A, Bm = "A" in parts, "B" in parts
                    if Bm:
                        weights(jt, v, 2)
                    if A:
                        first_scores(it, u)
                    if Bm:
                        weights(jt, v, 3)
                    if A:
                        chosen(it, u)
                        weights(it, u, 0)
                over_slots(pool, slot)

            @block.tensor
            def _(pe):
                pe.wait_ge(W.sem, W.ready)
                for k in range(8):
                    pe.matmul(pX[0][:, 0, k * NK:(k + 1) * NK], wqT[:, k * 128:(k + 1) * 128], keysT[:, k * NK:(k + 1) * NK], start=True, stop=True)
                centred_rows(pe, pX[0][:, 1, :], W["wdT"], BLK, g["cen"][:])
                centred_rows(pe, pX[0][:, 2, :], W["upT"], BLK, g["cen"][:])
                pe.matmul(pX[0][:, 3, 0:1], g["cen"][:], W["bd"][:], start=True, stop=True).then_inc(st.s_prep, 1)
                pe.wait_ge(st.s_copied, 1)

                def up_proj(u, k, step):
                    for j in range(2):
                        b = 2 * k + j
                        pe.matmul(pX[u][:, j, :], W["wg"][:, b * 128:(b + 1) * 128], xs[u][:], start=True, stop=True)
                        mm = pe.matmul(pX[u][:, 2 + j, :], W["wu"][:, b * 128:(b + 1) * 128], xs[u][:], start=True, stop=True)
                    PE.done(mm, u, step)

                def scores(it, u):
                    await_(pe, V_, u, it, "xs")
                    for c in range(TILES):
                        mm = pe.matmul(pX[u][:, c, :], xs[u][:, c * 128:(c + 1) * 128], km[:], start=True, stop=True)
                    PE.done(mm, u, "sim")

                def down(it, u):
                    await_(pe, A_, u, it, "s")
                    for b in range(BLK):
                        mm = pe.matmul(pX[u][:, b, :], W["downT"][:, b * 128:(b + 1) * 128], xs[u][:], start=True, stop=True)
                    PE.done(mm, u, "down")

                def tile(it, u, c):
                    if c == 0:
                        await_(pe, V_, u, it, "hm1")
                    await_(pe, V_, u, it, f"l{c}")
                    for b in range(BLK):
                        for h in range(PKH):
                            mm = pe.matmul(pX[u][:, b, c * 128:(c + 1) * 128], val[c][:, h, b * 128:(b + 1) * 128],
                                           g["eye"][:], start=(h == 0), stop=(h == PKH - 1))
                    PE.done(mm, u, f"g{c}")

                def out(it, u):
                    await_(pe, V_, u, it, "w0")
                    pe.matmul(pX[u][:, 0, :], g["cen"][:], xs[u][:], start=True, stop=False)
                    for b in range(BLK):
                        pe.matmul(pX[u][:, 0, :], wd[:, b * 128:(b + 1) * 128], hm[u][:, b, :], start=False, stop=False)
                    await_(pe, V_, u, it, "w")
                    for b in range(BLK):
                        mm = pe.matmul(pX[u][:, 0, :], up[:, b * 128:(b + 1) * 128], act_e[u][:, b, :], start=False,
                                       stop=(b == BLK - 1))
                    PE.done(mm, u, "out")

                def slot(it, u, parts):
                    v, jt = other(it, u)
                    A, Bm, Cn = "A" in parts, "B" in parts, "C" in parts
                    if Cn:
                        await_(pe, A_, u, it - 1, "sqo")
                        PE.done(pe.matmul(pX[u][:, 1, :], g["avg"][:], sq[u][:], start=True, stop=True), u, "var")
                    if A:
                        scores(it, u)
                    if Bm:
                        tile(jt, v, 0)
                    if A:
                        down(it, u)
                        await_(pe, A_, u, it, "down")
                        up_proj(u, 0, "up0")
                    if Bm:
                        tile(jt, v, 1)
                    if A:
                        await_(pe, V_, u, it, "hm0")
                        up_proj(u, 1, "up1")
                    if Bm:
                        tile(jt, v, 2)
                        tile(jt, v, 3)
                        out(jt, v)
                over_slots(pe, slot)

            @block.scalar
            def _(act):
                act.wait_ge(st.s_prep, 1)
                for k, t in enumerate((km, wd, up)):
                    act.activation(t[:], pX[0][:, k, :], ACT.Copy)
                act.activation(cb[:], pX[0][:, 3, 0:1], ACT.Copy).then_inc(st.s_copied, 1)

                def gate(u, k, step):
                    for j in range(2):
                        a = act.activation(sg[u][:, j, :], pX[u][:, j, :], ACT.Silu, bias=W["bg"][:, 2 * k + j:2 * k + j + 1])
                    A_.done(a, u, step)

                def slot(it, u, parts):
                    if "C" in parts:
                        await_(act, PE, u, it - 1, "var")
                        rsqrt_steps(act, st, g, it - 1, u, pX[u][:, 1, :], rs[u][:])
                    if "A" in parts:
                        await_(act, PE, u, it, "sim")
                        A_.done(act.activation(S_[u][:].rearrange("p s (c h) k -> p c s (h k)", c=TILES),
                                               pX[u][:].rearrange("p c (s n) -> p c s n", s=2), ACT.Copy), u, "s")
                        await_(act, PE, u, it, "down")
                        A_.done(act.activation(act_e[u][:], pX[u][:], ACT.Silu), u, "down")
                        await_(act, PE, u, it, "up0")
                        gate(u, 0, "sg0")
                        await_(act, P_, u, it, "ea")
                        A_.done(act.activation(ey[u][:], ey[u][:], ACT.Exp), u, "ey")
                        A_.done(act.activation(ea[u][:], ea[u][:], ACT.Exp), u, "ea")
                        await_(act, P_, u, it, "rel")
                        A_.done(act.activation(pairs[u][:], pairs[u][:], ACT.Exp), u, "ex")
                        await_(act, PE, u, it, "up1")
                        gate(u, 1, "sg1")
                        await_(act, V_, u, it, "xw")
                        v, jt = other(it, u)
                        await_(act, PE, v, jt, "g1")
                        for h in range(PKH):
                            for a_ in range(ROWS):
                                a = act.activation(val[1][:, h, a_ * NK:(a_ + 1) * NK], ey[u][:, PKH + h, :], ACT.Copy,
                                                   scale=ea[u][:, PKH + h, a_:a_ + 1])
                        A_.done(a, u, "v1")
                    if "B" in parts:
                        v, jt = other(it, u)
                        await_(act, PE, v, jt, "out")
                        A_.done(act.activation(sq[v][:], pX[v][:, 0, :], ACT.Square, bias=cb[:]), v, "sqo")
                over_slots(act, slot)

            @block.vector
            def _(dve):
                def hidden(it, u, k):
                    await_(dve, A_, u, it, f"sg{k}")
                    for j in range(2):
                        b = 2 * k + j
                        a = dve.scalar_tensor_tensor(hm[u][:, b, :], pX[u][:, 2 + j, :], W["bu"][:, b:b + 1], sg[u][:, j, :],
                                                     ALU.add, ALU.mult)
                    V_.done(a, u, f"hm{k}")

                def best_keys(it, u):
                    await_(dve, A_, u, it, "s")
                    st.carry(dve)
                    for s in range(2):
                        for k in range(CHD):
                            a = dve.max(T_[u][:, s, k, :], S_[u][:, s, k, :])
                    V_.done(a, u, "top")
                    await_(dve, V_, u, it, "top")
                    st.carry(dve)
                    for k in range(CHD):
                        a = dve.max_index(ixu[u][:, k, :], T_[u][:, 0, k, :], S_[u][:, 0, k, :])
                    V_.done(a, u, "ix")
                    await_(dve, V_, u, it, "ix")
                    V_.done(dve.tensor_copy(ixf[u][:], ixu[u][:]), u, "ixf")

                def best_pairs(it, u):
                    await_(dve, P_, u, it, "pairs")
                    st.carry(dve)
                    for k in range(CHD):
                        a = dve.max(best[u][:, k, :], pairs[u][:, k, :])
                    V_.done(a, u, "best")
                    await_(dve, V_, u, it, "best")
                    st.carry(dve)
                    for k in range(CHD):
                        a = dve.match_replace(sel[u][:, k, :], best[u][:, k, :], pairs[u][:, k, :], -3e38)
                    V_.done(a, u, "rep")
                    hidden(it, u, 0)
                    await_(dve, V_, u, it, "rep")
                    V_.done(dve.tensor_tensor(sel[u][:], sel[u][:], pairs[u][:], ALU.is_lt), u, "sel")

                def ranks(it, u):
                    await_(dve, P_, u, it, "keep")
                    V_.done(dve.tensor_reduce(row[u][:], g8(pairs[u][:]), AX, ALU.add), u, "row")
                    await_(dve, V_, u, it, "row")
                    V_.done(dve.tensor_reduce(z[u][:], row[u][:], AX, ALU.add), u, "z")
                    await_(dve, V_, u, it, "z")
                    V_.done(dve.reciprocal(z[u][:], z[u][:]), u, "rz")
                    await_(dve, V_, u, it, "rz")
                    await_(dve, A_, u, it, "ea")
                    zb = z[u][:].unsqueeze(2).to_broadcast([128, CHD, 8])
                    V_.done(dve.tensor_tensor(ea[u][:], ea[u][:], zb, ALU.mult), u, "xw")

                def positions(it, u):
                    await_(dve, P_, u, it, "far1")
                    V_.done(dve.tensor_reduce(tau[u][:], g8(far[u][:]), AX, ALU.min), u, "tau")
                    await_(dve, V_, u, it, "tau")
                    for a_ in range(ROWS):
                        a = dve.tensor_scalar(g8(ne[u][:])[:, :, a_, :], ixf[u][:], float(a_), BIG, ALU.not_equal, ALU.mult)
                    V_.done(a, u, "ne")
                    await_(dve, V_, u, it, "ne")
                    V_.done(dve.tensor_tensor(g8(ne[u][:]), g8(ne[u][:]),
                                              tau[u][:].unsqueeze(2).to_broadcast([128, CHD, 8, 8]), ALU.add), u, "nt")
                    zb = z[u][:].unsqueeze(2).to_broadcast([128, CHD, 8])
                    V_.done(dve.scalar_tensor_tensor(outr[u][:], ixf[u][:], float(ROWS), row[u][:], ALU.is_ge, ALU.mult),
                            u, "far")
                    await_(dve, V_, u, it, "far")
                    V_.done(dve.tensor_tensor(outr[u][:], outr[u][:], zb, ALU.mult), u, "far2")
                    await_(dve, V_, u, it, "far2")
                    V_.done(dve.tensor_reduce(rest[u][:], outr[u][:].rearrange("p (c h) i -> p c (h i)", c=TILES),
                                              AX, ALU.add), u, "rest")

                def thresholds(it, u):
                    await_(dve, V_, u, it, "nt")
                    V_.done(dve.tensor_reduce(thr[u][:], g8(ne[u][:]), AX, ALU.min), u, "thr")

                def tile(it, u, c):
                    if c == 0:
                        await_(dve, V_, u, it, "thr")
                        v, jt = other(it, u)
                        await_(dve, V_, v, jt, f"l{TILES - 1}")
                    else:
                        await_(dve, V_, u, it, f"l{c - 1}")
                    t = slice(c * PKH, (c + 1) * PKH)
                    V_.done(dve.tensor_tensor(reach[:].rearrange("p h (a b) -> p h a b", a=ROWS),
                                              S_[u][:, 1, t, :].unsqueeze(2).to_broadcast([128, PKH, ROWS, NK]),
                                              thr[u][:, t, :].unsqueeze(3).to_broadcast([128, PKH, ROWS, NK]),
                                              ALU.is_ge), u, f"m{c}")
                    await_(dve, V_, u, it, f"m{c}")
                    await_(dve, A_ if c == 1 else P_, u, it, f"v{c}")
                    V_.done(dve.tensor_tensor(val[c][:], reach[:], val[c][:], ALU.mult), u, f"f{c}")
                    await_(dve, V_, u, it, f"f{c}")
                    last = val[c][:, PKH - 1, NEXP - 1:NEXP]
                    V_.done(dve.tensor_tensor(last, last, rest[u][:, c:c + 1], ALU.add), u, f"l{c}")

                def slot(it, u, parts):
                    v, jt = other(it, u)
                    A, Bm, Cn = "A" in parts, "B" in parts, "C" in parts
                    if Bm:
                        tile(jt, v, 0)
                    if Cn:
                        await_(dve, A_, u, it - 1, "rs")
                        V_.done(dve.scalar_tensor_tensor(g["resid"][:, cols(it * 2 - 2 + u)], pX[u][:, 0, :], cb[:],
                                                         rs[u][:], ALU.add, ALU.mult), u, "norm")
                    if A:
                        take_input(dve, st, g, xs, it, u, it == 0 if isinstance(it, int) else False)
                    if Bm:
                        tile(jt, v, 1)
                        tile(jt, v, 2)
                    if A:
                        best_keys(it, u)
                        best_pairs(it, u)
                    if Bm:
                        tile(jt, v, 3)
                    if A:
                        hidden(it, u, 1)
                        ranks(it, u)
                    if Bm:
                        await_(dve, PE, v, jt, f"g{TILES - 1}")
                        for step, t in (("w0", slice(0, 1)), ("w", slice(1, BLK))):
                            V_.done(dve.tensor_tensor(act_e[v][:, t, :], pX[v][:, t, :], act_e[v][:, t, :], ALU.mult), v, step)
                    if A:
                        positions(it, u)
                        thresholds(it, u)
                dve.wait_ge(W.sem, W.ready)
                over_slots(dve, slot)


def gated_scan(nc, g):
    ctx = ExitStack()
    with ctx:
        st = Stage(nc, ctx, "r", pe="u z lam out var", act="u z lam sqo ln rs",
                   dve="xs one in zero scan gate norm", pool="")
        PE, A_, V_, P_, pX = st.PE, st.ACT, st.DVE, st.POOL, st.pX
        PREP, PREA, PREV = (Progress([st.sem(f"{n}{u}") for u in range(2)], steps.split())
                            for n, steps in (("prep", "ms"), ("prea", "ln rs"), ("prev", "sq h")))
        W = g["w"]["gated"]
        wo = st.sb("wo", [128, HALF * 128])
        xs, sqi, rsi, sq, rs, hn = (st.two(n, [128, CH]) for n in ("xs", "sqi", "rsi", "sq", "rs", "hn"))
        uz = st.two("uz", [128, 4, CH])
        lam, one, s_ = (st.two(n, [128, HALF, CH]) for n in ("lam", "one", "s"))
        ld = g["in"]

        with nc.Block() as block:
            @block.sync
            def _(sp):
                W.load(sp, ld)
                g["w"]["moe"].load(sp, ld)

            @block.tensor
            def _(pe):
                pe.wait_ge(W.sem, W.ready)
                centred_rows(pe, pX[0][:, 0, :], W["rwoT"], HALF, g["cen"][:]).then_inc(st.s_prep, 1)
                pe.wait_ge(st.s_copied, 1)

                def project(it, u, k):
                    await_(pe, PREV, u, it, "h")
                    if k:
                        await_(pe, V_, u, it - 1, "norm")
                    for b in (2 * k, 2 * k + 1):
                        mm = pe.matmul(pX[u][:, b, :], W["rwin"][:, b * 128:(b + 1) * 128], hn[u][:], start=True, stop=True)
                    PE.done(mm, u, "uz"[k])

                def gates(it, u):
                    await_(pe, A_, u, it, "u")
                    for h in range(HALF):
                        for k in range(HALF):
                            mm = pe.matmul(pX[u][:, h, :], W["rwdt"][:, k, h * 128:(h + 1) * 128], uz[u][:, k, :],
                                           start=(k == 0), stop=(k == HALF - 1))
                    PE.done(mm, u, "lam")

                def mean_square(it, u):
                    await_(pe, PREV, u, it, "sq")
                    await_(pe, A_, u, it - 1, "lam")
                    PREP.done(pe.matmul(pX[u][:, 0, :], g["avg"][:], sqi[u][:], start=True, stop=True), u, "ms")

                def out(it, u):
                    await_(pe, V_, u, it, "gate")
                    pe.matmul(pX[u][:, 2, :], g["cen2"][:], xs[u][:], start=True, stop=False)
                    for k in range(HALF):
                        mm = pe.matmul(pX[u][:, 2, :], wo[:, k * 128:(k + 1) * 128], s_[u][:, k, :], start=False,
                                       stop=(k == HALF - 1))
                    PE.done(mm, u, "out")

                def variance(it, u):
                    await_(pe, A_, u, it, "sqo")
                    PE.done(pe.matmul(pX[u][:, 3, :], g["avg"][:], sq[u][:], start=True, stop=True), u, "var")

                def slot(it, u, parts):
                    v, jt = other(it, u)
                    if "B" in parts:
                        project(jt, v, 0)
                        project(jt, v, 1)
                    if "A" in parts:
                        mean_square(it, u)
                    if "B" in parts:
                        gates(jt, v)
                    if "C" in parts:
                        out(it - 1, u)
                        variance(it - 1, u)
                over_slots(pe, slot)

            @block.scalar
            def _(act):
                act.wait_ge(st.s_prep, 1)
                act.activation(wo[:], pX[0][:, 0, 0:HALF * 128], ACT.Copy).then_inc(st.s_copied, 1)

                def inputs(it, u):
                    for k, n in enumerate("uz"):
                        await_(act, PE, u, it, n)
                        A_.done(act.activation(uz[u][:, 2 * k:2 * k + 2, :], pX[u][:, 2 * k:2 * k + 2, :], ACT.Silu), u, n)

                def gates(it, u):
                    await_(act, PE, u, it, "lam")
                    for h in range(HALF):
                        a = act.activation(lam[u][:, h, :], pX[u][:, h, :], ACT.Sigmoid, bias=W["rbdt"][:, h:h + 1])
                    A_.done(a, u, "lam")

                def scale(it, u):
                    await_(act, PREP, u, it, "ms")
                    await_(act, PREV, u, it - 1, "h")
                    PREA.done(act.activation(rsi[u][:], pX[u][:, 0, :], ACT.Ln, bias=g["eps"][:]), u, "ln")
                    await_(act, PREA, u, it, "ln")
                    PREA.done(act.activation(rsi[u][:], rsi[u][:], ACT.Exp, scale=-0.5), u, "rs")

                def inverse(it, u):
                    await_(act, PE, u, it, "out")
                    A_.done(act.activation(sq[u][:], pX[u][:, 2, :], ACT.Square), u, "sqo")
                    await_(act, PE, u, it, "var")
                    rsqrt_steps(act, st, g, it, u, pX[u][:, 3, :], rs[u][:])

                def slot(it, u, parts):
                    v, jt = other(it, u)
                    if "B" in parts:
                        inputs(jt, v)
                    if "A" in parts:
                        act.preload_act_table_set("natural_log_exp_and_others")
                        scale(it, u)
                    if "B" in parts:
                        gates(jt, v)
                    if "C" in parts:
                        act.preload_act_table_set("natural_log_exp_and_others")
                        inverse(it - 1, u)
                over_slots(act, slot)

            @block.vector
            def _(dve):
                dve.wait_ge(W.sem, W.ready)
                flat = lambda t: t.rearrange("p h t -> p (h t)")

                def square(it, u):
                    await_(dve, PREP, u, it - 1, "ms")
                    x = g["resid"][:, cols(it * 2 + u)]
                    PREV.done(dve.tensor_tensor(sqi[u][:], x, x, ALU.mult), u, "sq")

                def scaled(it, u):
                    await_(dve, PREA, u, it, "rs")
                    await_(dve, PE, u, it - 1, "z")
                    PREV.done(dve.scalar_tensor_tensor(hn[u][:], g["resid"][:, cols(it * 2 + u)], W["rnorm"][:], rsi[u][:],
                                                       ALU.mult, ALU.mult), u, "h")

                def scan(it, u):
                    await_(dve, A_, u, it, "lam")
                    V_.done(dve.tensor_scalar(one[u][:], lam[u][:], -1.0, 1.0, ALU.mult, ALU.add), u, "one")
                    await_(dve, V_, u, it, "one")
                    V_.done(dve.tensor_tensor(one[u][:], one[u][:], uz[u][:, 0:HALF, :], ALU.mult), u, "in")
                    V_.done(dve.memset(flat(lam[u][:]).rearrange("p (s t) -> p s t", t=S)[:, :, 0:1], 0.0), u, "zero")
                    await_(dve, V_, u, it, "zero")
                    V_.done(dve.tensor_tensor_scan(flat(s_[u][:]), flat(lam[u][:]), flat(one[u][:]), 0.0, ALU.mult,
                                                   ALU.add), u, "scan")
                    await_(dve, V_, u, it, "scan")
                    V_.done(dve.tensor_tensor(s_[u][:], s_[u][:], uz[u][:, HALF:4, :], ALU.mult), u, "gate")

                def norm(it, u):
                    await_(dve, A_, u, it, "rs")
                    V_.done(dve.tensor_tensor(g["resid"][:, cols(it * 2 + u)], pX[u][:, 2, :], rs[u][:], ALU.mult), u, "norm")

                def slot(it, u, parts):
                    v, jt = other(it, u)
                    if "A" in parts:
                        square(it, u)
                    if "B" in parts:
                        take_input(dve, st, g, xs, jt, v, isinstance(jt, int) and jt == 0)
                    if "C" in parts:
                        scan(it - 1, u)
                    if "A" in parts:
                        scaled(it, u)
                    if "C" in parts:
                        norm(it - 1, u)
                over_slots(dve, slot)


def context_experts(nc, g):
    ctx = ExitStack()
    with ctx:
        st = Stage(nc, ctx, "e", pe="", act="", dve="", pool="")
        prog = lambda n, steps: Progress([st.sem(f"{n}{w}") for w in range(4)], steps.split())
        PE, A_, V_ = prog("pe", "x1 out cen var"), prog("act", "gelu sqo ln rs"), prog("dve", "xs h add norm")
        ps = [st.pX[w // 2][:, 2 * (w % 2):2 * (w % 2) + 2, :] for w in range(4)]
        four = lambda n, s: [st.sb(f"{n}{w}", s) for w in range(4)]
        xs, xr, sq, rs, cT = (four(n, [128, CH]) for n in ("xs", "xr", "sq", "rs", "cT"))
        cr = four("cr", [128, SEQ // 2, 128])
        hT = four("hT", [128, SEQ // 2, S])
        s_c = [st.sem(f"ctx{w}") for w in range(4)]
        ld = g["in"]
        chunk = lambda it, w: it * 4 + w
        half = CH // 2

        with nc.Block() as block:
            @block.sync
            def _(sp):
                def load(it, w):
                    c = chunk(it, w)
                    sp.dma_start(cT[w][:], ld["ctxT"][:, cols(c)]).then_inc(s_c[w], 16)
                    sp.dma_start(cr[w][:], ld["ctxrow"][:, bass.ds(c * (SEQ // 2), SEQ // 2), :]).then_inc(s_c[w], 16)
                for w in range(4):
                    load(0, w)
                with sp.Fori(1, NCH // 4) as it:
                    for w in range(4):
                        await_(sp, PE, w, it - 1, "out")
                        load(it, w)

            @block.tensor
            def _(pe):
                def first(it, w):
                    pe.wait_ge(s_c[w], (it + 1) * 32)
                    await_(pe, V_, w, it, "xs")
                    for b in range(SEQ):
                        r, pair = b % 2, b // 2
                        mm = pe.matmul(ps[w][r * S:(r + 1) * S, 0, pair * S:(pair + 1) * S], cT[w][:, b * S:(b + 1) * S],
                                       xs[w][:, b * S:(b + 1) * S], start=True, stop=True)
                    PE.done(mm, w, "x1")

                def second(it, w):
                    await_(pe, V_, w, it, "h")
                    for b in range(SEQ):
                        r, pair = b % 2, b // 2
                        mm = pe.matmul(ps[w][:, r, pair * S:(pair + 1) * S], cr[w][r * S:(r + 1) * S, pair, :],
                                       hT[w][r * S:(r + 1) * S, pair, :], start=True, stop=True)
                    PE.done(mm, w, "out")

                def centre(it, w):
                    await_(pe, V_, w, it, "add")
                    PE.done(pe.matmul(ps[w][:, 0, :], g["cen"][:], xr[w][:], start=True, stop=True), w, "cen")

                def variance(it, w):
                    await_(pe, A_, w, it, "sqo")
                    PE.done(pe.matmul(ps[w][:, 1, :], g["avg"][:], sq[w][:], start=True, stop=True), w, "var")

                def slot(it, u, parts):
                    v, jt = other(it, u)
                    for step, part in ((centre, "B"), (first, "A"), (variance, "B"), (second, "A")):
                        if part in parts:
                            k, x = (it, u) if part == "A" else (jt, v)
                            for w in (2 * x, 2 * x + 1):
                                step(k, w)
                over_slots(pe, slot, NCH // 2)

            @block.scalar
            def _(act):
                def gelu(it, w):
                    await_(act, PE, w, it, "x1")
                    A_.done(act.activation(hT[w][:].rearrange("p a t -> p (a t)"), ps[w][:, 0, 0:half],
                                           ACT.Gelu_apprx_tanh), w, "gelu")

                def squares(it, w):
                    await_(act, PE, w, it, "cen")
                    A_.done(act.activation(sq[w][:], ps[w][:, 0, :], ACT.Square), w, "sqo")

                def log(it, w):
                    await_(act, PE, w, it, "var")
                    A_.done(act.activation(rs[w][:], ps[w][:, 1, :], ACT.Ln, bias=g["eps"][:]), w, "ln")

                def inverse(it, w):
                    await_(act, A_, w, it, "ln")
                    A_.done(act.activation(rs[w][:], rs[w][:], ACT.Exp, scale=-0.5), w, "rs")

                def slot(it, u, parts):
                    v, jt = other(it, u)
                    for step, part in ((squares, "B"), (gelu, "A"), (log, "B"), (inverse, "B")):
                        if part in parts:
                            k, x = (it, u) if part == "A" else (jt, v)
                            for w in (2 * x, 2 * x + 1):
                                step(k, w)
                over_slots(act, slot, NCH // 2)

            @block.vector
            def _(dve):
                def take(it, w):
                    await_(dve, V_, w, it - 1, "norm")
                    V_.done(dve.tensor_scalar(xs[w][:], g["resid"][:, cols(chunk(it, w))], 1.0, 0.0, ALU.mult, ALU.add),
                            w, "xs")

                def hidden(it, w):
                    await_(dve, A_, w, it, "gelu")
                    h = hT[w][:].rearrange("p a t -> p (a t)")
                    V_.done(dve.tensor_tensor(h, h, ps[w][:, 0, 0:half], ALU.mult), w, "h")

                def add(it, w):
                    await_(dve, PE, w, it, "out")
                    V_.done(dve.tensor_tensor(
                        xr[w][:].rearrange("p (a r t) -> p r a t", r=2, t=S),
                        xs[w][:].rearrange("p (a r t) -> p r a t", r=2, t=S),
                        ps[w][:, 0:2, 0:half].rearrange("p r (a t) -> p r a t", t=S), ALU.add), w, "add")

                def norm(it, w):
                    await_(dve, A_, w, it, "rs")
                    V_.done(dve.tensor_tensor(g["resid"][:, cols(chunk(it, w))], ps[w][:, 0, :], rs[w][:], ALU.mult),
                            w, "norm")

                def slot(it, u, parts):
                    v, jt = other(it, u)
                    for step, part in ((take, "A"), (hidden, "A"), (add, "A"), (norm, "B")):
                        if part in parts:
                            k, x = (it, u) if part == "A" else (jt, v)
                            for w in (2 * x, 2 * x + 1):
                                step(k, w)
                over_slots(dve, slot, NCH // 2)


def moe(nc, g):
    ALLX = EXPERTS + 1
    ctx = ExitStack()
    with ctx:
        st = Stage(nc, ctx, "g",
                   pe="lg cwT a0 b0 " + " ".join(f"a{e} b{e} ac{e - 1}" for e in range(1, ALLX)) + f" ac{EXPERTS}",
                   act="le hi cwf " + " ".join(f"sa{e}" for e in range(ALLX)),
                   dve="xs lmax lsub ls lr p top ix ixf eq0 eq1 eqs cw r1 mid lo hid0 "
                       + " ".join(f"g{e} hid{e}" for e in range(1, ALLX)),
                   pool="")
        PE, A_, V_, P_, pX = st.PE, st.ACT, st.DVE, st.POOL, st.pX
        TAIL, VAR, NORM = (Progress([st.sem(f"{n}{u}") for u in range(2)], steps.split())
                           for n, steps in (("tail", "sqo xo ln rs"), ("var", "var"), ("norm", "norm")))
        AB = [pX[0][:, 0:2, :], pX[0][:, 2:4, :]]
        SP = [pX[1][:, 0, :], pX[1][:, 1, :]]
        ACC, MISC = pX[1][:, 2, :], pX[1][:, 3, :]
        AT_CW = 5
        side = lambda u, e: (u + e) % 2
        W = g["w"]["moe"]
        w2, rb2, cb = st.sb("w2", [128, ALLX * 128]), st.sb("rb2", [EXPERTS, 128]), st.sb("cb", [128, 1])
        xs, sq, rs, xo, sa, hid, res = (st.two(n, [128, CH]) for n in ("xs", "sq", "rs", "xo", "sa", "hid", "res"))
        lg, eq = st.two("lg", [128, TILES, 8]), st.two("eq", [128, 2, TILES, 8])
        lm, top, ixu, ixf = (st.two("lm", [128, TILES]), st.two("top", [128, TILES, 8]),
                             st.two("ixu", [128, TILES, 8], U32), st.two("ixf", [128, TILES, 8]))
        cw3 = st.two("cw3", [128, TILES, 3, 32])
        parts, r1, cwf = st.two("parts", [96, CH], BF16), st.two("r1", [64, CH]), st.two("cwf", [EXPERTS, CH])
        s_out = [st.sem(f"out{u}") for u in range(2)]
        s_zero = st.sem("zero")
        ld = g["in"]

        with nc.Block() as block:
            @block.sync
            def _(sp):
                with sp.Fori(0, NCH // 2) as it:
                    for u in range(2):
                        await_(sp, NORM, u, it, "norm")
                        sp.dma_start(g["out"][:, cols(it * 2 + u)], res[u][:]).then_inc(s_out[u], 16)
                for u in range(2):
                    sp.wait_ge(s_out[u], 16 * (NCH // 2))

            @block.tensor
            def _(pe):
                pe.wait_ge(W.sem, W.ready)
                for b in range(3):
                    n = min(4, ALLX - 4 * b)
                    centred_rows(pe, pX[0][:, b, :], W["w2T"][:, 512 * b:], n, g["cen"][:])
                pe.matmul(pX[0][0:EXPERTS, 3, 0:128], W["rb2T"][:], g["cen"][:], start=True, stop=True)
                pe.matmul(pX[0][:, 3, 128:129], g["cen"][:], W["sb2"][:], start=True, stop=True).then_inc(st.s_prep, 1)
                pe.wait_ge(st.s_copied, 1)

                def up(it, u, e):
                    v, jt = other(it, u)
                    k = side(u, e)
                    if e == 0:
                        await_(pe, V_, v, jt, f"hid{EXPERTS - 1}")
                    elif e == 1:
                        await_(pe, V_, v, jt, f"hid{EXPERTS}")
                        await_(pe, V_, u, it, "lo")
                    else:
                        await_(pe, V_, u, it, f"hid{e - 2}")
                        if e == 2:
                            await_(pe, TAIL, v, jt, "ln")
                    for j, n in enumerate("ab"):
                        mm = pe.matmul(AB[k][:, j, :], W["w1"][:, e, j * FFN:(j + 1) * FFN], xs[u][:], start=True, stop=True)
                        if e and n == "b":
                            mm = pe.matmul(SP[k], g["sel"][:, e - 1, :], parts[u][:], start=True, stop=True)
                        PE.done(mm, u, f"{n}{e}")

                def add(it, u, e):
                    if e == 0:
                        v, jt = other(it, u)
                        await_(pe, TAIL, v, jt, "xo")
                        pe.matmul(ACC, g["cen"][:], xs[u][:], start=True, stop=False)
                    await_(pe, V_, u, it, f"hid{e}")
                    mm = pe.matmul(ACC, w2[:, e * 128:(e + 1) * 128], hid[side(u, e)][:], start=False, stop=False)
                    if e == EXPERTS:
                        mm = pe.matmul(ACC, rb2[:], cwf[u][:], start=False, stop=True)
                    PE.done(mm, u, f"ac{e}")

                def slot(it, u, what):
                    v, jt = other(it, u)
                    for e in range(1, ALLX):
                        if "B" in what:
                            up(jt, v, e)
                        if "C" in what and e == 1:
                            await_(pe, TAIL, u, it - 1, "sqo")
                            await_(pe, V_, u, it - 1, f"hid{EXPERTS}")
                            VAR.done(pe.matmul(SP[side(v, 0)], g["avg"][:], sq[u][:], start=True, stop=True), u, "var")
                        if "A" in what and e == 1:
                            await_(pe, V_, v, jt, "lo")
                            await_(pe, V_, u, it, "xs")
                            for c in range(TILES):
                                o = MISC[:, c * 8:(c + 1) * 8]
                                pe.matmul(o, xs[u][:, c * 128:(c + 1) * 128], W["gw"][:], start=True, stop=False)
                                mm = pe.matmul(o, W["one1"][:], W["gb"][:], start=False, stop=True)
                            PE.done(mm, u, "lg")
                        if "A" in what and e == AT_CW:
                            await_(pe, V_, u, it, "cw")
                            for c in range(TILES):
                                mm = pe.matmul(MISC[0:96, c * 128:(c + 1) * 128],
                                               cw3[u][:, c, :, :].rearrange("p r e -> p (r e)"), g["eye"][:], start=True, stop=True)
                            PE.done(mm, u, "cwT")
                        if "B" in what:
                            add(jt, v, e - 1)
                    if "A" in what:
                        up(it, u, 0)
                    if "B" in what:
                        add(jt, v, EXPERTS)
                over_slots(pe, slot)

            @block.scalar
            def _(act):
                act.wait_ge(st.s_prep, 1)
                act.activation(w2[:], pX[0][:, 0:3, :].rearrange("p b n -> p (b n)")[:, 0:ALLX * 128], ACT.Copy)
                act.activation(rb2[:], pX[0][0:EXPERTS, 3, 0:128], ACT.Copy)
                act.activation(cb[:], pX[0][:, 3, 128:129], ACT.Copy).then_inc(st.s_copied, 1)

                act.wait_ge(st.s_copied, 1)

                def expert(it, u, e):
                    await_(act, PE, u, it, f"a{e}")
                    k = side(u, e)
                    A_.done(act.activation(sa[k][:], AB[k][:, 0, :], ACT.Silu, bias=W["b1"][:, e, 0:1]), u, f"sa{e}")

                def slot(it, u, what):
                    v, jt = other(it, u)
                    for e in range(ALLX):
                        if "B" in what:
                            expert(jt, v, e)
                        if "C" in what and e == 0:
                            await_(act, PE, u, it - 1, f"ac{EXPERTS}")
                            TAIL.done(act.activation(sq[u][:], ACC, ACT.Square, bias=cb[:]), u, "sqo")
                            TAIL.done(act.activation(xo[u][:], ACC, ACT.Identity, bias=cb[:]), u, "xo")
                        if "C" in what and e == 1:
                            await_(act, VAR, u, it - 1, "var")
                            TAIL.done(act.activation(rs[u][:], SP[side(v, 0)], ACT.Ln, bias=g["eps"][:]), u, "ln")
                            await_(act, TAIL, u, it - 1, "ln")
                            TAIL.done(act.activation(rs[u][:], rs[u][:], ACT.Exp, scale=-0.5), u, "rs")
                        if "A" in what and e == 1:
                            await_(act, V_, u, it, "lsub")
                            A_.done(act.activation(lg[u][:], lg[u][:], ACT.Exp), u, "le")
                        if "A" in what and e == AT_CW:
                            await_(act, PE, u, it, "cwT")
                            A_.done(act.activation(parts[u][:], MISC[0:96, :], ACT.Copy), u, "hi")
                            A_.done(act.activation(cwf[u][:], MISC[0:EXPERTS, :], ACT.Copy), u, "cwf")
                over_slots(act, slot)

            @block.vector
            def _(dve):
                for u in range(2):
                    dve.memset(cw3[u][:], 0.0).then_inc(s_zero, 1)
                dve.wait_ge(s_zero, 2)
                dve.wait_ge(W.sem, W.ready)
                wide = lambda t: t.unsqueeze(2).to_broadcast([128, TILES, 8])

                def hidden(it, u, e):
                    k = side(u, e)
                    v, jt = other(it, u)
                    await_(dve, PE, u, it, f"b{e}")
                    await_(dve, A_, u, it, f"sa{e}")
                    if e < 2:
                        await_(dve, PE, v, jt, f"ac{EXPERTS - 1 + e}")
                    else:
                        await_(dve, PE, u, it, f"ac{e - 2}")
                    a = dve.scalar_tensor_tensor(hid[k][:], AB[k][:, 1, :], W["b1"][:, e, 1:2], sa[k][:], ALU.add,
                                                 ALU.mult)
                    if e:
                        V_.done(a, u, f"g{e}")
                        await_(dve, V_, u, it, f"g{e}")
                        a = dve.tensor_tensor(hid[k][:], hid[k][:], SP[k], ALU.mult)
                    V_.done(a, u, f"hid{e}")

                def routing(it, u, e):
                    if e == 0:
                        await_(dve, PE, u, it, "lg")
                        logits = MISC[:, 0:TILES * 8].rearrange("p (c e) -> p c e", e=8)
                        V_.done(dve.tensor_reduce(lm[u][:], logits, AX, ALU.max), u, "lmax")
                        await_(dve, V_, u, it, "lmax")
                        V_.done(dve.tensor_tensor(lg[u][:], logits, wide(lm[u][:]), ALU.subtract), u, "lsub")
                    if e == 2:
                        await_(dve, A_, u, it, "le")
                        V_.done(dve.tensor_reduce(lm[u][:], lg[u][:], AX, ALU.add), u, "ls")
                        await_(dve, V_, u, it, "ls")
                        V_.done(dve.reciprocal(lm[u][:], lm[u][:]), u, "lr")
                        await_(dve, V_, u, it, "lr")
                        V_.done(dve.tensor_tensor(lg[u][:], lg[u][:], wide(lm[u][:]), ALU.mult), u, "p")
                        await_(dve, V_, u, it, "p")
                        st.carry(dve)
                        for c in range(TILES):
                            a = dve.max(top[u][:, c, :], lg[u][:, c, :])
                        V_.done(a, u, "top")
                        await_(dve, V_, u, it, "top")
                        st.carry(dve)
                        for c in range(TILES):
                            a = dve.max_index(ixu[u][:, c, :], top[u][:, c, :], lg[u][:, c, :])
                        V_.done(a, u, "ix")
                    if e == 3:
                        await_(dve, V_, u, it, "ix")
                        V_.done(dve.tensor_copy(ixf[u][:], ixu[u][:]), u, "ixf")
                        await_(dve, V_, u, it, "ixf")
                        for k in range(2):
                            V_.done(dve.tensor_tensor(eq[u][:, k, :, :], W["iota8"][:, None, :].to_broadcast([128, TILES, 8]),
                                                      ixf[u][:, :, k:k + 1].to_broadcast([128, TILES, 8]), ALU.is_equal),
                                    u, f"eq{k}")
                        await_(dve, V_, u, it, "eq1")
                        V_.done(dve.tensor_tensor(eq[u][:, 0, :, :], eq[u][:, 0, :, :], eq[u][:, 1, :, :], ALU.add), u, "eqs")
                        await_(dve, V_, u, it, "eqs")
                        V_.done(dve.tensor_tensor(cw3[u][:, :, :, 0:8],
                                                  lg[u][:].unsqueeze(2).to_broadcast([128, TILES, 3, 8]),
                                                  eq[u][:, 0, :, :].unsqueeze(2).to_broadcast([128, TILES, 3, 8]),
                                                  ALU.mult), u, "cw")
                    if e == AT_CW:
                        await_(dve, A_, u, it, "cwf")
                        V_.done(dve.tensor_tensor(r1[u][:], MISC[0:64, :], parts[u][0:64, :], ALU.subtract), u, "r1")
                        await_(dve, V_, u, it, "r1")
                        V_.done(dve.tensor_copy(parts[u][0:64, :], r1[u][:]), u, "mid")
                        await_(dve, V_, u, it, "mid")
                        V_.done(dve.tensor_tensor(parts[u][0:32, :], r1[u][0:32, :], parts[u][0:32, :], ALU.subtract), u, "lo")

                def slot(it, u, what):
                    v, jt = other(it, u)
                    if "A" in what:
                        await_(dve, PE, u, it - 1, f"ac{EXPERTS}")
                        V_.done(dve.tensor_scalar(xs[u][:], g["resid"][:, cols(it * 2 + u)], 1.0, 0.0, ALU.mult, ALU.add), u, "xs")
                    for e in range(ALLX):
                        if "B" in what:
                            hidden(jt, v, e)
                        if "A" in what:
                            routing(it, u, e)
                        if "C" in what and e == 3:
                            await_(dve, TAIL, u, it - 1, "rs")
                            if not isinstance(it, int) or it > 1:
                                dve.wait_ge(s_out[u], (it - 1) * 16)
                            NORM.done(dve.tensor_tensor(res[u][:], xo[u][:], rs[u][:], ALU.mult), u, "norm")
                over_slots(dve, slot)



def build(nc, ld, out):
    g = {"in": ld, "out": out}
    ctx = ExitStack()
    with ctx:
        sb = lambda n, s, d=F32: ctx.enter_context(nc.sbuf_tensor(n, s, d))
        g["resid"] = sb("resid", [128, TOK])
        g["cen"] = sb("cen", [128, 128])
        g["cen2"] = sb("cen2", [128, 128])
        g["avg"] = sb("avg", [128, 128])
        g["avgh"] = sb("avgh", [128, 128])
        g["eye"] = sb("eye", [128, 128])
        self_ = sb("sel_f", [96, 128])
        g["sel"] = sb("sel", [96, 2 * NSTATE, 128], BF16)
        g["eps"] = sb("eps", [128, 1])
        g["s_const"] = ctx.enter_context(nc.semaphore("s_const"))
        with nc.Block() as block:
            @block.sync
            def _(sp):
                for n, t in (("cen", g["cen"]), ("avg", g["avg"]), ("avgh", g["avgh"]), ("eye", g["eye"])):
                    sp.dma_start(t[:], ld[n]).then_inc(g["s_const"], 16)
                sp.dma_start(self_[:, 0:32], ld["mod32"]).then_inc(g["s_const"], 16)

            @block.vector
            def _(dve):
                dve.memset(g["eps"][:], EPS).then_inc(g["s_const"], 1)
                dve.wait_ge(g["s_const"], 81)
                dve.tensor_scalar(g["cen2"][:], g["cen"][:], 2.0, None, ALU.mult).then_inc(g["s_const"], 1)
                dve.tensor_copy(g["sel"][:], self_[:, 0:32].unsqueeze(2).to_broadcast([96, 32, 128]))\
                   .then_inc(g["s_const"], 1)
        g["const_ready"] = 83
        g["w"] = {"experts": experts_weights(nc, ctx)}
        with ExitStack() as until_cross:
            g["w"]["cross"] = cross_weights(nc, until_cross)
            mamba(nc, g)
            cross(nc, g)
        experts(nc, g)
        g["w"].update(gated=gated_weights(nc, ctx), moe=moe_weights(nc, ctx))
        gated_scan(nc, g)
        context_experts(nc, g)
        moe(nc, g)


def layout(x):
    f = lambda a: np.ascontiguousarray(a)
    eye = np.eye(128, dtype=np.float32)
    column = lambda v: v.reshape(-1, 1)
    halves = lambda v: f(v.reshape(HALF, 128).T)
    xp = x["L0_attn_x_proj_w"].T.reshape(HALF, 128, 96).transpose(1, 0, 2)
    a = {
        "xT": x["x"].reshape(TOK, D).T,
        "cen": eye - np.float32(1 / D), "avg": np.full((128, 128), 1 / D, np.float32), "eye": eye,
        "avgh": np.kron(np.eye(2, dtype=np.float32), np.full((64, 64), 1 / 64, np.float32)),
        "mod32": np.tile(np.eye(32, dtype=np.float32), (3, 1)),
        "win": x["L0_attn_in_proj_w"].T,
        "convw": np.broadcast_to(x["L0_attn_conv_w"].T[None], (128, KCONV, INNER)),
        "convb": halves(x["L0_attn_conv_b"]),
        "xproj": np.concatenate([xp[:, :, 64:96]] * 2 + [xp[:, :, 0:64]], axis=2),
        "dtproj": x["L0_attn_dt_proj_w"].T,
        "dtb": halves(x["L0_attn_dt_proj_b"]),
        "alog": x["L0_attn_A_log"].reshape(HALF, 128, NSTATE).transpose(1, 0, 2),
        "dpar": halves(x["L0_attn_D_param"]),
        "woT": x["L0_attn_out_proj_w"],
        "ctxT": x["ctx_1024"].reshape(TOK, D).T,
        "mask": x["mask_BxS2_bk0"].reshape(B // 2, 2, S).transpose(1, 0, 2).reshape(2, B // 2 * S),
        "xwq": x["L0_xattn_W_q"], "xwkv": x["L0_xattn_W_kv"], "xwoT": x["L0_xattn_W_out"].T,
        "xbo": column(x["L0_xattn_b_out"]),
        "gx": column(x["L0_xattn_ln_x_g"]), "bx": column(x["L0_xattn_ln_x_b"]),
        "gl": column(x["L0_xattn_ln_l_g"]), "bl": column(x["L0_xattn_ln_l_b"]),
        "gq": column(np.tile(x["L0_xattn_q_gamma"], 2)), "gk": column(np.tile(x["L0_xattn_k_gamma"], 2)),
        "wg": x["L0_ffn_Wg"], "wu": x["L0_ffn_Wu"], "bg": x["L0_ffn_bg"].reshape(BLK, 128).T,
        "bu": x["L0_ffn_bu"].reshape(BLK, 128).T, "wdT": x["L0_ffn_Wd"].T, "bd": column(x["L0_ffn_bd"]),
        "wqT": x["L0_ffn_Wq"].T.reshape(8, 64, 128).transpose(1, 0, 2).reshape(64, 8 * 128),
        "keysT": x["L0_ffn_keys"].transpose(3, 2, 0, 1).reshape(64, 8 * NK),
        "downT": x["L0_ffn_down_embed"].T, "upT": x["L0_ffn_up_embed"].T,
        "rnorm": column(x["L1_attn_w_norm"]), "rwin": x["L1_attn_W_in"].T,
        "rwdt": x["L1_attn_W_dt"].T.reshape(HALF, 128, INNER).transpose(1, 0, 2),
        "rbdt": halves(x["L1_attn_b_dt"]), "rwoT": x["L1_attn_W_out"],
        "ctxrow": x["ctx_1024"].reshape(B // 2, 2 * S, D).transpose(1, 0, 2),
        "gw": x["L1_ffn_gate_w"], "gb": x["L1_ffn_gate_b"].reshape(1, EXPERTS), "one1": np.ones((1, 128), np.float32),
        "iota8": np.tile(np.arange(EXPERTS, dtype=np.float32), (128, 1)),
        "w1": np.concatenate([x["L1_ffn_sw1"], x["L1_ffn_rw1"]]).transpose(1, 0, 2),
        "b1": np.concatenate([x["L1_ffn_sb1"], x["L1_ffn_rb1"]]).reshape(EXPERTS + 1, 2, FFN).transpose(2, 0, 1),
        "w2T": np.concatenate([x["L1_ffn_sw2"], x["L1_ffn_rw2"]]).transpose(2, 0, 1).reshape(D, (EXPERTS + 1) * FFN),
        "rb2T": x["L1_ffn_rb2"].T, "sb2": x["L1_ffn_sb2"].T,
    }
    return {k: f(v) for k, v in a.items()}


def kernel(**inputs):
    from concourse import bacc
    from concourse.bass_utils import run_bass_kernel_spmd

    nc = bacc.Bacc("TRN2", target_bir_lowering=False, num_devices=1)
    arrays = layout({k: np.asarray(v) for k, v in inputs.items()})
    ld = {k: nc.dram_tensor("in_" + k, a.shape, mybir.dt.from_np(a.dtype), kind="ExternalInput").ap()
          for k, a in arrays.items()}
    out = nc.dram_tensor("out", (D, TOK), F32, kind="ExternalOutput").ap()
    build(nc, ld, out)
    r = run_bass_kernel_spmd(nc, [{"in_" + k: a for k, a in arrays.items()}], core_ids=[0])
    return np.ascontiguousarray(r.results[0]["out"].T).reshape(B, S, D)
```
